# Optimizing a Trainium2 kernel written in Bass

```python
import numpy as np
import jax
import jax.numpy as jnp

def _softmax(x, axis=-1):
    return jax.nn.softmax(x, axis=axis)

def _gelu(x):
    return jax.nn.gelu(x, approximate=True)

def _silu(x):
    return jax.nn.silu(x)

def _sigmoid(x):
    return jax.nn.sigmoid(x)

def _layernorm(x, axis=-1, eps=1e-05):
    m = jnp.mean(x, axis=axis, keepdims=True)
    v = jnp.var(x, axis=axis, keepdims=True)
    return (x - m) / jnp.sqrt(v + eps)

def _scatter_add(tgt, idx, src, axis=0):
    return tgt.at[idx].add(src)

def _segment_sum(src, seg, n):
    return jax.ops.segment_sum(src, seg, n)
kernel_name = 'mk_xattn_ffn_d2_seqx_r4_84fccd'

def setup_inputs(seed: int=0):
    np.random.seed(seed)
    _w = jnp.asarray

    def _rec_inputs():
        import jax
        import jax.numpy as jnp
        _rk = jax.random.key(seed)
        x = 7.22e-05 + 1 * jax.random.normal(jax.random.fold_in(_rk, 1), (16, 128, 512), jnp.float32)
        _lenS = 128 - jax.random.randint(jax.random.fold_in(_rk, 7), (16,), 0, max(1, 128 // 4) + 1, jnp.int32)
        _lenS2 = 128 - jax.random.randint(jax.random.fold_in(_rk, 8), (16,), 0, max(1, 128 // 4) + 1, jnp.int32)
        _ctx_512P = jax.random.normal(jax.random.fold_in(_rk, 11), (16, 16, 128), jnp.float32)
        _ctx_512c = jax.random.dirichlet(jax.random.fold_in(_rk, 511), 0.3 * jnp.ones((16,), jnp.float32), (16, 128))
        _ctx_512t = jnp.einsum('bsk,bkd->bsd', _ctx_512c, _ctx_512P)
        _ctx_512t = _ctx_512t * jax.lax.rsqrt(jnp.mean(jnp.square(_ctx_512t)) + 1e-12) * 0.953939
        ctx_512 = -0.000514642 + 1.00011 * (_ctx_512t + 0.3 * jax.random.normal(jax.random.fold_in(_rk, 611), (16, 128, 128), jnp.float32))
        return (x, ctx_512)
    x, ctx_512 = _rec_inputs()

    def _L0_xattn_setup():
        import jax, jax.numpy as jnp
        import numpy as np
        B, S, H, NH, L = (2, 512, 512, 16, 128)
        HD = H // NH
        key = jax.random.key(seed)
        k1, k2, k3, k4, k5 = jax.random.split(key, 5)
        scale = 0.02
        return {'q': jax.random.normal(k1, (B, S, H), dtype=jnp.float32), 'latent_kv': jax.random.normal(k2, (B, S, L), dtype=jnp.float32), 'Wq': jax.random.normal(k3, (H, H), dtype=jnp.float32) * scale, 'Wkv_expand': jax.random.normal(k4, (2 * H, L), dtype=jnp.float32) * scale, 'Wout': jax.random.normal(k5, (H, H), dtype=jnp.float32) * scale}
    _L0_xattn_all = _L0_xattn_setup()
    _L0_xattn_in = {k: v for k, v in _L0_xattn_all.items() if k in ('Wq', 'Wkv_expand', 'Wout')}
    del _L0_xattn_all

    def _L0_ffn_setup():
        import jax, jax.numpy as jnp
        import numpy as np
        B, S, H = (2, 512, 512)
        FFN = 256
        E = 8
        TOP_K = 2
        key = jax.random.key(seed)
        ks = jax.random.split(key, 5)
        scale = 0.02
        hidden_states = jax.random.normal(ks[0], (B, S, H), dtype=jnp.float32)
        Wg = jax.random.normal(ks[1], (E, H), dtype=jnp.float32) * scale
        W1 = jax.random.normal(ks[2], (E, FFN, H), dtype=jnp.float32) * scale
        W3 = jax.random.normal(ks[3], (E, FFN, H), dtype=jnp.float32) * scale
        W2 = jax.random.normal(ks[4], (E, H, FFN), dtype=jnp.float32) * scale
        bias = jnp.zeros((E,), dtype=jnp.float32)
        return {'hidden_states': hidden_states, 'Wg': Wg, 'W1': W1, 'W2': W2, 'W3': W3, 'bias': bias}
    _L0_ffn_all = _L0_ffn_setup()
    _L0_ffn_in = {k: v for k, v in _L0_ffn_all.items() if k in ('Wg', 'W1', 'W2', 'W3', 'bias')}
    del _L0_ffn_all

    def _L1_xattn_setup():
        import jax, jax.numpy as jnp
        import numpy as np
        B, S, E = (2, 512, 512)
        QH, KVH = (32, 8)
        D = E // QH
        G = QH // KVH
        DROPOUT = 1.0
        key = jax.random.key(seed)
        k1, k2, k3 = jax.random.split(key, 3)
        q = jax.random.normal(k1, (B, S, E), dtype=jnp.float32)
        k = jax.random.normal(k2, (B, S, E // G), dtype=jnp.float32)
        v = jax.random.normal(k3, (B, S, E // G), dtype=jnp.float32)
        return {'q': q, 'k': k, 'v': v}
    _L1_xattn_all = _L1_xattn_setup()
    _L1_xattn_in = {k: v for k, v in _L1_xattn_all.items() if k in ()}
    del _L1_xattn_all

    def _L1_ffn_setup():
        import jax, jax.numpy as jnp
        import numpy as np
        HIDDEN = 512
        INTER = 1408
        EPS = 1e-05

        def rms_norm(x, g):
            var = jnp.mean(x * x, axis=-1, keepdims=True)
            return x * jax.lax.rsqrt(var + EPS) * g

        def activation_quant(x):
            scale = 127.0 / jnp.clip(jnp.max(jnp.abs(x), axis=-1, keepdims=True), 1e-05, None)
            return jnp.clip(jnp.round(x * scale), -128, 127) / scale

        def weight_quant(w):
            scale = 1.0 / jnp.clip(jnp.mean(jnp.abs(w)), 1e-05, None)
            return jnp.clip(jnp.round(w * scale), -1, 1) / scale

        def ste(x, q):
            return x + jax.lax.stop_gradient(q - x)

        def bit_linear(x, w, g):
            xn = rms_norm(x, g)
            xq = ste(xn, activation_quant(xn))
            wq = ste(w, weight_quant(w))
            return xq @ wq.T
        key = jax.random.key(seed)
        k1, k2, k3 = jax.random.split(key, 3)
        x = jax.random.normal(k1, (4, 512, HIDDEN), dtype=jnp.float32)
        gate_w = jax.random.normal(k2, (2 * INTER, HIDDEN), dtype=jnp.float32) * HIDDEN ** (-0.5)
        down_w = jax.random.normal(k3, (HIDDEN, INTER), dtype=jnp.float32) * INTER ** (-0.5)
        gate_norm_w = jnp.ones((HIDDEN,), dtype=jnp.float32)
        down_norm_w = jnp.ones((INTER,), dtype=jnp.float32)
        return {'x': x, 'gate_w': gate_w, 'down_w': down_w, 'gate_norm_w': gate_norm_w, 'down_norm_w': down_norm_w}
    _L1_ffn_all = _L1_ffn_setup()
    _L1_ffn_in = {k: v for k, v in _L1_ffn_all.items() if k in ('gate_w', 'down_w', 'gate_norm_w', 'down_norm_w')}
    del _L1_ffn_all
    return {'x': x, 'ctx_512': ctx_512, 'L0_xattn_Wq': _L0_xattn_in['Wq'], 'L0_xattn_Wkv_expand': _L0_xattn_in['Wkv_expand'], 'L0_xattn_Wout': _L0_xattn_in['Wout'], 'L0_ffn_Wg': _L0_ffn_in['Wg'], 'L0_ffn_W1': _L0_ffn_in['W1'], 'L0_ffn_W2': _L0_ffn_in['W2'], 'L0_ffn_W3': _L0_ffn_in['W3'], 'L0_ffn_bias': _L0_ffn_in['bias'], 'L1_ffn_gate_w': _L1_ffn_in['gate_w'], 'L1_ffn_down_w': _L1_ffn_in['down_w'], 'L1_ffn_gate_norm_w': _L1_ffn_in['gate_norm_w'], 'L1_ffn_down_norm_w': _L1_ffn_in['down_norm_w']}

def reference(x, ctx_512, L0_xattn_Wq, L0_xattn_Wkv_expand, L0_xattn_Wout, L0_ffn_Wg, L0_ffn_W1, L0_ffn_W2, L0_ffn_W3, L0_ffn_bias, L1_ffn_gate_w, L1_ffn_down_w, L1_ffn_gate_norm_w, L1_ffn_down_norm_w):
    import jax
    import jax.numpy as jnp

    def _L0_xattn_ref(q, latent_kv, Wq, Wkv_expand, Wout):
        import jax, jax.numpy as jnp
        import numpy as np
        B, S, H, NH, L = (2, 512, 512, 16, 128)
        HD = H // NH
        b, sq, _ = q.shape
        sk = latent_kv.shape[1]
        qp = q @ Wq.T
        kv = latent_kv @ Wkv_expand.T
        k, v = jnp.split(kv, 2, axis=-1)
        qh = qp.reshape(b, sq, NH, HD).transpose(0, 2, 1, 3)
        kh = k.reshape(b, sk, NH, HD).transpose(0, 2, 1, 3)
        vh = v.reshape(b, sk, NH, HD).transpose(0, 2, 1, 3)
        inv_sqrt_d = 1.0 / jnp.sqrt(jnp.float32(HD))
        scores = jnp.einsum('bhqd,bhkd->bhqk', qh, kh) * inv_sqrt_d
        causal = jnp.tril(jnp.ones((sq, sk), dtype=bool))
        scores = jnp.where(causal, scores, jnp.finfo(scores.dtype).min)
        attn = jax.nn.softmax(scores, axis=-1)
        out = jnp.einsum('bhqk,bhkd->bhqd', attn, vh)
        out = out.transpose(0, 2, 1, 3).reshape(b, sq, H)
        return out @ Wout.T

    def _L0_ffn_ref(hidden_states, Wg, W1, W2, W3, bias):
        import jax, jax.numpy as jnp
        import numpy as np
        B, S, H = (2, 512, 512)
        FFN = 256
        E = 8
        TOP_K = 2
        bsz, seq_len, hidden_dim = hidden_states.shape
        x = hidden_states.reshape(-1, hidden_dim)
        router_logits = x @ Wg.T
        routing_weights = jax.nn.sigmoid(router_logits.astype(jnp.float32))
        scores = routing_weights + bias
        _, top_k_index = jax.lax.top_k(scores, TOP_K)
        top_k_weights = jnp.take_along_axis(routing_weights, top_k_index, axis=1)
        top_k_weights = top_k_weights / top_k_weights.sum(axis=-1, keepdims=True)
        top_k_weights = top_k_weights.astype(x.dtype)
        one_hot = jax.nn.one_hot(top_k_index, Wg.shape[0], dtype=x.dtype)
        expert_w = jnp.einsum('tk,tke->te', top_k_weights, one_hot)
        h1 = jnp.einsum('th,efh->tef', x, W1)
        h3 = jnp.einsum('th,efh->tef', x, W3)
        g = jax.nn.silu(h1) * h3 * expert_w[:, :, None]
        out = jnp.einsum('tef,ehf->th', g, W2)
        return out.reshape(bsz, seq_len, hidden_dim)

    def _L1_xattn_ref(q, k, v):
        import jax, jax.numpy as jnp
        import numpy as np
        B, S, E = (2, 512, 512)
        QH, KVH = (32, 8)
        D = E // QH
        G = QH // KVH
        DROPOUT = 1.0
        b, s, _ = q.shape
        qh = q.reshape(b, s, KVH, G, D).transpose(0, 2, 3, 1, 4)
        kh = k.reshape(b, s, KVH, D).transpose(0, 2, 1, 3)
        vh = v.reshape(b, s, KVH, D).transpose(0, 2, 1, 3)
        scale = 1.0 / jnp.sqrt(jnp.float32(D))
        scores = jnp.einsum('bkgsd,bktd->bkgst', qh, kh) * scale
        attn = jax.nn.softmax(scores, axis=-1) / DROPOUT
        out = jnp.einsum('bkgst,bktd->bkgsd', attn, vh)
        return out.transpose(0, 3, 1, 2, 4).reshape(b, s, E)

    def _L1_ffn_ref(x, gate_w, down_w, gate_norm_w, down_norm_w):
        import jax, jax.numpy as jnp
        import numpy as np
        HIDDEN = 512
        INTER = 1408
        EPS = 1e-05

        def rms_norm(x, g):
            var = jnp.mean(x * x, axis=-1, keepdims=True)
            return x * jax.lax.rsqrt(var + EPS) * g

        def activation_quant(x):
            scale = 127.0 / jnp.clip(jnp.max(jnp.abs(x), axis=-1, keepdims=True), 1e-05, None)
            return jnp.clip(jnp.round(x * scale), -128, 127) / scale

        def weight_quant(w):
            scale = 1.0 / jnp.clip(jnp.mean(jnp.abs(w)), 1e-05, None)
            return jnp.clip(jnp.round(w * scale), -1, 1) / scale

        def ste(x, q):
            return x + jax.lax.stop_gradient(q - x)

        def bit_linear(x, w, g):
            xn = rms_norm(x, g)
            xq = ste(xn, activation_quant(xn))
            wq = ste(w, weight_quant(w))
            return xq @ wq.T
        y = bit_linear(x, gate_w, gate_norm_w)
        gate, up = jnp.split(y, 2, axis=-1)
        h = gate * jax.nn.sigmoid(gate) * up
        return bit_linear(h, down_w, down_norm_w)
    x = x + _L0_xattn_ref(_layernorm(x, axis=-1), ctx_512, L0_xattn_Wq, L0_xattn_Wkv_expand, L0_xattn_Wout)
    x = x + _L0_ffn_ref(_layernorm(x, axis=-1), L0_ffn_Wg, L0_ffn_W1, L0_ffn_W2, L0_ffn_W3, L0_ffn_bias)
    x = x + _L1_xattn_ref(_layernorm(x, axis=-1), ctx_512, ctx_512)
    x = x + _L1_ffn_ref(_layernorm(x, axis=-1), L1_ffn_gate_w, L1_ffn_down_w, L1_ffn_gate_norm_w, L1_ffn_down_norm_w)
    return x

_drawn_inputs = setup_inputs


def setup_inputs(seed=0):
    import zlib

    import numpy as np

    out = dict(_drawn_inputs(seed))
    spreads = {'L0_ffn_bias': (0.0, 0.1),
     'L1_ffn_gate_norm_w': (1.0, 0.2),
     'L1_ffn_down_norm_w': (1.0, 0.2)}
    factors = {'L0_xattn_Wq': 16.282}
    for name, (base, spread) in spreads.items():
        noise = np.random.default_rng([zlib.crc32(name.encode()), seed]).standard_normal(out[name].shape)
        drawn = base * np.exp(spread * noise) if base else spread * noise
        out[name] = jnp.asarray(drawn.astype(out[name].dtype))
    for name, factor in factors.items():
        out[name] = (out[name] * factor).astype(out[name].dtype)
    return out
```

```python
from contextlib import ExitStack

import concourse.bass as bass
from concourse import mybir

P = 128
ALU = mybir.AluOpType
ACT = mybir.ActivationFunctionType
AX = mybir.AxisListType
F32 = mybir.dt.float32
F16 = mybir.dt.float16
BF16 = mybir.dt.bfloat16
I32 = mybir.dt.int32
U32 = mybir.dt.uint32

B = 16
H = 512
HC = H // P
L = 128
EPS = 1e-5
NH0, HD0 = 16, 32
E, FF = 8, 256
FC = FF // P
QH, KVH, HD1 = 32, 8, 16
GROUP = QH // KVH
INTER = 1408
IC = INTER // P
GATE_TILES = 2 * INTER // P
SLOT_TILES = (2 * B * P + E * (P - 1)) // P + 1
SLOT_TILES += SLOT_TILES % 2
SLOTS = SLOT_TILES * P
NEG = -3.0e38
BIG = 3.0e38
ROUND = 12582912.0
GATE_ABS = GATE_TILES * H // B
DOWN_ABS = HC * INTER // B
CHUNKS = [(0, 512), (512, 512), (1024, 384)]
HG = 4


def need(eng, sem, value, alone=False):
    if isinstance(value, int) and value <= 0:
        return
    eng.wait_ge(sem, value)
    if alone and not isinstance(value, int):
        eng.nop(nofuse=True)


def at(t, i, *rest):
    if isinstance(i, int):
        return t[(slice(None), i) + rest]
    ap = t[(slice(None), bass.ds(i, 1)) + rest]
    n = len(ap.shape)
    names = " ".join("abcdef"[k] for k in range(n - 2))
    return ap.rearrange(f"p o {names} -> p (o a) {names[2:]}" if n > 2 else "p o -> p o")


def bodies(eng, count, body, head=1, tail=1):
    for b in range(2 * head):
        body(b, b % 2, b // 2)
    with eng.Fori(head, count // 2 - tail) as j:
        for p in range(2):
            body(j * 2 + p, p, j)
    for b in range(count - 2 * tail, count):
        body(b, b % 2, b // 2)


class Steps:

    def __init__(self, eng, sem, per=0, alone=False):
        self.eng, self.sem, self.per, self.alone, self.base, self.n = eng, sem, per, alone, 0, 0

    def body(self, b):
        self.base, self.n = b * self.per, 0

    def mark(self, ins):
        ins.then_inc(self.sem, 1)
        self.n += 1
        return self.base + self.n

    def then(self, ins):
        need(self.eng, self.sem, self.mark(ins), self.alone)

    def end(self):
        rest = self.per - self.n
        assert rest >= 0, (self.n, self.per)
        if rest:
            self.eng.drain().then_inc(self.sem, rest)
        self.n = self.per
        self.eng.wait_ge(self.sem, self.base + self.n)


def decoder_kernel(nc, x, ctx, Wq, Wkv, Wout, Wg, W1, W2, W3, bias, gate_w, down_w, gnorm, dnorm, out):
    slots_in = nc.dram_tensor("slots_in", [SLOTS, H], F32, kind="Internal").ap()
    slots_out = nc.dram_tensor("slots_out", [SLOTS, H], F32, kind="Internal").ap()
    with ExitStack() as stack:
        def sb(name, shape, dt=F32):
            return stack.enter_context(nc.sbuf_tensor(name, shape, dt))

        def sem(name):
            return stack.enter_context(nc.semaphore(name))

        m = {}
        m["X"] = sb("X", [P, B, H])
        m["CTX"] = sb("CTX", [P, B, L])
        m["ident"] = sb("ident", [P, P])
        m["identh"] = sb("identh", [P, P], F16)
        m["identb"] = sb("identb", [P, P], BF16)
        m["absum"] = sb("absum", [P, 2, B])
        m["ones"] = sb("ones", [P, P])
        m["half"] = sb("half", [P, 1])
        m["pos"] = sb("pos", [P, 2, B], U32)
        m["wt"] = sb("wt", [P, 2, B])
        m["wmean"] = sb("wmean", [P, 2])
        m["wscale"] = sb("wscale", [P, 2])
        m["R"] = sb("R", [P, HC * 2 * INTER + IC * H], BF16)
        with ExitStack() as moe:
            m["first"] = []
            m["sem"] = lambda name: m["first"].append(moe.enter_context(nc.semaphore(name))) or m["first"][-1]
            m["W13T"] = moe.enter_context(nc.sbuf_tensor("W13T", [P, E, HC, 2 * FF], F32))
            m["W2T"] = moe.enter_context(nc.sbuf_tensor("W2T", [P, E, FC, H], F32))
            m["logits"] = moe.enter_context(nc.sbuf_tensor("logits", [P, B, E], F32))
            m["stats2"] = moe.enter_context(nc.sbuf_tensor("stats2", [P, B, 2], F32))
            m["rstd2"] = moe.enter_context(nc.sbuf_tensor("rstd2", [P, B], F32))
            layer0_attention(nc, m, x, ctx, Wq, Wkv, Wout, Wg, W1, W2, W3, gate_w, down_w, slots_in)
            m["sem"] = sem
            experts(nc, m, bias, gate_w, down_w, slots_in, slots_out)
        layer1(nc, m, slots_out, gnorm, dnorm, out)


def layer0_attention(nc, m, x, ctx, Wq, Wkv, Wout, Wg, W1, W2, W3, gate_w, down_w, slots_in):
    X, CTX, ident, identh, identb = m["X"], m["CTX"], m["ident"], m["identh"], m["identb"]
    W13T, W2T, logits, ones, half = m["W13T"], m["W2T"], m["logits"], m["ones"], m["half"]
    SCALE = float(HD0) ** -0.5
    NB = B + 2
    with ExitStack() as stack:
        def sb(name, shape, dt=F32):
            return stack.enter_context(nc.sbuf_tensor("a_" + name, shape, dt))

        def sem(name):
            return m["sem"]("a_" + name)

        def bank(name):
            return stack.enter_context(nc.psum_tensor("a_" + name, [P, 512], F32))

        reg = m["R"][:, 0:2 * (2 * HC * H + 2 * H)].bitcast(F32)
        WqT = reg[:, 0:HC * H].rearrange("p (c f) -> p c f", c=HC)
        WoutT = reg[:, HC * H:2 * HC * H].rearrange("p (c f) -> p c f", c=HC)
        WkvT = reg[:, 2 * HC * H:2 * HC * H + 2 * H]
        WgT = sb("WgT", [P, HC, E])
        mask4 = sb("mask4", [P, HG, P], BF16)
        wn = sb("wn", [P, 3, H])
        pre = W13T[:, 0:2, :, :].rearrange("p e c n -> p (e c) n")
        prekv = W13T[:, 2, 0:2, :].rearrange("p c (t n) -> p (c t) n", n=P)
        preg = W13T[0:E, 3, 0, :]
        zero = W2T[:, E - 1, FC - 1, :]
        absn = sb("absn", [P, GATE_ABS + DOWN_ABS])
        xn = sb("xn", [P, H])
        cx = sb("cx", [P, L])
        xn2 = sb("xn2", [P, H])
        xT = sb("xT", [P, HC, P])
        x2T = sb("x2T", [P, HC, P])
        ctxT = sb("ctxT", [P, P])
        qT = sb("qT", [P, 2, HC, P])
        kT = sb("kT", [P, 2, HC, P])
        V = sb("V", [P, 2, NH0, HD0 + 1])
        mx = sb("mx", [P, 2, HG])
        spare = m["R"][:, 2 * (2 * HC * H + 2 * H):][:, 0:12 * H].bitcast(F32)
        D = spare[:, 0:2 * H].rearrange("p (g h k) -> p g h k", g=2, h=HG)
        PT = spare[:, 2 * H:4 * H].rearrange("p (g h k) -> p g h k", g=2, h=HG)
        On = spare[:, 4 * H:5 * H]
        OT = spare[:, 5 * H:6 * H].rearrange("p (c n) -> p c n", c=HC)
        rden = sb("rden", [P, 2, 8])
        st = sb("st", [P, 2, 6])
        mv1 = sb("mv1", [P, 2])
        rs1 = sb("rs1", [P, 1])
        mv2 = sb("mv2", [P, 2])
        rs2 = sb("rs2", [P, 1])

        S = [bank("S0"), bank("S1")]
        T = [bank("T0"), bank("T1")]
        Fb = bank("F")
        Dk = bank("Dk")
        O = [bank("O0"), bank("O1")]

        ld_x, ld_ctx, ld_w = [sem("ld_x0"), sem("ld_x1")], sem("ld_ctx"), sem("ld_w")
        ld_stage, ld_abs = sem("ld_stage"), sem("ld_abs")
        zeroed, filled = sem("zeroed"), sem("filled")
        consts, consts_dve = sem("consts"), sem("consts_dve")
        pre_t, pre_e = sem("pre_t"), sem("pre_e")
        front = ["xT", "cT", "K", "Q", "V"]
        att = ["T0", "T1", "T2", "T3", "W0", "W1", "W2"]
        tail = ["OT", "x2T"]
        ready = {k: sem("ready_" + k) for k in front + att + tail}
        evac = {k: sem("evac_" + k) for k in front + att + tail}
        s_done, s_max, s_sub, s_exp = sem("s_done"), sem("s_max"), sem("s_sub"), sem("s_exp")
        pv_done, o_done = sem("pv_done"), sem("o_done")
        rstd1_done, rstd2_done = sem("rstd1_done"), sem("rstd2_done")
        stats1, stats2, xn_done, xn2_done = sem("stats1"), sem("stats2"), sem("xn_done"), sem("xn2_done")
        y_done, x2_done, r_done, l_done = sem("y_done"), sem("x2_done"), sem("r_done"), sem("l_done")
        abs_done, cx_done = sem("abs_done"), sem("cx_done")
        dve_steps, pool_steps = sem("dve_steps"), sem("pool_steps")

        def count(kind, b):
            return b + 1 if kind in front else b if kind in att else b - 1

        def has(kind, b):
            if not isinstance(b, int):
                return True
            return 0 <= count(kind, b) - 1 < B

        ring = {"T": ["OT", "T0", "xT", "T1", "T2", "T3", "x2T"], "F": ["cT", "K", "W0", "Q", "W1", "V", "W2"]}
        where = {k: (r, i) for r, ks in ring.items() for i, k in enumerate(ks)}

        def before(kind, b):
            r, i = where[kind]
            ks, back = ring[r], 2 if r == "T" else 1
            while True:
                i -= back
                if i < 0:
                    i, b = i + len(ks), b - 1
                if has(ks[i], b) or (isinstance(b, int) and b < 0):
                    return ks[i], b

        def tbank(kind, p):
            return T[(p * len(ring["T"]) + where[kind][1]) % 2]

        pre_jobs = [("q", r) for r in range(HC)] + [("kv", r) for r in range(2)] + [("o", r) for r in range(HC)] \
            + [("g", 0)]

        block = stack.enter_context(nc.Block())

        @block.sync
        def _(sp):
            sp.dma_start(X[:, 0:2, :], x[0:2].rearrange("b p d -> p b d")).then_inc(ld_x[0], 16)
            sp.dma_start(CTX[:], ctx.rearrange("b p d -> p b d")).then_inc(ld_ctx, 16)
            sp.dma_start(pre[:, 0:HC, :], Wq.rearrange("(t p) n -> p t n", p=P)).then_inc(ld_w, 16)
            sp.dma_start(prekv, Wkv.rearrange("(t p) n -> p t n", p=P)).then_inc(ld_w, 16)
            sp.dma_start(pre[:, HC:2 * HC, :], Wout.rearrange("(t p) n -> p t n", p=P)).then_inc(ld_w, 16)
            sp.dma_start(preg, Wg).then_inc(ld_w, 16)
            sp.dma_start(X[:, 2:B, :], x[2:B].rearrange("b p d -> p b d")).then_inc(ld_x[1], 16)

            def body(b, p, j):
                e, e_half = j - 1 + p, 1 - p
                if has("W0", b):
                    need(sp, ready["W2"], b - 1)
                    rows = slice(e_half * P, (e_half + 1) * P)
                    if isinstance(e, int):
                        w1, w3, w2 = W1[e], W3[e], W2[e]
                    else:
                        w1, w3, w2 = (w[bass.ds(e, 1)].rearrange("o a b -> (o a) b") for w in (W1, W3, W2))
                    sp.dma_start(wn[:, 0, :], w1[rows, :]).then_inc(ld_stage, 16)
                    sp.dma_start(wn[:, 1, :], w3[rows, :]).then_inc(ld_stage, 16)
                    sp.dma_start(wn[:, 2, :].rearrange("p (t n) -> p t n", n=P),
                                 w2[:, rows].rearrange("(t p) n -> p t n", p=P)).then_inc(ld_stage, 16)
                if has("xT", b):
                    need(sp, abs_done, b)
                    gf = gate_w.rearrange("(p a) b -> p (a b)", p=P)
                    df = down_w.rearrange("(p a) b -> p (a b)", p=P)
                    sp.dma_start(absn[:, 0:GATE_ABS], gf[:, bass.ds(b * GATE_ABS, GATE_ABS)]).then_inc(ld_abs, 16)
                    sp.dma_start(absn[:, GATE_ABS:], df[:, bass.ds(b * DOWN_ABS, DOWN_ABS)]).then_inc(ld_abs, 16)
                if isinstance(b, int) and b == 1:
                    sp.wait_ge(zeroed, 1)
                    for t in range(4):
                        n = SLOTS // 4
                        sp.dma_start(slots_in[t * n:(t + 1) * n, :].rearrange("(k p) d -> p k d", p=P),
                                     zero[:, None, :].broadcast_to([P, n // P, H])).then_inc(filled, 16)

            bodies(sp, NB, body)
            sp.wait_ge(filled, 64)

        @block.gpsimd
        def _(pool):
            step = Steps(pool, pool_steps)
            step.then(pool.memset(ident[:], 0.0))
            pool.affine_select(out=ident[:], in_=ident[:], compare_op=ALU.not_equal, fill=1.0, base=0,
                               pattern=[[-1, P]], channel_multiplier=1).then_inc(consts, 1)
            step.then(pool.memset(mask4[:], 0.0))
            pool.affine_select(out=mask4[:], in_=mask4[:], compare_op=ALU.is_ge, fill=NEG, base=0,
                               pattern=[[0, HG], [-1, P]], channel_multiplier=1).then_inc(consts, 1)
            pool.memset(half[:], -0.5).then_inc(consts, 1)
            pool.memset(V[:, :, :, HD0:HD0 + 1], 1.0).then_inc(consts, 1)
            pool.memset(ones[:], 1.0).then_inc(consts, 1)
            pool.memset(zero, 0.0).then_inc(zeroed, 1)
            pool.wait_ge(consts, 5)
            pool.tensor_copy(identh[:], ident[:]).then_inc(consts, 1)
            pool.tensor_copy(identb[:], ident[:]).then_inc(consts, 1)
            pool.wait_ge(consts, 7)
            first = step.n
            step.per, step.alone = 2, True

            def body(b, p, j):
                step.base, step.n = first + b * 2, 0
                if has("xT", b):
                    if isinstance(b, int) and b == 0:
                        pool.wait_ge(ld_ctx, 16)
                    need(pool, ready["cT"], b, True)
                    pool.tensor_copy(cx[:], at(CTX, b)).then_inc(cx_done, 1)
                    need(pool, stats1, b + 1, True)
                    need(pool, xn_done, b, True)
                    step.then(pool.tensor_scalar(rs1[:], mv1[:, 1:2], EPS, None, ALU.add))
                    pool.tensor_tensor(rs1[:], rs1[:], half[:], ALU.pow).then_inc(rstd1_done, 1)
                if has("OT", b):
                    need(pool, stats2, b - 1, True)
                    need(pool, xn2_done, b - 2, True)
                    step.then(pool.tensor_scalar(rs2[:], mv2[:, 1:2], EPS, None, ALU.add))
                    pool.tensor_tensor(rs2[:], rs2[:], half[:], ALU.pow).then_inc(rstd2_done, 1)
                step.end()

            bodies(pool, NB, body)

        @block.tensor
        def _(pe):
            pe.wait_ge(consts, 7)
            pe.wait_ge(ld_w, 64)
            for n, (kind, r) in enumerate(pre_jobs):
                if n >= 2:
                    pe.wait_ge(pre_e, n - 1)
                bk = T[n % 2]
                if kind == "g":
                    for c in range(HC):
                        last = pe.transpose(bk[:, c * E:(c + 1) * E], preg[:, c * P:(c + 1) * P], ident[0:E, 0:E])
                else:
                    for c in range(4):
                        src = (pre[:, r, c * P:(c + 1) * P] if kind == "q" else prekv[:, 4 * r + c, :] if kind == "kv"
                               else pre[:, HC + r, c * P:(c + 1) * P])
                        last = pe.transpose(bk[:, c * P:(c + 1) * P], src, ident[:])
                last.then_inc(pre_t, 1)
            pe.wait_ge(pre_e, len(pre_jobs))

            def free(kind, b):
                k, bb = before(kind, b)
                need(pe, evac[k], count(k, bb))

            def scores(b, p, g):
                q = 1 - p
                n = 4 * b - 4 + g
                need(pe, s_sub, n - 1)
                if g == 0:
                    pe.wait_ge(evac["Q"], b)
                    pe.wait_ge(evac["K"], b)
                bk, rows = S[g % 2], slice(HD0 * g, HD0 * (g + 1))
                pe.matmul(bk[:], identb[:], mask4[:].rearrange("p a b -> p (a b)"), start=True, stop=False)
                for c in range(HG):
                    last = pe.matmul(bk[:, c * P:(c + 1) * P], qT[rows, q, c, :], kT[rows, q, c, :],
                                     start=False, stop=(c == HG - 1), tile_position=(HD0 * g, 0))
                last.then_inc(s_done, 1)

            def probs_t(b, p, g):
                pe.wait_ge(s_exp, 4 * b - 3 + g)
                free(f"T{g}", b)
                bk = tbank(f"T{g}", p)
                for j in range(HG):
                    last = pe.transpose(bk[:, j * P:(j + 1) * P], D[:, g % 2, j, :], ident[:])
                last.then_inc(ready[f"T{g}"], 1)

            def pv(b, p, g):
                q = 1 - p
                pe.wait_ge(evac[f"T{g}"], b)
                if g == 0:
                    pe.wait_ge(evac["V"], b)
                if g % 2 == 0:
                    need(pe, o_done, 2 * b - 3 + g // 2)
                for j in range(HG):
                    c = (4 * (g % 2) + j) * (HD0 + 1)
                    last = pe.matmul(O[g // 2][:, c:c + HD0 + 1], PT[:, g % 2, j, :], V[:, q, 4 * j + g, :],
                                     start=True, stop=True)
                last.then_inc(pv_done, 1)

            def four(kind, b, p, src, wait, value):
                need(pe, wait, value)
                free(kind, b)
                bk = tbank(kind, p)
                for c in range(HC):
                    last = pe.transpose(bk[:, c * P:(c + 1) * P], src[:, c * P:(c + 1) * P], ident[:])
                last.then_inc(ready[kind], 1)

            def weights(b, p, j, k):
                if k == 0:
                    pe.wait_ge(ld_stage, 48 * b)
                free(f"W{k}", b)
                for c in range(4):
                    last = pe.transpose(Fb[:, c * P:(c + 1) * P], wn[:, k, c * P:(c + 1) * P], ident[:])
                last.then_inc(ready[f"W{k}"], 1)

            def body(b, p, j):
                a, f, t = has("T0", b), has("xT", b), has("OT", b)
                if a:
                    scores(b, p, 0)
                    scores(b, p, 1)
                if t:
                    four("OT", b, p, On, o_done, 2 * b - 2)
                if a:
                    probs_t(b, p, 0)
                if f:
                    four("xT", b, p, xn, xn_done, b + 1)
                    pe.wait_ge(cx_done, b + 1)
                    free("cT", b)
                    pe.transpose(Fb[:, 0:P], cx[:], ident[:]).then_inc(ready["cT"], 1)
                if a:
                    pv(b, p, 0)
                    scores(b, p, 2)
                if t:
                    pe.wait_ge(evac["OT"], b - 1)
                    need(pe, l_done, b - 2)
                    for c in range(HC):
                        last = pe.matmul(Dk[:], OT[:, c, :], WoutT[:, c, :], start=(c == 0), stop=(c == HC - 1))
                    last.then_inc(y_done, 1)
                if a:
                    probs_t(b, p, 1)
                if f:
                    pe.wait_ge(evac["cT"], b + 1)
                    for g in range(HC):
                        last = pe.matmul(Fb[:, g * P:(g + 1) * P], WkvT[:, g * P:(g + 1) * P], ctxT[:],
                                         start=True, stop=True)
                    last.then_inc(ready["K"], 1)
                if a:
                    pv(b, p, 1)
                    scores(b, p, 3)
                    weights(b, p, j, 0)
                    probs_t(b, p, 2)
                if f:
                    pe.wait_ge(evac["xT"], b + 1)
                    free("Q", b)
                    for g in range(HC):
                        for c in range(HC):
                            last = pe.matmul(Fb[:, g * P:(g + 1) * P], WqT[:, c, g * P:(g + 1) * P], xT[:, c, :],
                                             start=(c == 0), stop=(c == HC - 1))
                    last.then_inc(ready["Q"], 1)
                if a:
                    pv(b, p, 2)
                    weights(b, p, j, 1)
                    probs_t(b, p, 3)
                if f:
                    free("V", b)
                    pe.matmul(Fb[:], ctxT[:], WkvT[:, H:2 * H], start=True, stop=True).then_inc(ready["V"], 1)
                if t:
                    four("x2T", b, p, xn2, xn2_done, b - 1)
                if a:
                    weights(b, p, j, 2)
                    pv(b, p, 3)
                if t:
                    pe.wait_ge(evac["x2T"], b - 1)
                    pe.wait_ge(x2_done, b - 1)
                    for c in range(HC):
                        last = pe.matmul(Dk[:, 0:E], x2T[:, c, :], WgT[:, c, :], start=(c == 0), stop=(c == HC - 1))
                    last.then_inc(r_done, 1)

            bodies(pe, NB, body)

        @block.scalar
        def _(act):
            for n, (kind, r) in enumerate(pre_jobs):
                act.wait_ge(pre_t, n + 1)
                bk = T[n % 2]
                if kind == "g":
                    dst, src = WgT[:], bk[:, 0:HC * E].rearrange("p (c e) -> p c e", c=HC)
                elif kind == "kv":
                    dst, src = WkvT[:, 4 * P * r:4 * P * (r + 1)], bk[:]
                else:
                    dst = (WqT if kind == "q" else WoutT)[:, :, r * P:(r + 1) * P]
                    src = bk[:].rearrange("p (c f) -> p c f", c=HC)
                act.copy(dst, src).then_inc(pre_e, 1)

            def take(kind, b, dst, src):
                act.wait_ge(ready[kind], count(kind, b))
                act.copy(dst, src).then_inc(evac[kind], 1)

            def chunked(bk):
                return bk[:].rearrange("p (c n) -> p c n", c=4)

            def exps(b, g):
                n = 4 * b - 4 + g
                act.wait_ge(s_sub, n + 1)
                act.activation(D[:, g % 2], D[:, g % 2], ACT.Exp, scale=SCALE).then_inc(s_exp, 1)

            def take_probs(b, p, g):
                n = 4 * b - 4 + g
                need(act, pv_done, n - 1)
                take(f"T{g}", b, PT[:, g % 2], chunked(tbank(f"T{g}", p)))

            def weights(b, p, j, k):
                e, half_e = j - 1 + p, 1 - p
                if k == 2 and isinstance(b, int) and b == B:
                    act.wait_ge(filled, 64)
                if k < 2:
                    lo = k * FF + half_e * P
                    take(f"W{k}", b, at(W13T, e, slice(None), slice(lo, lo + P)), chunked(Fb))
                else:
                    take("W2", b, at(W2T, e, half_e), Fb[:])

            def body(b, p, j):
                a, f, t = has("T0", b), has("xT", b), has("OT", b)
                q = 1 - p
                if a:
                    exps(b, 0)
                if t:
                    need(act, y_done, b - 2)
                    take("OT", b, OT, chunked(tbank("OT", p)))
                if a:
                    exps(b, 1)
                    take_probs(b, p, 0)
                if f:
                    need(act, ready["Q"], b)
                    take("xT", b, xT[:], chunked(tbank("xT", p)))
                    need(act, ready["V"], b)
                    take("cT", b, ctxT[:], Fb[:, 0:P])
                if a:
                    exps(b, 2)
                    take_probs(b, p, 1)
                if f:
                    take("K", b, kT[:, p], chunked(Fb))
                if a:
                    exps(b, 3)
                    weights(b, p, j, 0)
                    take_probs(b, p, 2)
                if f:
                    take("Q", b, qT[:, p], chunked(Fb))
                if a:
                    weights(b, p, j, 1)
                    take_probs(b, p, 3)
                if f:
                    need(act, pv_done, 4 * b - 4)
                    take("V", b, V[:, p, :, 0:HD0], Fb[:].rearrange("p (h d) -> p h d", h=NH0))
                if t:
                    need(act, r_done, b - 2)
                    take("x2T", b, x2T[:], chunked(tbank("x2T", p)))
                if a:
                    weights(b, p, j, 2)

            bodies(act, NB, body)

        @block.vector
        def _(dve):
            step = Steps(dve, dve_steps, per=7, alone=True)

            def ln_stats(src, dst, k, signal):
                step.then(dve.bn_stats(st[:, k, :], src))
                dve.bn_aggr(dst, st[:, k, :]).then_inc(signal, 1)

            def normalise(dst, src, mv, rs, signal):
                dve.tensor_scalar(dst[:], src, mv[:, 0:1], rs[:], ALU.subtract, ALU.mult).then_inc(signal, 1)

            def softmax_head(b, g):
                n = 4 * b - 4 + g
                dve.wait_ge(s_done, n + 1)
                bk = S[g % 2][:].rearrange("p (h k) -> p h k", h=HG)
                dve.tensor_reduce(mx[:, g % 2, :], bk, AX.X, ALU.max).then_inc(s_max, 1)
                dve.wait_ge(s_max, n + 1)
                if g >= 2:
                    dve.wait_ge(ready[f"T{g - 2}"], b)
                else:
                    need(dve, ready[f"T{g + 2}"], b - 1)
                dve.tensor_tensor(D[:, g % 2], bk, mx[:, g % 2, :, None].broadcast_to([P, HG, P]),
                                  ALU.subtract).then_inc(s_sub, 1)

            def out_half(b, p, k):
                q = 1 - p
                dve.wait_ge(pv_done, 4 * b - 4 + 2 * k + 2)
                bk = O[k][:, 0:8 * (HD0 + 1)].rearrange("p (h d) -> p h d", h=8)
                step.then(dve.reciprocal(rden[:, k, :], bk[:, :, HD0]))
                need(dve, ready["OT"], b - 1)
                four = "p (g c) d -> p g c d"
                rd = rden[:, k, :, None].broadcast_to([P, 8, HD0])
                dve.tensor_tensor(On.rearrange("p (c g d) -> p g c d", g=HG, d=HD0)[:, 2 * k:2 * k + 2],
                                  bk[:, :, 0:HD0].rearrange(four, g=2), rd.rearrange(four, g=2),
                                  ALU.mult).then_inc(o_done, 1)

            def body(b, p, j):
                a, f, t = has("T0", b), has("xT", b), has("OT", b)
                step.body(b)
                if f:
                    if isinstance(b, int) and b < 2:
                        dve.wait_ge(ld_x[b], 16)
                    ln_stats(at(X, b), mv1[:], 0, stats1)
                if a:
                    softmax_head(b, 0)
                    softmax_head(b, 1)
                if f:
                    need(dve, rstd1_done, b + 1)
                    need(dve, ready["xT"], b)
                    normalise(xn, at(X, b), mv1, rs1, xn_done)
                if a:
                    softmax_head(b, 2)
                if t:
                    dve.wait_ge(y_done, b - 1)
                    xb = at(X, b - 2)
                    dve.tensor_tensor(xb, Dk[:], xb, ALU.add).then_inc(x2_done, 1)
                    need(dve, x2_done, b - 1, True)
                    ln_stats(xb, mv2[:], 1, stats2)
                if a:
                    softmax_head(b, 3)
                if t:
                    need(dve, rstd2_done, b - 1)
                    need(dve, ready["x2T"], b - 2)
                    normalise(xn2, xb, mv2, rs2, xn2_done)
                    step.mark(dve.tensor_copy(at(m["stats2"], b - 2), mv2[:]))
                    step.mark(dve.tensor_copy(m["rstd2"][:, bass.ds(b - 2, 1)], rs2[:]))
                if a:
                    out_half(b, p, 0)
                if f:
                    dve.wait_ge(ld_abs, 32 * (b + 1))
                    bb = bass.ds(b, 1)
                    step.mark(dve.tensor_reduce(m["absum"][:, 0, bb], absn[:, 0:GATE_ABS], AX.X, ALU.add,
                                                apply_absolute_value=True))
                    dve.tensor_reduce(m["absum"][:, 1, bb], absn[:, GATE_ABS:], AX.X, ALU.add,
                                      apply_absolute_value=True).then_inc(abs_done, 1)
                if a:
                    out_half(b, p, 1)
                if t:
                    dve.wait_ge(r_done, b - 1)
                    dve.tensor_copy(at(logits, b - 2), Dk[:, 0:E]).then_inc(l_done, 1)
                step.end()

            bodies(dve, NB, body)


def experts(nc, m, bias, gate_w, down_w, slots_in, slots_out):
    X, W13T, W2T, logits, ones = m["X"], m["W13T"], m["W2T"], m["logits"], m["ones"]
    ident, identb = m["ident"], m["identb"]
    gateT = m["R"][:, 0:HC * 2 * INTER].rearrange("p (c n) -> p c n", c=HC)
    downT = m["R"][:, HC * 2 * INTER:].rearrange("p (c n) -> p c n", c=IC)
    NB = SLOT_TILES + 2
    XS = 4
    with ExitStack() as stack:
        def sb(name, shape, dt=F32):
            return stack.enter_context(nc.sbuf_tensor("e_" + name, shape, dt))

        def sem(name):
            return m["sem"]("e_" + name)

        def bank(name, dt=F32):
            return stack.enter_context(nc.psum_tensor("e_" + name, [P, 2048 // mybir.dt.size(dt)], dt))

        brow = sb("brow", [1, E])
        prob = sb("prob", [P, B, E])
        score = sb("score", [P, B, E])
        tmp = sb("tmp", [P, B, E])
        pick = sb("pick", [P, 2, B, E])
        both = sb("both", [P, B, E], BF16)
        best = sb("best", [P, B])
        den = sb("den", [P, B])
        iota = sb("iota", [P, SLOT_TILES])
        order = sb("order", [P, E])
        tri = sb("tri", [P, P], BF16)
        onesb = sb("onesb", [P, P], BF16)
        tiles = sb("tiles", [P, E])
        upto = sb("upto", [P, E])
        base = sb("base", [P, E])
        cmp = sb("cmp", [1, SLOT_TILES, E])
        whichf = sb("whichf", [1, SLOT_TILES])
        which = sb("which", [1, SLOT_TILES], I32)
        asum = sb("asum", [P, 2])
        xs = sb("xs", [P, XS, H])
        slot = sb("slot", [P, XS, 2], U32)
        xg, y = xs[:, 0:2, :], xs[:, 2:4, :]
        xT = sb("xT", [P, 2, HC, P])
        sg = sb("sg", [P, FF])
        g = sb("g", [P, 2, FF])
        gT = sb("gT", [P, FC, P])
        wst = sb("wst", [P, 2, H])
        wr = sb("wr", [P, H])
        wq = sb("wq", [P, 2, H], BF16)

        XB = [bank("X0"), bank("X1")]
        GB = bank("G")
        HB = [bank("H0"), bank("H1")]
        YB = [bank("Y0"), bank("Y1")]
        WB = bank("W", BF16)

        ld_b, cst, s_exp, s_bias, s_cnt, s_both = (sem(k) for k in ("ld_b", "cst", "exp", "bias", "cnt", "both"))
        s_sum, s_mean, s_pos, s_table, steps = (sem(k) for k in ("sum", "mean", "pos", "table", "steps"))
        xs_ready = sem("xs_ready")
        sent = [sem(f"sent{k}") for k in range(XS)]
        ld_xg = [sem("ld_xg0"), sem("ld_xg1")]
        ld_wst = [sem("ld_wst0"), sem("ld_wst1")]
        x_t, x_e, h_done, silu_done, g_done, g_t, g_e, y_done, y_e = (
            sem(k) for k in ("x_t", "x_e", "h_done", "silu_done", "g_done", "g_t", "g_e", "y_done", "y_e"))
        stored = [sem("stored0"), sem("stored1")]
        wq_r, wq_m, wq_done, wq_t, wq_e = (sem(k) for k in ("wq_r", "wq_m", "wq_done", "wq_t", "wq_e"))

        def run(eng, body):
            jobs = GATE_TILES + IC
            assert GATE_TILES % 2 == 0 and jobs < SLOT_TILES
            body(0, 0, 0, "gate")
            body(1, 1, 0, "gate")
            with eng.Fori(1, GATE_TILES // 2) as j:
                for p in range(2):
                    body(j * 2 + p, p, j, "gate")
            with eng.Fori(GATE_TILES // 2, jobs // 2) as j:
                for p in range(2):
                    body(j * 2 + p, p, j, "down")
            j = jobs // 2
            if jobs % 2:
                body(2 * j, 0, j, "down")
                body(2 * j + 1, 1, j, None)
                j += 1
            with eng.Fori(j, NB // 2 - 1) as j:
                for p in range(2):
                    body(j * 2 + p, p, j, None)
            for p in range(2):
                body(NB - 2 + p, p, NB // 2 - 1, None)

        def stage(b, k):
            return not isinstance(b, int) or 0 <= b - k < SLOT_TILES

        block = stack.enter_context(nc.Block())

        @block.sync
        def _(sp):
            for s in m["first"]:
                sp.sem_clear(s)
            sp.dma_start(brow[:], bias.rearrange("(a n) -> a n", a=1)).then_inc(ld_b, 16)

            def body(b, p, j, job):
                if job:
                    need(sp, wq_r, b - 1)
                    if job == "gate":
                        sp.dma_start(wst[:, p, :], gate_w[bass.ds(b * P, P), :]).then_inc(ld_wst[p], 16)
                    else:
                        sp.dma_start(wst[:, p, :].rearrange("p (t n) -> p t n", n=P),
                                     down_w[:, bass.ds((b - GATE_TILES) * P, P)].rearrange("(t p) n -> p t n", p=P)
                                     ).then_inc(ld_wst[p], 16)
                if stage(b, 0):
                    if isinstance(b, int) and b == 0:
                        for k in range(XS):
                            sp.wait_ge(sent[k], 32 * B // XS)
                    need(sp, x_t, b - 1)
                    sp.dma_start(xg[:, p, :], slots_in[bass.ds(b * P, P), :]).then_inc(ld_xg[p], 16)
                if stage(b, 2):
                    sp.wait_ge(y_e, b - 1)
                    sp.dma_start(slots_out[bass.ds((b - 2) * P, P), :], y[:, p, :]).then_inc(stored[p], 16)

            run(sp, body)
            for p in range(2):
                sp.wait_ge(stored[p], 16 * SLOT_TILES // 2)

        @block.gpsimd
        def _(pool):
            pool.memset(onesb[:], 1.0).then_inc(cst, 1)
            pool.wait_ge(cst, 1)
            pool.affine_select(out=tri[:], in_=onesb[:], compare_op=ALU.is_ge, fill=0.0, base=-1,
                               pattern=[[1, P]], channel_multiplier=-1).then_inc(cst, 1)
            pool.wait_ge(s_pos, 2)
            with pool.Fori(0, B // XS) as j:
                for k in range(XS):
                    need(pool, xs_ready, j * XS + k + 1, True)
                    for c in range(2):
                        pool.indirect_dma_start(
                            out=slots_in, out_offset=bass.IndirectOffsetOnAxis(
                                ap=slot[:, k, c:c + 1], axis=0),
                            in_=xs[:, k, :], in_offset=None).then_inc(sent[k], 16)
            for k in range(XS):
                pool.wait_ge(sent[k], 32 * B // XS)

        @block.tensor
        def _(pe):
            pe.wait_ge(ld_b, 16)
            pe.matmul(GB[:, 0:E], ones[0:1, :], brow[:], start=True, stop=True).then_inc(s_bias, 1)
            pe.wait_ge(s_sum, 1)
            pe.matmul(YB[0][:, 0:2], ones[:], asum[:], start=True, stop=True).then_inc(s_bias, 1)
            pe.wait_ge(s_both, 1)
            pe.wait_ge(cst, 2)
            ahead = XB[0][:, 0:B * E]
            pe.matmul(ahead, tri[:], both[:].rearrange("p b e -> p (b e)"), start=True, stop=False)
            for s in range(1, B):
                pe.matmul(ahead[:, s * E:], onesb[:], both[:, 0:B - s, :].rearrange("p b e -> p (b e)"),
                          start=False, stop=(s == B - 1))
            for s in range(B):
                last = pe.matmul(XB[1][:, 0:E], onesb[:], both[:, s, :], start=(s == 0), stop=(s == B - 1))
            last.then_inc(s_cnt, 1)
            pe.wait_ge(s_table, 1)

            def expert(i):
                pe.nop(nofuse=True)
                return pe.value_load(which[0:1, bass.ds(i, 1)], min_val=0, max_val=E - 1)

            def body(b, p, j, job):
                if stage(b, 2):
                    pe.wait_ge(g_done, b - 1)
                    need(pe, g_e, b - 2)
                    for c in range(FC):
                        last = pe.transpose(GB[:, c * P:(c + 1) * P], g[:, p, c * P:(c + 1) * P], ident[:])
                    last.then_inc(g_t, 1)
                if job:
                    pe.wait_ge(wq_done, b + 1)
                    need(pe, wq_e, b)
                    for c in range(4):
                        last = pe.transpose(WB[:, c * P:(c + 1) * P], wq[:, p, c * P:(c + 1) * P], identb[:])
                    last.then_inc(wq_t, 1)
                if stage(b, 0):
                    pe.wait_ge(ld_xg[p], 16 * (j + 1))
                    need(pe, x_e, b - 1)
                    for c in range(HC):
                        last = pe.transpose(XB[p][:, c * P:(c + 1) * P], xg[:, p, c * P:(c + 1) * P], ident[:])
                    last.then_inc(x_t, 1)
                if stage(b, 1):
                    pe.wait_ge(x_e, b)
                    need(pe, g_done, b - 2)
                    e = expert(b - 1)
                    for c in range(HC):
                        last = pe.matmul(HB[1 - p][:], xT[:, 1 - p, c, :], at(W13T, e, c), start=(c == 0),
                                         stop=(c == HC - 1))
                    last.then_inc(h_done, 1)
                if stage(b, 2):
                    pe.wait_ge(g_e, b - 1)
                    need(pe, y_e, b - 2)
                    e = expert(b - 2)
                    for c in range(FC):
                        last = pe.matmul(YB[p][:], gT[:, c, :], at(W2T, e, c), start=(c == 0), stop=(c == FC - 1))
                    last.then_inc(y_done, 1)

            run(pe, body)

        @block.scalar
        def _(act):
            act.activation(prob[:], logits[:], ACT.Exp, scale=-1.0).then_inc(s_exp, 1)

            def body(b, p, j, job):
                if stage(b, 2):
                    act.wait_ge(g_t, b - 1)
                    need(act, y_done, b - 2)
                    act.copy(gT[:], GB[:, 0:FF].rearrange("p (c n) -> p c n", c=FC)).then_inc(g_e, 1)
                if job:
                    act.wait_ge(wq_t, b + 1)
                    src = WB[:, 0:H]
                    if job == "gate":
                        act.copy(gateT[:, :, bass.ds(b * P, P)], src.rearrange("p (c n) -> p c n", c=HC)).then_inc(wq_e, 1)
                    else:
                        act.copy(at(downT, b - GATE_TILES), src).then_inc(wq_e, 1)
                if stage(b, 0):
                    act.wait_ge(x_t, b + 1)
                    need(act, h_done, b - 1)
                    act.copy(xT[:, p], XB[p][:].rearrange("p (c n) -> p c n", c=HC)).then_inc(x_e, 1)
                if stage(b, 1):
                    act.wait_ge(h_done, b)
                    need(act, g_done, b - 1)
                    act.activation(sg[:], HB[1 - p][:, 0:FF], ACT.Silu).then_inc(silu_done, 1)

            run(act, body)

        @block.vector
        def _(dve):
            step = Steps(dve, steps)
            then = step.then
            dve.tensor_reduce(asum[:], m["absum"][:], AX.X, ALU.add).then_inc(s_sum, 1)
            then(dve.tensor_tensor_scan(iota[:], ones[:, 0:SLOT_TILES], ones[:, 0:SLOT_TILES], -1.0,
                                        ALU.mult, ALU.add))
            then(dve.tensor_scalar(order[:], iota[:, 0:E], -1.0, float(E), ALU.mult, ALU.add))
            dve.wait_ge(s_bias, 2)
            for k, n in enumerate((2 * INTER * H, INTER * H)):
                step.mark(dve.tensor_scalar(m["wmean"][:, k:k + 1], YB[0][:, k:k + 1], 1.0 / n, 1e-5, ALU.mult, ALU.max))
            dve.wait_ge(steps, step.n)
            then(dve.reciprocal(m["wscale"][:], m["wmean"][:]))
            dve.wait_ge(s_exp, 1)
            then(dve.tensor_scalar(tmp[:], prob[:], 1.0, None, ALU.add))
            then(dve.reciprocal(prob[:], tmp[:]))
            then(dve.tensor_tensor(score[:], prob[:], GB[:, None, 0:E].broadcast_to([P, B, E]), ALU.add))

            def spread(t):
                return t[:, :, None].broadcast_to([P, B, E])

            for c in range(2):
                then(dve.tensor_reduce(best[:], score[:], AX.X, ALU.max))
                then(dve.tensor_tensor(tmp[:], score[:], spread(best), ALU.is_ge))
                then(dve.tensor_tensor(tmp[:], tmp[:], order[:, None, :].broadcast_to([P, B, E]), ALU.mult))
                then(dve.tensor_reduce(best[:], tmp[:], AX.X, ALU.max))
                then(dve.tensor_tensor(pick[:, c], tmp[:], spread(best), ALU.is_equal))
                if c == 0:
                    then(dve.scalar_tensor_tensor(score[:].rearrange("p b e -> p (b e)"),
                                                  pick[:, 0].rearrange("p b e -> p (b e)"), -BIG,
                                                  score[:].rearrange("p b e -> p (b e)"), ALU.mult, ALU.add))
            dve.tensor_tensor(both[:], pick[:, 0], pick[:, 1], ALU.add).then_inc(s_both, 1)
            for c in range(2):
                then(dve.tensor_tensor(tmp[:], prob[:], pick[:, c], ALU.mult))
                then(dve.tensor_reduce(m["wt"][:, c, :], tmp[:], AX.X, ALU.add))
            then(dve.tensor_tensor(den[:], m["wt"][:, 0, :], m["wt"][:, 1, :], ALU.add))
            then(dve.reciprocal(den[:], den[:]))
            then(dve.tensor_tensor(m["wt"][:], m["wt"][:], den[:, None, :].broadcast_to([P, 2, B]), ALU.mult))
            dve.wait_ge(s_cnt, 1)
            then(dve.tensor_scalar(tiles[:], XB[1][:, 0:E], P / 2 - 0.5, 1.0 / P, ALU.add, ALU.mult))
            then(dve.tensor_scalar(tiles[:], tiles[:], ROUND, -ROUND, ALU.add, ALU.add))
            then(dve.tensor_tensor_scan(upto[:], ones[:, 0:E], tiles[:], 0.0, ALU.mult, ALU.add))
            then(dve.tensor_tensor(base[:], upto[:], tiles[:], ALU.subtract))
            then(dve.tensor_scalar(base[:], base[:], float(P), None, ALU.mult))
            then(dve.tensor_tensor(score[:], XB[0][:, 0:B * E].rearrange("p (b e) -> p b e", e=E),
                                   base[:, None, :].broadcast_to([P, B, E]), ALU.add))
            for c in range(2):
                then(dve.tensor_tensor(tmp[:], score[:], pick[:, c], ALU.mult))
                then(dve.tensor_reduce(best[:], tmp[:], AX.X, ALU.add))
                dve.tensor_copy(m["pos"][:, c, :], best[:]).then_inc(s_pos, 1)
                dve.wait_ge(s_pos, c + 1)
            then(dve.tensor_tensor(cmp[:], upto[0:1, None, :].broadcast_to([1, SLOT_TILES, E]),
                                   iota[0:1, :, None].broadcast_to([1, SLOT_TILES, E]), ALU.is_le))
            then(dve.tensor_reduce(whichf[:], cmp[:], AX.X, ALU.add))
            dve.tensor_scalar(which[:], whichf[:], float(E - 1), None, ALU.min).then_inc(s_table, 1)
            with dve.Fori(0, B // XS) as j:
                for k in range(XS):
                    i = j * XS + k
                    dve.wait_ge(sent[k], 32 * j)
                    dve.tensor_copy(slot[:, k, :], m["pos"][:, :, bass.ds(i, 1)].rearrange("p c o -> p (c o)"))
                    dve.tensor_scalar(xs[:, k, :], at(X, i), at(m["stats2"], i, slice(0, 1)),
                                      m["rstd2"][:, bass.ds(i, 1)], ALU.subtract, ALU.mult).then_inc(xs_ready, 1)

            def body(b, p, j, job):
                if job:
                    k = 0 if job == "gate" else 1
                    dve.wait_ge(ld_wst[p], 16 * (j + 1))
                    need(dve, wq_done, b)
                    dve.tensor_scalar(wr[:], wst[:, p, :], m["wscale"][:, k:k + 1], ROUND, ALU.mult,
                                      ALU.add).then_inc(wq_r, 1)
                    dve.wait_ge(wq_r, b + 1)
                    need(dve, wq_t, b - 1)
                    dve.tensor_scalar(wr[:], wr[:], -ROUND, 1.0, ALU.add, ALU.min).then_inc(wq_m, 1)
                    dve.wait_ge(wq_m, b + 1)
                    dve.tensor_scalar(wq[:, p, :], wr[:], -1.0, None, ALU.max).then_inc(wq_done, 1)
                if stage(b, 1):
                    dve.wait_ge(silu_done, b)
                    need(dve, g_t, b - 2)
                    dve.tensor_tensor(g[:, 1 - p, :], HB[1 - p][:, FF:2 * FF], sg[:], ALU.mult).then_inc(g_done, 1)
                if stage(b, 2):
                    dve.wait_ge(y_done, b - 1)
                    need(dve, stored[p], 16 * (j - 1))
                    dve.tensor_copy(y[:, p, :], YB[p][:]).then_inc(y_e, 1)

            run(dve, body)


def layer1(nc, m, slots_out, gnorm, dnorm, out):
    X, CTX, ident, identh, identb, half = m["X"], m["CTX"], m["ident"], m["identh"], m["identb"], m["half"]
    gateT = m["R"][:, 0:HC * 2 * INTER].rearrange("p (c n) -> p c n", c=HC)
    downT = m["R"][:, HC * 2 * INTER:].rearrange("p (c n) -> p c n", c=IC)
    SCALE = float(HD1) ** -0.5
    NB = B + 4
    PARTS = 4
    HV = HD1 + 1
    OH = QH // 2
    with ExitStack() as stack:
        def sb(name, shape, dt=F32):
            return stack.enter_context(nc.sbuf_tensor("c_" + name, shape, dt))

        def sem(name):
            return m["sem"]("c_" + name)

        def bank(name):
            return stack.enter_context(nc.psum_tensor("c_" + name, [P, 512], F32))

        g1 = sb("g1", [P, H])
        g2 = sb("g2", [P, INTER])
        yg = sb("yg", [P, 2, 2, H])
        slot = sb("slot", [P, 2, 2], U32)
        xn = sb("xn", [P, H])
        qs = sb("qs", [P, QH, PARTS, HD1], F16)
        ks = sb("ks", [P, KVH, 2, PARTS, HD1], F16)
        qT = sb("qT", [P, 2, QH // 2, P], F16)
        kT = sb("kT", [P, 2, KVH, P], F16)
        V = sb("V", [P, 2, KVH, HV])
        D = sb("D", [P, 2, HG, P])
        mx = sb("mx", [P, 2, HG])
        PB = sb("PB", [P, 2, HG, P])
        PT = sb("PT", [P, 2, HG, P])
        On = sb("On", [P, H])
        rden = sb("rden", [P, 2, OH])
        st = sb("st", [P, 2, 6])
        mv3 = sb("mv3", [P, 2])
        rs3 = sb("rs3", [P, 1])
        mv4 = sb("mv4", [P, 2])
        nrm = sb("nrm", [P, 4])
        t1 = sb("t1", [P, H])
        am = sb("am", [P, 4])
        mq = sb("mq", [P, 1])
        dqg = sb("dqg", [P, 2])
        xq = sb("xq", [P, H], BF16)
        xqT = sb("xqT", [P, HC, P], BF16)
        th = sb("th", [P, H])
        ga = sb("ga", [P, H])
        h = sb("h", [P, INTER])
        hg = sb("hg", [P, INTER])
        junk = sb("junk", [P, INTER], BF16)
        ss = sb("ss", [P, 1])
        hn = sb("hn", [P, 4])
        ah = sb("ah", [P, 4])
        dqd = sb("dqd", [P, 1])
        hq = sb("hq", [P, INTER], BF16)
        hT = sb("hT", [P, IC, P], BF16)
        xo = sb("xo", [P, 2, H])

        S = [bank("S0"), bank("S1")]
        T = [bank("T0"), bank("T1")]
        O = [bank("O0"), bank("O1")]
        GB, UB = bank("G"), bank("U")

        ld_g = sem("ld_g")
        gathered = [sem("gathered0"), sem("gathered1")]
        stored = [sem("stored0"), sem("stored1")]
        kinds = ["T0", "hTa", "T1", "hTb", "T2", "xqT", "T3", "T4", "q0", "T5", "T6", "q1", "T7", "kT"]
        delay = {k: 1 for k in kinds}
        delay.update(hTa=3, hTb=3, xqT=2, q0=0, q1=0, kT=0)
        ready = {k: sem("ready_" + k) for k in kinds}
        evac = {k: sem("evac_" + k) for k in kinds}
        s_done, s_max, s_sub, s_exp, pv_done, o_done = (
            sem(k) for k in ("s_done", "s_max", "s_sub", "s_exp", "pv_done", "o_done"))
        slot_set = sem("slot_set")
        v_set, x3_a, x3_done, stats3, xn_done, qs_done, ks_done, v_done = (
            sem(k) for k in ("v_set", "x3_a", "x3_done", "stats3", "xn_done", "qs_done", "ks_done", "v_done"))
        x4_done, stats4, nrm_done, mq_done, xr_done, xq_done = (
            sem(k) for k in ("x4_done", "stats4", "nrm_done", "mq_done", "xr_done", "xq_done"))
        gu_done, th_done, ga_done, h_done = (sem(k) for k in ("gu_done", "th_done", "ga_done", "h_done"))
        ss_done, hg_done, hn_done, mh_done, hr_done, hq_done, down_done, out_done = (
            sem(k) for k in ("ss_done", "hg_done", "hn_done", "mh_done", "hr_done", "hq_done", "down_done", "out_done"))
        dve_steps, pool_steps = sem("dve_steps"), sem("pool_steps")

        def stage(b, k):
            return not isinstance(b, int) or 0 <= b - k < B

        def before(kind, b):
            i = kinds.index(kind)
            while True:
                i -= 2
                if i < 0:
                    i, b = i + len(kinds), b - 1
                if stage(b, delay[kinds[i]]) or (isinstance(b, int) and b < 0):
                    return kinds[i], b

        def tbank(kind):
            return T[kinds.index(kind) % 2]

        block = stack.enter_context(nc.Block())

        @block.sync
        def _(sp):
            sp.dma_start(g1[:], gnorm.rearrange("(a n) -> a n", a=1).broadcast_to([P, H])).then_inc(ld_g, 16)
            sp.dma_start(g2[:], dnorm.rearrange("(a n) -> a n", a=1).broadcast_to([P, INTER])).then_inc(ld_g, 16)

            def body(b, p, j):
                if stage(b, 3):
                    sp.wait_ge(out_done, b - 2)
                    sp.dma_start(out[bass.ds(b - 3, 1)].rearrange("o p d -> (o p) d"), xo[:, 1 - p, :]
                                 ).then_inc(stored[1 - p], 16)

            bodies(sp, NB, body, head=2, tail=3)
            for p in range(2):
                sp.wait_ge(stored[p], 16 * B // 2)

        @block.gpsimd
        def _(pool):
            step = Steps(pool, pool_steps, per=15, alone=True)

            def gather(b, p):
                need(pool, x3_done, b - 1, True)
                pool.tensor_copy(slot[:, p, :], m["pos"][:, :, bass.ds(b, 1)].rearrange("p c o -> p (c o)")
                                 ).then_inc(slot_set, 1)
                need(pool, slot_set, b + 1, True)
                for c in range(2):
                    pool.indirect_dma_start(out=yg[:, p, c, :], out_offset=None, in_=slots_out,
                                            in_offset=bass.IndirectOffsetOnAxis(
                                                ap=slot[:, p, c:c + 1], axis=0)).then_inc(gathered[p], 16)

            pool.memset(V[:, :, :, HD1:HV], 1.0).then_inc(v_set, 1)
            pool.wait_ge(v_set, 1)
            gather(0, 0)

            def body(b, p, j):
                step.body(b)
                if stage(b + 1, 0):
                    gather(b + 1, 1 - p)
                if stage(b, 2):
                    need(pool, stats4, b - 1, True)
                    r, v, f, g = (nrm[:, k:k + 1] for k in range(4))
                    step.then(pool.tensor_scalar(v, mv4[:, 1:2], EPS, None, ALU.add))
                    step.then(pool.tensor_tensor(r, v, half[:], ALU.pow))
                    step.then(pool.tensor_tensor(f, r, r, ALU.mult))
                    step.then(pool.tensor_scalar(f, f, mv4[:, 1:2], EPS, ALU.mult, ALU.add))
                    step.then(pool.tensor_tensor(f, f, half[:], ALU.pow))
                    pool.tensor_tensor(g, r, f, ALU.mult).then_inc(nrm_done, 1)
                if stage(b, 0):
                    kv = at(CTX, b).rearrange("p (k d) -> p k d", d=HD1)[:, :, None, :].broadcast_to([P, KVH, 4, HD1])
                    kview = ks[:].rearrange("p k r (a s) d -> p k (r a) s d", s=2)
                    need(pool, ready["kT"], b, True)
                    step.then(pool.tensor_copy(kview[:, :, :, 0, :], kv))
                    pool.tensor_tensor(kview[:, :, :, 1, :], kv, kview[:, :, :, 0, :], ALU.subtract).then_inc(ks_done, 1)
                    need(pool, pv_done, 8 * b - 8, True)
                    pool.tensor_copy(V[:, p, :, 0:HD1],
                                     at(CTX, b).rearrange("p (k d) -> p k d", d=HD1)).then_inc(v_done, 1)
                    need(pool, stats3, b + 1, True)
                    step.then(pool.tensor_scalar(rs3[:], mv3[:, 1:2], EPS, None, ALU.add))
                    step.then(pool.tensor_tensor(rs3[:], rs3[:], half[:], ALU.pow))
                    need(pool, qs_done, b, True)
                    step.then(pool.tensor_tensor(xn[:], at(X, b), mv3[:, 0:1].broadcast_to([P, H]), ALU.subtract))
                    pool.tensor_tensor(xn[:], xn[:], rs3[:].broadcast_to([P, H]), ALU.mult).then_inc(xn_done, 1)
                    need(pool, xn_done, b + 1, True)
                    need(pool, ready["q1"], b, True)
                    xv = xn[:].rearrange("p (h d) -> p h d", d=HD1)[:, :, None, :].broadcast_to([P, QH, 2, HD1])
                    step.then(pool.tensor_copy(qs[:, :, 0:2, :], xv))
                    pool.tensor_tensor(qs[:, :, 2:4, :], xv, qs[:, :, 0:2, :], ALU.subtract).then_inc(qs_done, 1)
                if stage(b, 2):
                    need(pool, mq_done, b - 1, True)
                    pool.tensor_scalar(t1[:], t1[:], mq[:], ROUND, ALU.mult, ALU.add).then_inc(xr_done, 1)
                    need(pool, h_done, 3 * (b - 1), True)
                    need(pool, hq_done, b - 2, True)
                    pool.tensor_tensor(hg[:], h[:], g2[:], ALU.mult).then_inc(hg_done, 1)
                    need(pool, ss_done, b - 1, True)
                    c2, v2, r2, f2 = (hn[:, k:k + 1] for k in range(4))
                    step.then(pool.tensor_tensor(c2, dqg[:, 0:1], dqg[:, 1:2], ALU.mult))
                    step.then(pool.tensor_tensor(v2, c2, c2, ALU.mult))
                    step.then(pool.tensor_scalar(v2, v2, ss[:], 1.0 / INTER, ALU.mult, ALU.mult))
                    step.then(pool.tensor_scalar(v2, v2, EPS, None, ALU.add))
                    step.then(pool.tensor_tensor(r2, v2, half[:], ALU.pow))
                    pool.tensor_tensor(f2, r2, c2, ALU.mult).then_inc(hn_done, 1)
                    need(pool, mh_done, b - 1, True)
                    pool.tensor_scalar(hg[:], hg[:], ah[:, 2:3], ROUND, ALU.mult, ALU.add).then_inc(hr_done, 1)
                if stage(b, 1):
                    need(pool, o_done, 2 * b, True)
                    xb = at(X, b - 1)
                    pool.tensor_tensor(xb, xb, On[:], ALU.add).then_inc(x4_done, 1)
                step.end()

            bodies(pool, NB, body, head=2, tail=3)

        @block.tensor
        def _(pe):
            def free(kind, b):
                k, bb = before(kind, b)
                need(pe, evac[k], bb - delay[k] + 1)

            def scores(b, p, g):
                q = 1 - p
                n = 8 * b - 8 + g
                need(pe, s_sub, n - 1)
                if g == 0:
                    pe.wait_ge(evac["q1"], b)
                    pe.wait_ge(evac["kT"], b)
                r = 64 * (g % 2)
                for j in range(HG):
                    pair = g // 2 * 4 + j
                    last = pe.matmul(S[g % 2][:, j * P:(j + 1) * P], qT[r:r + 64, q, pair, :],
                                     kT[r:r + 64, q, pair // 2, :], start=True, stop=True, tile_position=(r, 0))
                last.then_inc(s_done, 1)

            def probs_t(b, p, g):
                pe.wait_ge(s_exp, 8 * b - 7 + g)
                free(f"T{g}", b)
                for j in range(HG):
                    last = pe.transpose(tbank(f"T{g}")[:, j * P:(j + 1) * P], PB[:, g % 2, j, :], ident[:])
                last.then_inc(ready[f"T{g}"], 1)

            def pv(b, p, g):
                q = 1 - p
                pe.wait_ge(evac[f"T{g}"], b)
                if g == 0:
                    pe.wait_ge(v_done, b)
                if g % 4 == 0:
                    need(pe, o_done, 2 * b - 3 + g // 4)
                for j in range(HG):
                    pair = g // 2 * 4 + j
                    c = (2 * pair + g % 2) % OH * HV
                    last = pe.matmul(O[g // 4][:, c:c + HV], PT[:, g % 2, j, :], V[:, q, pair // 2, :],
                                     start=True, stop=True)
                last.then_inc(pv_done, 1)

            def transposes(kind, b, src, dt, idn, wait, value):
                pe.wait_ge(wait, value)
                free(kind, b)
                bk = tbank(kind)[:].bitcast(dt)
                for c, s in enumerate(src):
                    last = pe.transpose(bk[:, c * P:(c + 1) * P], s, idn[:])
                last.then_inc(ready[kind], 1)

            def gate_up(b, n):
                lo, size = CHUNKS[n]
                if n == 0:
                    pe.wait_ge(evac["xqT"], b - 1)
                need(pe, ga_done, 3 * (b - 2) + n)
                need(pe, h_done, 3 * (b - 2) + n)
                if n == 0:
                    need(pe, out_done, b - 2 if stage(b, 3) else 0)
                for bk, first in ((GB, lo), (UB, INTER + lo)):
                    for c in range(HC):
                        last = pe.matmul(bk[:, 0:size], xqT[:, c, :], gateT[:, c, first:first + size],
                                         start=(c == 0), stop=(c == HC - 1))
                last.then_inc(gu_done, 1)

            def down(b):
                pe.wait_ge(evac["hTb"], b - 2)
                need(pe, h_done, 3 * (b - 2))
                for c in range(IC):
                    last = pe.matmul(UB[:], hT[:, c, :], downT[:, c, :], start=(c == 0), stop=(c == IC - 1))
                last.then_inc(down_done, 1)

            def body(b, p, j):
                f, a, u, d = (stage(b, k) for k in range(4))

                def cols(t, lo, hi):
                    return [t[:, c * P:(c + 1) * P] for c in range(lo, hi)]

                def group(g):
                    if a:
                        pv(b, p, g)
                        if g + 2 < KVH:
                            scores(b, p, g + 2)

                def probs(g):
                    if a:
                        probs_t(b, p, g)

                if a:
                    scores(b, p, 0)
                    scores(b, p, 1)
                probs(0)
                if d:
                    transposes("hTa", b, cols(hq, 0, 8), BF16, identb, hq_done, b - 2)
                group(0)
                probs(1)
                if d:
                    transposes("hTb", b, cols(hq, 8, IC), BF16, identb, hq_done, b - 2)
                group(1)
                probs(2)
                if u:
                    transposes("xqT", b, cols(xq, 0, HC), BF16, identb, xq_done, b - 1)
                if d:
                    down(b)
                group(2)
                probs(3)
                if u:
                    gate_up(b, 0)
                group(3)
                probs(4)
                qv = qs[:].rearrange("p h s d -> p (h s d)")
                if f:
                    transposes("q0", b, cols(qv, 0, 8), F16, identh, qs_done, b + 1)
                group(4)
                probs(5)
                if u:
                    gate_up(b, 1)
                group(5)
                probs(6)
                if f:
                    transposes("q1", b, cols(qv, 8, 16), F16, identh, qs_done, b + 1)
                group(6)
                probs(7)
                if u:
                    gate_up(b, 2)
                if f:
                    kv = ks[:].rearrange("p k r s d -> p (k r s d)")
                    transposes("kT", b, cols(kv, 0, 8), F16, identh, ks_done, b + 1)
                group(7)

            bodies(pe, NB, body, head=2, tail=3)

        @block.scalar
        def _(act):
            def take(kind, b, dst, src):
                act.wait_ge(ready[kind], b - delay[kind] + 1)
                act.copy(dst, src).then_inc(evac[kind], 1)

            def view(kind, dt, n):
                return tbank(kind)[:].bitcast(dt)[:, 0:n * P].rearrange("p (c n) -> p c n", n=P)

            def body(b, p, j):
                f, a, u, d = (stage(b, k) for k in range(4))

                def exps(g):
                    if not a:
                        return
                    n = 8 * b - 8 + g
                    act.wait_ge(s_sub, n + 1)
                    if g >= 2:
                        act.wait_ge(ready[f"T{g - 2}"], b)
                    else:
                        need(act, ready[f"T{g + 6}"], b - 1)
                    act.activation(PB[:, g % 2], D[:, g % 2], ACT.Exp, scale=SCALE).then_inc(s_exp, 1)

                def probs(g):
                    if a:
                        need(act, pv_done, 8 * b - 8 + g - 1)
                        take(f"T{g}", b, PT[:, g % 2], view(f"T{g}", F32, HG))

                def gates(n):
                    if u:
                        lo, size = CHUNKS[n]
                        act.wait_ge(gu_done, 3 * (b - 2) + n + 1)
                        need(act, ga_done, 3 * (b - 2) + n)
                        act.activation(th[:, 0:size], GB[:, 0:size], ACT.Tanh, scale=dqg[:, 1:2]).then_inc(th_done, 1)

                exps(0)
                probs(0)
                if d:
                    need(act, down_done, b - 3)
                    take("hTa", b, hT[:, 0:8, :], view("hTa", BF16, 8))
                exps(1)
                probs(1)
                if d:
                    take("hTb", b, hT[:, 8:IC, :], view("hTb", BF16, IC - 8))
                exps(2)
                probs(2)
                if u:
                    need(act, gu_done, 3 * (b - 2))
                    take("xqT", b, xqT[:], view("xqT", BF16, HC))
                exps(3)
                probs(3)
                exps(4)
                gates(0)
                probs(4)
                if f:
                    take("q0", b, qT[:, p, 0:8, :], view("q0", F16, 8))
                exps(5)
                probs(5)
                exps(6)
                gates(1)
                probs(6)
                if f:
                    take("q1", b, qT[:, p, 8:16, :], view("q1", F16, 8))
                exps(7)
                probs(7)
                gates(2)
                if f:
                    take("kT", b, kT[:, p], view("kT", F16, 8))
                if u:
                    act.wait_ge(h_done, 3 * (b - 1))
                    need(act, hn_done, b - 2)
                    act.activation(junk[:], h[:], ACT.Square, accum_out=ss[:]).then_inc(ss_done, 1)

            bodies(act, NB, body, head=2, tail=3)

        @block.vector
        def _(dve):
            step = Steps(dve, dve_steps, per=14, alone=True)
            dve.wait_ge(ld_g, 32)

            def body(b, p, j):
                f, a, u, d = (stage(b, k) for k in range(4))
                step.body(b)

                def softmax_head(g):
                    if not a:
                        return
                    n = 8 * b - 8 + g
                    dve.wait_ge(s_done, n + 1)
                    bk = S[g % 2][:].rearrange("p (h k) -> p h k", h=HG)
                    dve.tensor_reduce(mx[:, g % 2, :], bk, AX.X, ALU.max).then_inc(s_max, 1)
                    dve.wait_ge(s_max, n + 1)
                    need(dve, s_exp, n - 1)
                    dve.tensor_tensor(D[:, g % 2], bk, mx[:, g % 2, :, None].broadcast_to([P, HG, P]),
                                      ALU.subtract).then_inc(s_sub, 1)

                def out_half(k):
                    if not a:
                        return
                    dve.wait_ge(pv_done, 8 * b - 8 + 4 * (k + 1))
                    bk = O[k][:, 0:OH * HV].rearrange("p (h d) -> p h d", h=OH)
                    step.then(dve.reciprocal(rden[:, k, :], bk[:, :, HD1]))
                    need(dve, x4_done, b - 1)
                    dve.tensor_tensor(On[:, k * 256:(k + 1) * 256].rearrange("p (h d) -> p h d", h=OH),
                                      bk[:, :, 0:HD1], rden[:, k, :, None].broadcast_to([P, OH, HD1]),
                                      ALU.mult).then_inc(o_done, 1)

                def gated(n):
                    if not u:
                        return
                    lo, size = CHUNKS[n]
                    k = 3 * (b - 2) + n
                    dve.wait_ge(th_done, k + 1)
                    need(dve, h_done, k)
                    if n == 0:
                        need(dve, ss_done, b - 2)
                        need(dve, hg_done, b - 2)
                    dve.scalar_tensor_tensor(ga[:, 0:size], th[:, 0:size], 1.0, GB[:, 0:size], ALU.add,
                                             ALU.mult).then_inc(ga_done, 1)
                    dve.wait_ge(ga_done, k + 1)
                    dve.tensor_tensor(h[:, lo:lo + size], UB[:, 0:size], ga[:, 0:size], ALU.mult).then_inc(h_done, 1)

                if u:
                    xb = at(X, b - 2)
                    need(dve, x4_done, b - 1, True)
                    step.then(dve.bn_stats(st[:, 0, :], xb))
                    dve.bn_aggr(mv4[:], st[:, 0, :]).then_inc(stats4, 1)
                    dve.wait_ge(stats4, b - 1)
                    need(dve, xq_done, b - 2)
                    step.then(dve.scalar_tensor_tensor(t1[:], xb, mv4[:, 0:1], g1[:], ALU.subtract, ALU.mult))
                    step.then(dve.tensor_reduce(am[:, 0:1], t1[:], AX.X, ALU.max, apply_absolute_value=True))
                softmax_head(0)
                if u:
                    dve.wait_ge(nrm_done, b - 1)
                    a0, a1, a2 = (am[:, k:k + 1] for k in range(3))
                    step.then(dve.tensor_scalar(a1, a0, nrm[:, 3:4], 1e-5, ALU.mult, ALU.max))
                    step.then(dve.reciprocal(a2, a1))
                    need(dve, hn_done, b - 2)
                    step.then(dve.tensor_scalar(dqg[:, 0:1], a1, 1.0 / 127.0, m["wmean"][:, 0:1], ALU.mult, ALU.mult))
                    step.then(dve.tensor_scalar(dqg[:, 1:2], dqg[:, 0:1], 0.5, None, ALU.mult))
                    dve.tensor_scalar(mq[:], a2, 127.0, nrm[:, 3:4], ALU.mult, ALU.mult).then_inc(mq_done, 1)
                softmax_head(1)
                if f:
                    xf = at(X, b)
                    dve.wait_ge(gathered[p], 32 * (j + 1))
                    dve.scalar_tensor_tensor(xf, yg[:, p, 0, :], m["wt"][:, 0, bass.ds(b, 1)], xf, ALU.mult,
                                             ALU.add).then_inc(x3_a, 1)
                    dve.wait_ge(x3_a, b + 1)
                    dve.scalar_tensor_tensor(xf, yg[:, p, 1, :], m["wt"][:, 1, bass.ds(b, 1)], xf, ALU.mult,
                                             ALU.add).then_inc(x3_done, 1)
                    need(dve, x3_done, b + 1, True)
                    step.then(dve.bn_stats(st[:, 1, :], xf))
                    need(dve, xn_done, b, True)
                    dve.bn_aggr(mv3[:], st[:, 1, :]).then_inc(stats3, 1)
                softmax_head(2)
                if u:
                    dve.wait_ge(xr_done, b - 1)
                    need(dve, ready["xqT"], b - 2)
                    dve.tensor_scalar(xq[:], t1[:], -ROUND, None, ALU.add).then_inc(xq_done, 1)
                softmax_head(3)
                if d:
                    dve.wait_ge(down_done, b - 2)
                    need(dve, stored[1 - p], 16 * (j - 2 + p))
                    dve.scalar_tensor_tensor(xo[:, 1 - p, :], UB[:], dqd[:], at(X, b - 3), ALU.mult,
                                             ALU.add).then_inc(out_done, 1)
                softmax_head(4)
                out_half(0)
                gated(0)
                softmax_head(5)
                softmax_head(6)
                gated(1)
                softmax_head(7)
                gated(2)
                if u:
                    b0, b1, b2, b3 = (ah[:, k:k + 1] for k in range(4))
                    dve.wait_ge(hg_done, b - 1)
                    step.then(dve.tensor_reduce(b0, hg[:], AX.X, ALU.max, apply_absolute_value=True))
                    dve.wait_ge(hn_done, b - 1)
                    step.then(dve.tensor_scalar(b1, b0, hn[:, 3:4], 1e-5, ALU.mult, ALU.max))
                    step.then(dve.reciprocal(b3, b1))
                    if d:
                        dve.wait_ge(out_done, b - 2)
                    step.then(dve.tensor_scalar(dqd[:], b1, 1.0 / 127.0, m["wmean"][:, 1:2], ALU.mult, ALU.mult))
                    dve.tensor_scalar(b2, b3, 127.0, hn[:, 3:4], ALU.mult, ALU.mult).then_inc(mh_done, 1)
                    dve.wait_ge(hr_done, b - 1)
                    if d:
                        dve.wait_ge(ready["hTb"], b - 2)
                    dve.tensor_scalar(hq[:], hg[:], -ROUND, None, ALU.add).then_inc(hq_done, 1)
                out_half(1)
                step.end()

            bodies(dve, NB, body, head=2, tail=3)


_INS = ['x', 'ctx_512', 'L0_xattn_Wq', 'L0_xattn_Wkv_expand', 'L0_xattn_Wout', 'L0_ffn_Wg', 'L0_ffn_W1', 'L0_ffn_W2',
        'L0_ffn_W3', 'L0_ffn_bias', 'L1_ffn_gate_w', 'L1_ffn_down_w', 'L1_ffn_gate_norm_w', 'L1_ffn_down_norm_w']


def kernel(**inputs):
    import numpy as np
    import concourse.bacc as bacc
    from concourse import mybir as _mybir
    from concourse.bass_utils import run_bass_kernel_spmd

    nc = bacc.Bacc("TRN2", target_bir_lowering=False, num_devices=1)
    arrays, args = {}, {}
    for name in _INS:
        a = np.ascontiguousarray(inputs[name])
        arrays[f"in_{name}"] = a
        args[name] = nc.dram_tensor(f"in_{name}", a.shape, _mybir.dt.from_np(a.dtype), kind="ExternalInput").ap()
    out = nc.dram_tensor("out", (B, P, H), _mybir.dt.float32, kind="ExternalOutput").ap()
    decoder_kernel(nc, args["x"], args["ctx_512"], args["L0_xattn_Wq"], args["L0_xattn_Wkv_expand"],
                   args["L0_xattn_Wout"], args["L0_ffn_Wg"], args["L0_ffn_W1"], args["L0_ffn_W2"],
                   args["L0_ffn_W3"], args["L0_ffn_bias"], args["L1_ffn_gate_w"], args["L1_ffn_down_w"],
                   args["L1_ffn_gate_norm_w"], args["L1_ffn_down_norm_w"], out)
    r = run_bass_kernel_spmd(nc, [arrays], core_ids=[0])
    return r.results[0]["out"]
```

```python
from contextlib import ExitStack

import concourse.bass as bass
from concourse import mybir

P = 128
ALU = mybir.AluOpType
ACT = mybir.ActivationFunctionType
AX = mybir.AxisListType
F32 = mybir.dt.float32
F16 = mybir.dt.float16
BF16 = mybir.dt.bfloat16
I32 = mybir.dt.int32
U32 = mybir.dt.uint32

B = 16
H = 512
HC = H // P
L = 128
EPS = 1e-5
NH0, HD0 = 16, 32
E, FF = 8, 256
FC = FF // P
QH, KVH, HD1 = 32, 8, 16
GROUP = QH // KVH
INTER = 1408
IC = INTER // P
GATE_TILES = 2 * INTER // P
SLOT_TILES = (2 * B * P + E * (P - 1)) // P + 1
SLOT_TILES += SLOT_TILES % 2
SLOTS = SLOT_TILES * P
NEG = -3.0e38
BIG = 3.0e38
ROUND = 12582912.0
GATE_ABS = GATE_TILES * H // B
DOWN_ABS = HC * INTER // B
CHUNKS = [(0, 512), (512, 512), (1024, 384)]
HG = 4


def need(eng, sem, value, alone=False):
    if isinstance(value, int) and value <= 0:
        return
    eng.wait_ge(sem, value)
    if alone and not isinstance(value, int):
        eng.nop(nofuse=True)


def at(t, i, *rest):
    if isinstance(i, int):
        return t[(slice(None), i) + rest]
    ap = t[(slice(None), bass.ds(i, 1)) + rest]
    n = len(ap.shape)
    names = " ".join("abcdef"[k] for k in range(n - 2))
    return ap.rearrange(f"p o {names} -> p (o a) {names[2:]}" if n > 2 else "p o -> p o")


def bodies(eng, count, body, head=1, tail=1):
    for b in range(2 * head):
        body(b, b % 2, b // 2)
    with eng.Fori(head, count // 2 - tail) as j:
        for p in range(2):
            body(j * 2 + p, p, j)
    for b in range(count - 2 * tail, count):
        body(b, b % 2, b // 2)


class Steps:

    def __init__(self, eng, sem, per=0, alone=False):
        self.eng, self.sem, self.per, self.alone, self.first, self.base, self.n = eng, sem, per, alone, 0, 0, 0

    def loop(self, per):
        self.first, self.per, self.alone = self.n, per, True

    def body(self, b):
        self.base, self.n = b * self.per + self.first, 0

    def mark(self, ins):
        ins.then_inc(self.sem, 1)
        self.n += 1
        return self.base + self.n

    def then(self, ins):
        need(self.eng, self.sem, self.mark(ins), self.alone)

    def end(self):
        rest = self.per - self.n
        assert rest >= 0, (self.n, self.per)
        if rest:
            self.eng.drain().then_inc(self.sem, rest)
        self.n = self.per
        self.eng.wait_ge(self.sem, self.base + self.n)


def decoder_kernel(nc, x, ctx, Wq, Wkv, Wout, Wg, W1, W2, W3, bias, gate_w, down_w, gnorm, dnorm, out):
    slots_in = nc.dram_tensor("slots_in", [SLOTS, H], F32, kind="Internal").ap()
    slots_out = nc.dram_tensor("slots_out", [SLOTS, H], F32, kind="Internal").ap()
    with ExitStack() as stack:
        def sb(name, shape, dt=F32):
            return stack.enter_context(nc.sbuf_tensor(name, shape, dt))

        def sem(name):
            return stack.enter_context(nc.semaphore(name))

        m = {}
        m["X"] = sb("X", [P, B, H])
        m["CTX"] = sb("CTX", [P, B, L])
        m["ident"] = sb("ident", [P, P])
        m["identh"] = sb("identh", [P, P], F16)
        m["identb"] = sb("identb", [P, P], BF16)
        m["absum"] = sb("absum", [P, 2, B])
        m["ones"] = sb("ones", [P, P])
        m["half"] = sb("half", [P, 1])
        m["pos"] = sb("pos", [P, 2, B], U32)
        m["wt"] = sb("wt", [P, 2, B])
        m["wmean"] = sb("wmean", [P, 2])
        m["wscale"] = sb("wscale", [P, 2])
        m["R"] = sb("R", [P, HC * 2 * INTER + IC * H], BF16)
        with ExitStack() as moe:
            m["first"] = []
            m["sem"] = lambda name: m["first"].append(moe.enter_context(nc.semaphore(name))) or m["first"][-1]
            m["W13T"] = moe.enter_context(nc.sbuf_tensor("W13T", [P, E, HC, 2 * FF], F32))
            m["W2T"] = moe.enter_context(nc.sbuf_tensor("W2T", [P, E, FC, H], F32))
            m["logits"] = moe.enter_context(nc.sbuf_tensor("logits", [P, B, E], F32))
            m["stats2"] = moe.enter_context(nc.sbuf_tensor("stats2", [P, B, 2], F32))
            m["rstd2"] = moe.enter_context(nc.sbuf_tensor("rstd2", [P, B], F32))
            layer0_attention(nc, m, x, ctx, Wq, Wkv, Wout, Wg, W1, W2, W3, gate_w, down_w, slots_in)
            m["sem"] = sem
            experts(nc, m, bias, gate_w, down_w, slots_in, slots_out)
        layer1(nc, m, slots_out, gnorm, dnorm, out)


def layer0_attention(nc, m, x, ctx, Wq, Wkv, Wout, Wg, W1, W2, W3, gate_w, down_w, slots_in):
    X, CTX, ident, identh, identb = m["X"], m["CTX"], m["ident"], m["identh"], m["identb"]
    W13T, W2T, logits, ones, half = m["W13T"], m["W2T"], m["logits"], m["ones"], m["half"]
    SCALE = float(HD0) ** -0.5
    NB = B + 2
    with ExitStack() as stack:
        def sb(name, shape, dt=F32):
            return stack.enter_context(nc.sbuf_tensor("a_" + name, shape, dt))

        def sem(name):
            return m["sem"]("a_" + name)

        def bank(name):
            return stack.enter_context(nc.psum_tensor("a_" + name, [P, 512], F32))

        reg = m["R"][:, 0:2 * (2 * HC * H + 2 * H)].bitcast(F32)
        WqT = reg[:, 0:HC * H].rearrange("p (c f) -> p c f", c=HC)
        WoutT = reg[:, HC * H:2 * HC * H].rearrange("p (c f) -> p c f", c=HC)
        WkvT = reg[:, 2 * HC * H:2 * HC * H + 2 * H]
        WgT = sb("WgT", [P, HC, E])
        mask4 = sb("mask4", [P, HG, P], BF16)
        wn = sb("wn", [P, 3, H])
        pre = W13T[:, 0:2, :, :].rearrange("p e c n -> p (e c) n")
        prekv = W13T[:, 2, 0:2, :].rearrange("p c (t n) -> p (c t) n", n=P)
        preg = W13T[0:E, 3, 0, :]
        zero = W2T[:, E - 1, FC - 1, :]
        absn = sb("absn", [P, GATE_ABS + DOWN_ABS])
        xn = sb("xn", [P, H])
        cx = sb("cx", [P, L])
        xn2 = sb("xn2", [P, H])
        xT = sb("xT", [P, HC, P])
        x2T = sb("x2T", [P, HC, P])
        ctxT = sb("ctxT", [P, P])
        qT = sb("qT", [P, 2, HC, P])
        kT = sb("kT", [P, 2, HC, P])
        V = sb("V", [P, 2, NH0, HD0 + 1])
        mx = sb("mx", [P, 2, HG])
        spare = m["R"][:, 2 * (2 * HC * H + 2 * H):][:, 0:12 * H].bitcast(F32)
        D = spare[:, 0:2 * H].rearrange("p (g h k) -> p g h k", g=2, h=HG)
        PT = spare[:, 2 * H:4 * H].rearrange("p (g h k) -> p g h k", g=2, h=HG)
        On = spare[:, 4 * H:5 * H]
        OT = spare[:, 5 * H:6 * H].rearrange("p (c n) -> p c n", c=HC)
        rden = sb("rden", [P, 2, 8])
        st = sb("st", [P, 2, 6])
        mv1 = sb("mv1", [P, 2])
        rs1 = sb("rs1", [P, 1])
        mv2 = sb("mv2", [P, 2])
        rs2 = sb("rs2", [P, 1])

        S = [bank("S0"), bank("S1")]
        T = [bank("T0"), bank("T1")]
        Fb = bank("F")
        Dk = bank("Dk")
        O = [bank("O0"), bank("O1")]

        ld_x, ld_ctx, ld_w = [sem("ld_x0"), sem("ld_x1")], sem("ld_ctx"), sem("ld_w")
        ld_stage, ld_abs = sem("ld_stage"), sem("ld_abs")
        zeroed, filled = sem("zeroed"), sem("filled")
        consts, consts_dve = sem("consts"), sem("consts_dve")
        pre_t, pre_e = sem("pre_t"), sem("pre_e")
        front = ["xT", "cT", "K", "Q", "V"]
        att = ["T0", "T1", "T2", "T3", "W0", "W1", "W2"]
        tail = ["OT", "x2T"]
        ready = {k: sem("ready_" + k) for k in front + att + tail}
        evac = {k: sem("evac_" + k) for k in front + att + tail}
        s_done, s_max, s_sub, s_exp = sem("s_done"), sem("s_max"), sem("s_sub"), sem("s_exp")
        pv_done, o_done = sem("pv_done"), sem("o_done")
        rstd1_done, rstd2_done = sem("rstd1_done"), sem("rstd2_done")
        stats1, stats2, xn_done, xn2_done = sem("stats1"), sem("stats2"), sem("xn_done"), sem("xn2_done")
        y_done, x2_done, r_done, l_done = sem("y_done"), sem("x2_done"), sem("r_done"), sem("l_done")
        abs_done, cx_done = sem("abs_done"), sem("cx_done")
        dve_steps, pool_steps = sem("dve_steps"), sem("pool_steps")

        def count(kind, b):
            return b + 1 if kind in front else b if kind in att else b - 1

        def has(kind, b):
            if not isinstance(b, int):
                return True
            return 0 <= count(kind, b) - 1 < B

        ring = {"T": ["T0", "xT", "T1", "OT", "T2", "T3", "x2T"], "F": ["cT", "K", "Q", "W0", "V", "W1", "W2"]}
        where = {k: (r, i) for r, ks in ring.items() for i, k in enumerate(ks)}

        def before(kind, b):
            r, i = where[kind]
            ks, back = ring[r], 2 if r == "T" else 1
            while True:
                i -= back
                if i < 0:
                    i, b = i + len(ks), b - 1
                if has(ks[i], b) or (isinstance(b, int) and b < 0):
                    return ks[i], b

        def tbank(kind, p):
            return T[(p * len(ring["T"]) + where[kind][1]) % 2]

        pre_jobs = [("q", r) for r in range(HC)] + [("kv", r) for r in range(2)] + [("o", r) for r in range(HC)] \
            + [("g", 0)]

        block = stack.enter_context(nc.Block())

        @block.sync
        def _(sp):
            sp.dma_start(X[:, 0:2, :], x[0:2].rearrange("b p d -> p b d")).then_inc(ld_x[0], 16)
            sp.dma_start(CTX[:], ctx.rearrange("b p d -> p b d")).then_inc(ld_ctx, 16)
            sp.dma_start(pre[:, 0:HC, :], Wq.rearrange("(t p) n -> p t n", p=P)).then_inc(ld_w, 16)
            sp.dma_start(prekv, Wkv.rearrange("(t p) n -> p t n", p=P)).then_inc(ld_w, 16)
            sp.dma_start(pre[:, HC:2 * HC, :], Wout.rearrange("(t p) n -> p t n", p=P)).then_inc(ld_w, 16)
            sp.dma_start(preg, Wg).then_inc(ld_w, 16)
            sp.dma_start(X[:, 2:B, :], x[2:B].rearrange("b p d -> p b d")).then_inc(ld_x[1], 16)

            def body(b, p, j):
                e, e_half = j - 1 + p, 1 - p
                if has("W0", b):
                    need(sp, ready["W2"], b - 1)
                    rows = slice(e_half * P, (e_half + 1) * P)
                    if isinstance(e, int):
                        w1, w3, w2 = W1[e], W3[e], W2[e]
                    else:
                        w1, w3, w2 = (w[bass.ds(e, 1)].rearrange("o a b -> (o a) b") for w in (W1, W3, W2))
                    sp.dma_start(wn[:, 0, :], w1[rows, :]).then_inc(ld_stage, 16)
                    sp.dma_start(wn[:, 1, :], w3[rows, :]).then_inc(ld_stage, 16)
                    sp.dma_start(wn[:, 2, :].rearrange("p (t n) -> p t n", n=P),
                                 w2[:, rows].rearrange("(t p) n -> p t n", p=P)).then_inc(ld_stage, 16)
                if has("xT", b):
                    need(sp, abs_done, b)
                    gf = gate_w.rearrange("(p a) b -> p (a b)", p=P)
                    df = down_w.rearrange("(p a) b -> p (a b)", p=P)
                    sp.dma_start(absn[:, 0:GATE_ABS], gf[:, bass.ds(b * GATE_ABS, GATE_ABS)]).then_inc(ld_abs, 16)
                    sp.dma_start(absn[:, GATE_ABS:], df[:, bass.ds(b * DOWN_ABS, DOWN_ABS)]).then_inc(ld_abs, 16)
                if isinstance(b, int) and b == 1:
                    sp.wait_ge(zeroed, 1)
                    for t in range(4):
                        n = SLOTS // 4
                        sp.dma_start(slots_in[t * n:(t + 1) * n, :].rearrange("(k p) d -> p k d", p=P),
                                     zero[:, None, :].broadcast_to([P, n // P, H])).then_inc(filled, 16)

            bodies(sp, NB, body, tail=2)
            sp.wait_ge(filled, 64)

        @block.gpsimd
        def _(pool):
            step = Steps(pool, pool_steps)
            step.then(pool.memset(ident[:], 0.0))
            pool.affine_select(out=ident[:], in_=ident[:], compare_op=ALU.not_equal, fill=1.0, base=0,
                               pattern=[[-1, P]], channel_multiplier=1).then_inc(consts, 1)
            step.then(pool.memset(mask4[:], 0.0))
            pool.affine_select(out=mask4[:], in_=mask4[:], compare_op=ALU.is_ge, fill=NEG, base=0,
                               pattern=[[0, HG], [-1, P]], channel_multiplier=1).then_inc(consts, 1)
            pool.memset(half[:], -0.5).then_inc(consts, 1)
            pool.memset(V[:, :, :, HD0:HD0 + 1], 1.0).then_inc(consts, 1)
            pool.memset(ones[:], 1.0).then_inc(consts, 1)
            pool.memset(zero, 0.0).then_inc(zeroed, 1)
            pool.wait_ge(consts, 5)
            pool.tensor_copy(identh[:], ident[:]).then_inc(consts, 1)
            pool.tensor_copy(identb[:], ident[:]).then_inc(consts, 1)
            pool.wait_ge(consts, 7)

            def front(b):
                need(pool, ready["cT"], b, True)
                pool.tensor_copy(cx[:], at(CTX, b)).then_inc(cx_done, 1)
                need(pool, stats1, b + 1, True)
                need(pool, xn_done, b, True)
                step.then(pool.tensor_scalar(rs1[:], mv1[:, 1:2], EPS, None, ALU.add))
                pool.tensor_tensor(rs1[:], rs1[:], half[:], ALU.pow).then_inc(rstd1_done, 1)

            pool.wait_ge(ld_ctx, 16)
            front(0)
            step.loop(2)

            def body(b, p, j):
                step.body(b)
                if has("xT", b + 1):
                    front(b + 1)
                if has("OT", b):
                    need(pool, stats2, b - 1, True)
                    need(pool, xn2_done, b - 2, True)
                    step.then(pool.tensor_scalar(rs2[:], mv2[:, 1:2], EPS, None, ALU.add))
                    pool.tensor_tensor(rs2[:], rs2[:], half[:], ALU.pow).then_inc(rstd2_done, 1)
                step.end()

            bodies(pool, NB, body, tail=2)

        @block.tensor
        def _(pe):
            pe.wait_ge(consts, 7)
            pe.wait_ge(ld_w, 64)
            for n, (kind, r) in enumerate(pre_jobs):
                if n >= 2:
                    pe.wait_ge(pre_e, n - 1)
                bk = T[n % 2]
                if kind == "g":
                    for c in range(HC):
                        last = pe.transpose(bk[:, c * E:(c + 1) * E], preg[:, c * P:(c + 1) * P], ident[0:E, 0:E])
                else:
                    for c in range(4):
                        src = (pre[:, r, c * P:(c + 1) * P] if kind == "q" else prekv[:, 4 * r + c, :] if kind == "kv"
                               else pre[:, HC + r, c * P:(c + 1) * P])
                        last = pe.transpose(bk[:, c * P:(c + 1) * P], src, ident[:])
                last.then_inc(pre_t, 1)
            pe.wait_ge(pre_e, len(pre_jobs))

            def free(kind, b):
                k, bb = before(kind, b)
                need(pe, evac[k], count(k, bb))

            def scores(b, p, g):
                q = 1 - p
                n = 4 * b - 4 + g
                need(pe, s_sub, n - 1)
                if g == 0:
                    pe.wait_ge(evac["Q"], b)
                    pe.wait_ge(evac["K"], b)
                bk, rows = S[g % 2], slice(HD0 * g, HD0 * (g + 1))
                pe.matmul(bk[:], identb[:], mask4[:].rearrange("p a b -> p (a b)"), start=True, stop=False)
                for c in range(HG):
                    last = pe.matmul(bk[:, c * P:(c + 1) * P], qT[rows, q, c, :], kT[rows, q, c, :],
                                     start=False, stop=(c == HG - 1), tile_position=(HD0 * g, 0))
                last.then_inc(s_done, 1)

            def probs_t(b, p, g):
                pe.wait_ge(s_exp, 4 * b - 3 + g)
                free(f"T{g}", b)
                bk = tbank(f"T{g}", p)
                for j in range(HG):
                    last = pe.transpose(bk[:, j * P:(j + 1) * P], D[:, g % 2, j, :], ident[:])
                last.then_inc(ready[f"T{g}"], 1)

            def pv(b, p, g):
                q = 1 - p
                pe.wait_ge(evac[f"T{g}"], b)
                if g == 0:
                    pe.wait_ge(evac["V"], b)
                if g % 2 == 0:
                    need(pe, o_done, 2 * b - 3 + g // 2)
                for j in range(HG):
                    c = (4 * (g % 2) + j) * (HD0 + 1)
                    last = pe.matmul(O[g // 2][:, c:c + HD0 + 1], PT[:, g % 2, j, :], V[:, q, 4 * j + g, :],
                                     start=True, stop=True)
                last.then_inc(pv_done, 1)

            def four(kind, b, p, src, wait, value):
                need(pe, wait, value)
                free(kind, b)
                bk = tbank(kind, p)
                for c in range(HC):
                    last = pe.transpose(bk[:, c * P:(c + 1) * P], src[:, c * P:(c + 1) * P], ident[:])
                last.then_inc(ready[kind], 1)

            def weights(b, p, j, k):
                if k == 0:
                    pe.wait_ge(ld_stage, 48 * b)
                free(f"W{k}", b)
                for c in range(4):
                    last = pe.transpose(Fb[:, c * P:(c + 1) * P], wn[:, k, c * P:(c + 1) * P], ident[:])
                last.then_inc(ready[f"W{k}"], 1)

            def body(b, p, j):
                a, f, t = has("T0", b), has("xT", b), has("OT", b)
                if a:
                    scores(b, p, 2)
                    probs_t(b, p, 0)
                if f:
                    four("xT", b, p, xn, xn_done, b + 1)
                    pe.wait_ge(cx_done, b + 1)
                    free("cT", b)
                    pe.transpose(Fb[:, 0:P], cx[:], ident[:]).then_inc(ready["cT"], 1)
                if a:
                    scores(b, p, 3)
                    pv(b, p, 0)
                    probs_t(b, p, 1)
                if f:
                    pe.wait_ge(evac["cT"], b + 1)
                    for g in range(HC):
                        last = pe.matmul(Fb[:, g * P:(g + 1) * P], WkvT[:, g * P:(g + 1) * P], ctxT[:],
                                         start=True, stop=True)
                    last.then_inc(ready["K"], 1)
                if t:
                    four("OT", b, p, On, o_done, 2 * b - 2)
                if a:
                    pv(b, p, 1)
                    probs_t(b, p, 2)
                if f:
                    pe.wait_ge(evac["xT"], b + 1)
                    free("Q", b)
                    for g in range(HC):
                        for c in range(HC):
                            last = pe.matmul(Fb[:, g * P:(g + 1) * P], WqT[:, c, g * P:(g + 1) * P], xT[:, c, :],
                                             start=(c == 0), stop=(c == HC - 1))
                    last.then_inc(ready["Q"], 1)
                if t:
                    pe.wait_ge(evac["OT"], b - 1)
                    need(pe, l_done, b - 2)
                    for c in range(HC):
                        last = pe.matmul(Dk[:], OT[:, c, :], WoutT[:, c, :], start=(c == 0), stop=(c == HC - 1))
                    last.then_inc(y_done, 1)
                if a:
                    pv(b, p, 2)
                    probs_t(b, p, 3)
                    weights(b, p, j, 0)
                if f:
                    scores(b + 1, 1 - p, 0)
                    scores(b + 1, 1 - p, 1)
                    free("V", b)
                    pe.matmul(Fb[:], ctxT[:], WkvT[:, H:2 * H], start=True, stop=True).then_inc(ready["V"], 1)
                if t:
                    four("x2T", b, p, xn2, xn2_done, b - 1)
                if a:
                    pv(b, p, 3)
                    weights(b, p, j, 1)
                if t:
                    pe.wait_ge(evac["x2T"], b - 1)
                    pe.wait_ge(x2_done, b - 1)
                    for c in range(HC):
                        last = pe.matmul(Dk[:, 0:E], x2T[:, c, :], WgT[:, c, :], start=(c == 0), stop=(c == HC - 1))
                    last.then_inc(r_done, 1)
                if a:
                    weights(b, p, j, 2)

            bodies(pe, NB, body, tail=2)

        @block.scalar
        def _(act):
            for n, (kind, r) in enumerate(pre_jobs):
                act.wait_ge(pre_t, n + 1)
                bk = T[n % 2]
                if kind == "g":
                    dst, src = WgT[:], bk[:, 0:HC * E].rearrange("p (c e) -> p c e", c=HC)
                elif kind == "kv":
                    dst, src = WkvT[:, 4 * P * r:4 * P * (r + 1)], bk[:]
                else:
                    dst = (WqT if kind == "q" else WoutT)[:, :, r * P:(r + 1) * P]
                    src = bk[:].rearrange("p (c f) -> p c f", c=HC)
                act.copy(dst, src).then_inc(pre_e, 1)

            def take(kind, b, dst, src):
                act.wait_ge(ready[kind], count(kind, b))
                act.copy(dst, src).then_inc(evac[kind], 1)

            def chunked(bk):
                return bk[:].rearrange("p (c n) -> p c n", c=4)

            def exps(b, g):
                n = 4 * b - 4 + g
                act.wait_ge(s_sub, n + 1)
                act.activation(D[:, g % 2], D[:, g % 2], ACT.Exp, scale=SCALE).then_inc(s_exp, 1)

            def take_probs(b, p, g):
                n = 4 * b - 4 + g
                need(act, pv_done, n - 1)
                take(f"T{g}", b, PT[:, g % 2], chunked(tbank(f"T{g}", p)))

            def weights(b, p, j, k):
                e, half_e = j - 1 + p, 1 - p
                if k == 2 and isinstance(b, int) and b == B:
                    act.wait_ge(filled, 64)
                if k < 2:
                    lo = k * FF + half_e * P
                    take(f"W{k}", b, at(W13T, e, slice(None), slice(lo, lo + P)), chunked(Fb))
                else:
                    take("W2", b, at(W2T, e, half_e), Fb[:])

            def body(b, p, j):
                a, f, t = has("T0", b), has("xT", b), has("OT", b)
                q = 1 - p
                if a:
                    take_probs(b, p, 0)
                if f:
                    need(act, ready["Q"], b)
                    take("xT", b, xT[:], chunked(tbank("xT", p)))
                    need(act, ready["V"], b)
                    take("cT", b, ctxT[:], Fb[:, 0:P])
                if a:
                    exps(b, 2)
                    take_probs(b, p, 1)
                if f:
                    take("K", b, kT[:, p], chunked(Fb))
                if a:
                    exps(b, 3)
                if t:
                    need(act, y_done, b - 2)
                    take("OT", b, OT, chunked(tbank("OT", p)))
                if a:
                    take_probs(b, p, 2)
                if f:
                    take("Q", b, qT[:, p], chunked(Fb))
                if a:
                    take_probs(b, p, 3)
                    weights(b, p, j, 0)
                if f:
                    exps(b + 1, 0)
                    need(act, pv_done, 4 * b - 4)
                    take("V", b, V[:, p, :, 0:HD0], Fb[:].rearrange("p (h d) -> p h d", h=NH0))
                if t:
                    need(act, r_done, b - 2)
                    take("x2T", b, x2T[:], chunked(tbank("x2T", p)))
                if f:
                    exps(b + 1, 1)
                if a:
                    weights(b, p, j, 1)
                    weights(b, p, j, 2)

            bodies(act, NB, body, tail=2)

        @block.vector
        def _(dve):
            step = Steps(dve, dve_steps, alone=True)

            def ln_stats(src, dst, k, signal):
                step.then(dve.bn_stats(st[:, k, :], src))
                dve.bn_aggr(dst, st[:, k, :]).then_inc(signal, 1)

            def normalise(dst, src, mv, rs, signal):
                dve.tensor_scalar(dst[:], src, mv[:, 0:1], rs[:], ALU.subtract, ALU.mult).then_inc(signal, 1)

            def softmax_head(b, g):
                n = 4 * b - 4 + g
                dve.wait_ge(s_done, n + 1)
                bk = S[g % 2][:].rearrange("p (h k) -> p h k", h=HG)
                dve.tensor_reduce(mx[:, g % 2, :], bk, AX.X, ALU.max).then_inc(s_max, 1)
                dve.wait_ge(s_max, n + 1)
                if g >= 2:
                    dve.wait_ge(ready[f"T{g - 2}"], b)
                else:
                    need(dve, ready[f"T{g + 2}"], b - 1)
                dve.tensor_tensor(D[:, g % 2], bk, mx[:, g % 2, :, None].broadcast_to([P, HG, P]),
                                  ALU.subtract).then_inc(s_sub, 1)

            def out_half(b, p, k):
                q = 1 - p
                dve.wait_ge(pv_done, 4 * b - 4 + 2 * k + 2)
                bk = O[k][:, 0:8 * (HD0 + 1)].rearrange("p (h d) -> p h d", h=8)
                step.then(dve.reciprocal(rden[:, k, :], bk[:, :, HD0]))
                need(dve, ready["OT"], b - 1)
                four = "p (g c) d -> p g c d"
                rd = rden[:, k, :, None].broadcast_to([P, 8, HD0])
                dve.tensor_tensor(On.rearrange("p (c g d) -> p g c d", g=HG, d=HD0)[:, 2 * k:2 * k + 2],
                                  bk[:, :, 0:HD0].rearrange(four, g=2), rd.rearrange(four, g=2),
                                  ALU.mult).then_inc(o_done, 1)

            def front(b):
                if isinstance(b, int) and b < 2:
                    dve.wait_ge(ld_x[b], 16)
                ln_stats(at(X, b), mv1[:], 0, stats1)

            def front_norm(b):
                need(dve, rstd1_done, b + 1)
                need(dve, ready["xT"], b)
                normalise(xn, at(X, b), mv1, rs1, xn_done)

            front(0)
            front_norm(0)
            step.loop(7)

            def body(b, p, j):
                a, f, t = has("T0", b), has("xT", b), has("OT", b)
                step.body(b)
                if a:
                    softmax_head(b, 2)
                if has("xT", b + 1):
                    need(dve, xn_done, b + 1)
                    front(b + 1)
                if a:
                    softmax_head(b, 3)
                if has("xT", b + 1):
                    front_norm(b + 1)
                if f:
                    dve.wait_ge(ld_abs, 32 * (b + 1))
                    bb = bass.ds(b, 1)
                    step.mark(dve.tensor_reduce(m["absum"][:, 0, bb], absn[:, 0:GATE_ABS], AX.X, ALU.add,
                                                apply_absolute_value=True))
                    dve.tensor_reduce(m["absum"][:, 1, bb], absn[:, GATE_ABS:], AX.X, ALU.add,
                                      apply_absolute_value=True).then_inc(abs_done, 1)
                if a:
                    out_half(b, p, 0)
                if t:
                    dve.wait_ge(y_done, b - 1)
                    xb = at(X, b - 2)
                    dve.tensor_tensor(xb, Dk[:], xb, ALU.add).then_inc(x2_done, 1)
                    need(dve, x2_done, b - 1, True)
                    ln_stats(xb, mv2[:], 1, stats2)
                if f:
                    softmax_head(b + 1, 0)
                if t:
                    need(dve, rstd2_done, b - 1)
                    need(dve, ready["x2T"], b - 2)
                    normalise(xn2, xb, mv2, rs2, xn2_done)
                    step.mark(dve.tensor_copy(at(m["stats2"], b - 2), mv2[:]))
                    step.mark(dve.tensor_copy(m["rstd2"][:, bass.ds(b - 2, 1)], rs2[:]))
                if f:
                    softmax_head(b + 1, 1)
                if a:
                    out_half(b, p, 1)
                if t:
                    dve.wait_ge(r_done, b - 1)
                    dve.tensor_copy(at(logits, b - 2), Dk[:, 0:E]).then_inc(l_done, 1)
                step.end()

            bodies(dve, NB, body, tail=2)


def experts(nc, m, bias, gate_w, down_w, slots_in, slots_out):
    X, W13T, W2T, logits, ones = m["X"], m["W13T"], m["W2T"], m["logits"], m["ones"]
    ident, identb = m["ident"], m["identb"]
    gateT = m["R"][:, 0:HC * 2 * INTER].rearrange("p (c n) -> p c n", c=HC)
    downT = m["R"][:, HC * 2 * INTER:].rearrange("p (c n) -> p c n", c=IC)
    NB = SLOT_TILES + 2
    XS = 4
    with ExitStack() as stack:
        def sb(name, shape, dt=F32):
            return stack.enter_context(nc.sbuf_tensor("e_" + name, shape, dt))

        def sem(name):
            return m["sem"]("e_" + name)

        def bank(name, dt=F32):
            return stack.enter_context(nc.psum_tensor("e_" + name, [P, 2048 // mybir.dt.size(dt)], dt))

        brow = sb("brow", [1, E])
        prob = sb("prob", [P, B, E])
        score = sb("score", [P, B, E])
        tmp = sb("tmp", [P, B, E])
        pick = sb("pick", [P, 2, B, E])
        both = sb("both", [P, B, E], BF16)
        best = sb("best", [P, B])
        den = sb("den", [P, B])
        iota = sb("iota", [P, SLOT_TILES])
        order = sb("order", [P, E])
        tri = sb("tri", [P, P], BF16)
        onesb = sb("onesb", [P, P], BF16)
        tiles = sb("tiles", [P, E])
        upto = sb("upto", [P, E])
        base = sb("base", [P, E])
        cmp = sb("cmp", [1, SLOT_TILES, E])
        whichf = sb("whichf", [1, SLOT_TILES])
        which = sb("which", [1, SLOT_TILES], I32)
        asum = sb("asum", [P, 2])
        xs = sb("xs", [P, XS, H])
        slot = sb("slot", [P, XS, 2], U32)
        xg, y = xs[:, 0:2, :], xs[:, 2:4, :]
        xT = sb("xT", [P, 2, HC, P])
        sg = sb("sg", [P, FF])
        g = sb("g", [P, 2, FF])
        gT = sb("gT", [P, FC, P])
        wst = sb("wst", [P, 2, H])
        wr = sb("wr", [P, H])
        wq = sb("wq", [P, 2, H], BF16)

        XB = [bank("X0"), bank("X1")]
        GB = bank("G")
        HB = [bank("H0"), bank("H1")]
        YB = [bank("Y0"), bank("Y1")]
        WB = bank("W", BF16)

        ld_b, cst, s_exp, s_bias, s_cnt, s_both = (sem(k) for k in ("ld_b", "cst", "exp", "bias", "cnt", "both"))
        s_sum, s_mean, s_pos, s_table, steps = (sem(k) for k in ("sum", "mean", "pos", "table", "steps"))
        xs_ready = sem("xs_ready")
        sent = [sem(f"sent{k}") for k in range(XS)]
        ld_xg = [sem("ld_xg0"), sem("ld_xg1")]
        ld_wst = [sem("ld_wst0"), sem("ld_wst1")]
        x_t, x_e, h_done, silu_done, g_done, g_t, g_e, y_done, y_e = (
            sem(k) for k in ("x_t", "x_e", "h_done", "silu_done", "g_done", "g_t", "g_e", "y_done", "y_e"))
        stored = [sem("stored0"), sem("stored1")]
        wq_r, wq_m, wq_done, wq_t, wq_e = (sem(k) for k in ("wq_r", "wq_m", "wq_done", "wq_t", "wq_e"))

        def run(eng, body):
            jobs = GATE_TILES + IC
            assert GATE_TILES % 2 == 0 and jobs < SLOT_TILES
            for b in range(4):
                body(b, b % 2, b // 2, "gate")
            with eng.Fori(2, GATE_TILES // 2) as j:
                for p in range(2):
                    body(j * 2 + p, p, j, "gate")
            with eng.Fori(GATE_TILES // 2, jobs // 2) as j:
                for p in range(2):
                    body(j * 2 + p, p, j, "down")
            j = jobs // 2
            if jobs % 2:
                body(2 * j, 0, j, "down")
                body(2 * j + 1, 1, j, None)
                j += 1
            with eng.Fori(j, NB // 2 - 1) as j:
                for p in range(2):
                    body(j * 2 + p, p, j, None)
            for p in range(2):
                body(NB - 2 + p, p, NB // 2 - 1, None)

        def stage(b, k):
            return not isinstance(b, int) or 0 <= b - k < SLOT_TILES

        block = stack.enter_context(nc.Block())

        @block.sync
        def _(sp):
            for s in m["first"]:
                sp.sem_clear(s)
            sp.dma_start(brow[:], bias.rearrange("(a n) -> a n", a=1)).then_inc(ld_b, 16)

            def body(b, p, j, job):
                if job:
                    need(sp, wq_r, b - 1)
                    if job == "gate":
                        sp.dma_start(wst[:, p, :], gate_w[bass.ds(b * P, P), :]).then_inc(ld_wst[p], 16)
                    else:
                        sp.dma_start(wst[:, p, :].rearrange("p (t n) -> p t n", n=P),
                                     down_w[:, bass.ds((b - GATE_TILES) * P, P)].rearrange("(t p) n -> p t n", p=P)
                                     ).then_inc(ld_wst[p], 16)
                if stage(b, 0):
                    if isinstance(b, int) and b == 0:
                        for k in range(XS):
                            sp.wait_ge(sent[k], 32 * B // XS)
                    need(sp, x_t, b - 1)
                    sp.dma_start(xg[:, p, :], slots_in[bass.ds(b * P, P), :]).then_inc(ld_xg[p], 16)
                if stage(b, 3):
                    sp.wait_ge(y_e, b - 2)
                    sp.dma_start(slots_out[bass.ds((b - 3) * P, P), :], y[:, 1 - p, :]).then_inc(stored[1 - p], 16)

            run(sp, body)
            sp.wait_ge(y_e, SLOT_TILES)
            sp.dma_start(slots_out[(SLOT_TILES - 1) * P:, :], y[:, (SLOT_TILES - 1) % 2, :]
                         ).then_inc(stored[(SLOT_TILES - 1) % 2], 16)
            for p in range(2):
                sp.wait_ge(stored[p], 16 * SLOT_TILES // 2)

        @block.gpsimd
        def _(pool):
            pool.memset(onesb[:], 1.0).then_inc(cst, 1)
            pool.wait_ge(cst, 1)
            pool.affine_select(out=tri[:], in_=onesb[:], compare_op=ALU.is_ge, fill=0.0, base=-1,
                               pattern=[[1, P]], channel_multiplier=-1).then_inc(cst, 1)
            pool.wait_ge(s_pos, 2)
            with pool.Fori(0, B // XS) as j:
                for k in range(XS):
                    need(pool, xs_ready, j * XS + k + 1, True)
                    for c in range(2):
                        pool.indirect_dma_start(
                            out=slots_in, out_offset=bass.IndirectOffsetOnAxis(
                                ap=slot[:, k, c:c + 1], axis=0),
                            in_=xs[:, k, :], in_offset=None).then_inc(sent[k], 16)
            for k in range(XS):
                pool.wait_ge(sent[k], 32 * B // XS)

        @block.tensor
        def _(pe):
            pe.wait_ge(ld_b, 16)
            pe.matmul(GB[:, 0:E], ones[0:1, :], brow[:], start=True, stop=True).then_inc(s_bias, 1)
            pe.wait_ge(s_sum, 1)
            pe.matmul(YB[0][:, 0:2], ones[:], asum[:], start=True, stop=True).then_inc(s_bias, 1)
            pe.wait_ge(s_both, 1)
            pe.wait_ge(cst, 2)
            ahead = XB[0][:, 0:B * E]
            pe.matmul(ahead, tri[:], both[:].rearrange("p b e -> p (b e)"), start=True, stop=False)
            for s in range(1, B):
                pe.matmul(ahead[:, s * E:], onesb[:], both[:, 0:B - s, :].rearrange("p b e -> p (b e)"),
                          start=False, stop=(s == B - 1))
            for s in range(B):
                last = pe.matmul(XB[1][:, 0:E], onesb[:], both[:, s, :], start=(s == 0), stop=(s == B - 1))
            last.then_inc(s_cnt, 1)
            pe.wait_ge(s_table, 1)

            def expert(i):
                pe.nop(nofuse=True)
                return pe.value_load(which[0:1, bass.ds(i, 1)], min_val=0, max_val=E - 1)

            def body(b, p, j, job):
                if stage(b, 2):
                    pe.wait_ge(g_done, b - 1)
                    need(pe, g_e, b - 2)
                    for c in range(FC):
                        last = pe.transpose(GB[:, c * P:(c + 1) * P], g[:, p, c * P:(c + 1) * P], ident[:])
                    last.then_inc(g_t, 1)
                if stage(b, 0):
                    pe.wait_ge(ld_xg[p], 16 * (j + 1))
                    need(pe, x_e, b - 1)
                    for c in range(HC):
                        last = pe.transpose(XB[p][:, c * P:(c + 1) * P], xg[:, p, c * P:(c + 1) * P], ident[:])
                    last.then_inc(x_t, 1)
                if stage(b, 1):
                    pe.wait_ge(x_e, b)
                    need(pe, g_done, b - 2)
                    e = expert(b - 1)
                    for c in range(HC):
                        last = pe.matmul(HB[1 - p][:], xT[:, 1 - p, c, :], at(W13T, e, c), start=(c == 0),
                                         stop=(c == HC - 1))
                    last.then_inc(h_done, 1)
                if job:
                    pe.wait_ge(wq_done, b + 1)
                    need(pe, wq_e, b)
                    for c in range(4):
                        last = pe.transpose(WB[:, c * P:(c + 1) * P], wq[:, p, c * P:(c + 1) * P], identb[:])
                    last.then_inc(wq_t, 1)
                if stage(b, 2):
                    pe.wait_ge(g_e, b - 1)
                    need(pe, y_e, b - 2)
                    e = expert(b - 2)
                    for c in range(FC):
                        last = pe.matmul(YB[p][:], gT[:, c, :], at(W2T, e, c), start=(c == 0), stop=(c == FC - 1))
                    last.then_inc(y_done, 1)

            run(pe, body)

        @block.scalar
        def _(act):
            act.activation(prob[:], logits[:], ACT.Exp, scale=-1.0).then_inc(s_exp, 1)

            def body(b, p, j, job):
                if stage(b, 2):
                    act.wait_ge(g_t, b - 1)
                    need(act, y_done, b - 2)
                    act.copy(gT[:], GB[:, 0:FF].rearrange("p (c n) -> p c n", c=FC)).then_inc(g_e, 1)
                if stage(b, 0):
                    act.wait_ge(x_t, b + 1)
                    need(act, h_done, b - 1)
                    act.copy(xT[:, p], XB[p][:].rearrange("p (c n) -> p c n", c=HC)).then_inc(x_e, 1)
                if stage(b, 1):
                    act.wait_ge(h_done, b)
                    need(act, g_done, b - 1)
                    act.activation(sg[:], HB[1 - p][:, 0:FF], ACT.Silu).then_inc(silu_done, 1)
                if job:
                    act.wait_ge(wq_t, b + 1)
                    src = WB[:, 0:H]
                    if job == "gate":
                        act.copy(gateT[:, :, bass.ds(b * P, P)], src.rearrange("p (c n) -> p c n", c=HC)).then_inc(wq_e, 1)
                    else:
                        act.copy(at(downT, b - GATE_TILES), src).then_inc(wq_e, 1)

            run(act, body)

        @block.vector
        def _(dve):
            step = Steps(dve, steps)
            then = step.then
            dve.tensor_reduce(asum[:], m["absum"][:], AX.X, ALU.add).then_inc(s_sum, 1)
            then(dve.tensor_tensor_scan(iota[:], ones[:, 0:SLOT_TILES], ones[:, 0:SLOT_TILES], -1.0,
                                        ALU.mult, ALU.add))
            then(dve.tensor_scalar(order[:], iota[:, 0:E], -1.0, float(E), ALU.mult, ALU.add))
            dve.wait_ge(s_bias, 2)
            for k, n in enumerate((2 * INTER * H, INTER * H)):
                step.mark(dve.tensor_scalar(m["wmean"][:, k:k + 1], YB[0][:, k:k + 1], 1.0 / n, 1e-5, ALU.mult, ALU.max))
            dve.wait_ge(steps, step.n)
            then(dve.reciprocal(m["wscale"][:], m["wmean"][:]))
            dve.wait_ge(s_exp, 1)
            then(dve.tensor_scalar(tmp[:], prob[:], 1.0, None, ALU.add))
            then(dve.reciprocal(prob[:], tmp[:]))
            then(dve.tensor_tensor(score[:], prob[:], GB[:, None, 0:E].broadcast_to([P, B, E]), ALU.add))

            def spread(t):
                return t[:, :, None].broadcast_to([P, B, E])

            for c in range(2):
                then(dve.tensor_reduce(best[:], score[:], AX.X, ALU.max))
                then(dve.tensor_tensor(tmp[:], score[:], spread(best), ALU.is_ge))
                then(dve.tensor_tensor(tmp[:], tmp[:], order[:, None, :].broadcast_to([P, B, E]), ALU.mult))
                then(dve.tensor_reduce(best[:], tmp[:], AX.X, ALU.max))
                then(dve.tensor_tensor(pick[:, c], tmp[:], spread(best), ALU.is_equal))
                if c == 0:
                    then(dve.scalar_tensor_tensor(score[:].rearrange("p b e -> p (b e)"),
                                                  pick[:, 0].rearrange("p b e -> p (b e)"), -BIG,
                                                  score[:].rearrange("p b e -> p (b e)"), ALU.mult, ALU.add))
            dve.tensor_tensor(both[:], pick[:, 0], pick[:, 1], ALU.add).then_inc(s_both, 1)
            for c in range(2):
                then(dve.tensor_tensor(tmp[:], prob[:], pick[:, c], ALU.mult))
                then(dve.tensor_reduce(m["wt"][:, c, :], tmp[:], AX.X, ALU.add))
            then(dve.tensor_tensor(den[:], m["wt"][:, 0, :], m["wt"][:, 1, :], ALU.add))
            then(dve.reciprocal(den[:], den[:]))
            then(dve.tensor_tensor(m["wt"][:], m["wt"][:], den[:, None, :].broadcast_to([P, 2, B]), ALU.mult))
            dve.wait_ge(s_cnt, 1)
            then(dve.tensor_scalar(tiles[:], XB[1][:, 0:E], P / 2 - 0.5, 1.0 / P, ALU.add, ALU.mult))
            then(dve.tensor_scalar(tiles[:], tiles[:], ROUND, -ROUND, ALU.add, ALU.add))
            then(dve.tensor_tensor_scan(upto[:], ones[:, 0:E], tiles[:], 0.0, ALU.mult, ALU.add))
            then(dve.tensor_tensor(base[:], upto[:], tiles[:], ALU.subtract))
            then(dve.tensor_scalar(base[:], base[:], float(P), None, ALU.mult))
            then(dve.tensor_tensor(score[:], XB[0][:, 0:B * E].rearrange("p (b e) -> p b e", e=E),
                                   base[:, None, :].broadcast_to([P, B, E]), ALU.add))
            for c in range(2):
                then(dve.tensor_tensor(tmp[:], score[:], pick[:, c], ALU.mult))
                then(dve.tensor_reduce(best[:], tmp[:], AX.X, ALU.add))
                dve.tensor_copy(m["pos"][:, c, :], best[:]).then_inc(s_pos, 1)
                dve.wait_ge(s_pos, c + 1)
            then(dve.tensor_tensor(cmp[:], upto[0:1, None, :].broadcast_to([1, SLOT_TILES, E]),
                                   iota[0:1, :, None].broadcast_to([1, SLOT_TILES, E]), ALU.is_le))
            then(dve.tensor_reduce(whichf[:], cmp[:], AX.X, ALU.add))
            dve.tensor_scalar(which[:], whichf[:], float(E - 1), None, ALU.min).then_inc(s_table, 1)
            with dve.Fori(0, B // XS) as j:
                for k in range(XS):
                    i = j * XS + k
                    dve.wait_ge(sent[k], 32 * j)
                    dve.tensor_copy(slot[:, k, :], m["pos"][:, :, bass.ds(i, 1)].rearrange("p c o -> p (c o)"))
                    dve.tensor_scalar(xs[:, k, :], at(X, i), at(m["stats2"], i, slice(0, 1)),
                                      m["rstd2"][:, bass.ds(i, 1)], ALU.subtract, ALU.mult).then_inc(xs_ready, 1)

            def body(b, p, j, job):
                if job:
                    k = 0 if job == "gate" else 1
                    dve.wait_ge(ld_wst[p], 16 * (j + 1))
                    need(dve, wq_done, b)
                    dve.tensor_scalar(wr[:], wst[:, p, :], m["wscale"][:, k:k + 1], ROUND, ALU.mult,
                                      ALU.add).then_inc(wq_r, 1)
                    dve.wait_ge(wq_r, b + 1)
                    need(dve, wq_t, b - 1)
                    dve.tensor_scalar(wr[:], wr[:], -ROUND, 1.0, ALU.add, ALU.min).then_inc(wq_m, 1)
                    dve.wait_ge(wq_m, b + 1)
                    dve.tensor_scalar(wq[:, p, :], wr[:], -1.0, None, ALU.max).then_inc(wq_done, 1)
                if stage(b, 1):
                    dve.wait_ge(silu_done, b)
                    need(dve, g_t, b - 2)
                    dve.tensor_tensor(g[:, 1 - p, :], HB[1 - p][:, FF:2 * FF], sg[:], ALU.mult).then_inc(g_done, 1)
                if stage(b, 2):
                    dve.wait_ge(y_done, b - 1)
                    need(dve, stored[p], 16 * (j - 1))
                    dve.tensor_copy(y[:, p, :], YB[p][:]).then_inc(y_e, 1)

            run(dve, body)


def layer1(nc, m, slots_out, gnorm, dnorm, out):
    X, CTX, ident, identb, half = m["X"], m["CTX"], m["ident"], m["identb"], m["half"]
    gateT = m["R"][:, 0:HC * 2 * INTER].rearrange("p (c n) -> p c n", c=HC)
    downT = m["R"][:, HC * 2 * INTER:].rearrange("p (c n) -> p c n", c=IC)
    SCALE = float(HD1) ** -0.5
    NB = B + 4
    SLOT = 32
    HV = HD1 + 1
    OH = QH // 2
    with ExitStack() as stack:
        def sb(name, shape, dt=F32):
            return stack.enter_context(nc.sbuf_tensor("c_" + name, shape, dt))

        def sem(name):
            return m["sem"]("c_" + name)

        def bank(name):
            return stack.enter_context(nc.psum_tensor("c_" + name, [P, 512], F32))

        g1 = sb("g1", [P, H])
        g2 = sb("g2", [P, INTER])
        nround = sb("nround", [P, 1])
        yg = sb("yg", [P, 2, 2, H])
        slot = sb("slot", [P, 2, 2], U32)
        xn = sb("xn", [P, GROUP, KVH, SLOT])
        qT = sb("qT", [P, 2, GROUP, 2, P])
        kT = sb("kT", [P, 2, 2, P])
        V = sb("V", [P, 2, KVH, SLOT])
        D = sb("D", [P, 2, HG, P])
        mx = sb("mx", [P, 2, HG])
        PB = sb("PB", [P, 2, HG, P])
        PT = sb("PT", [P, 2, HG, P])
        On = sb("On", [P, H])
        rden = sb("rden", [P, 2, OH])
        st = sb("st", [P, 2, 6])
        mv3 = sb("mv3", [P, 2])
        rs3 = sb("rs3", [P, 2])
        mv4 = sb("mv4", [P, 2])
        nrm = sb("nrm", [P, 4])
        t1 = sb("t1", [P, H])
        am = sb("am", [P, 4])
        mq = sb("mq", [P, 1])
        dqg = sb("dqg", [P, 2, 2])
        xq = sb("xq", [P, H], BF16)
        xqT = sb("xqT", [P, HC, P], BF16)
        th = sb("th", [P, H])
        ga = sb("ga", [P, H])
        h = sb("h", [P, INTER])
        hg = sb("hg", [P, INTER])
        junk = sb("junk", [P, INTER], BF16)
        ss = sb("ss", [P, 1])
        hn = sb("hn", [P, 4])
        ah = sb("ah", [P, 4])
        hm = sb("hm", [P, 3])
        dqd = sb("dqd", [P, 2])
        hq = sb("hq", [P, INTER], BF16)
        hT = sb("hT", [P, IC, P], BF16)
        xo = sb("xo", [P, 2, H])

        S = [bank("S0"), bank("S1")]
        T = [bank("T0"), bank("T1")]
        O = [bank("O0"), bank("O1")]
        GB, UB = bank("G"), bank("U")

        ld_g = sem("ld_g")
        gathered = [sem("gathered0"), sem("gathered1")]
        stored = [sem("stored0"), sem("stored1")]
        kinds = ["T0", "T1", "kT", "q0", "q1", "T2", "xqT", "T3", "T4", "hTa", "T5", "hTb", "T6", "T7"]
        delay = {k: 1 for k in kinds}
        delay.update(hTa=3, hTb=3, xqT=2, q0=0, q1=0, kT=0)
        ready = {k: sem("ready_" + k) for k in kinds}
        evac = {k: sem("evac_" + k) for k in kinds}
        s_done, s_max, s_sub, s_exp, pv_done, o_done = (
            sem(k) for k in ("s_done", "s_max", "s_sub", "s_exp", "pv_done", "o_done"))
        slot_set = sem("slot_set")
        v_set, x3_a, x3_done, stats3, rs3_done, xn_done, v_done = (
            sem(k) for k in ("v_set", "x3_a", "x3_done", "stats3", "rs3_done", "xn_done", "v_done"))
        x4_done, stats4, nrm_done, mq_done, xq_done = (
            sem(k) for k in ("x4_done", "stats4", "nrm_done", "mq_done", "xq_done"))
        gu_done, th_done, ga_done, h_done = (sem(k) for k in ("gu_done", "th_done", "ga_done", "h_done"))
        ss_done, hm_done, hg_done, hn_done, mh_done, hr_done, hq_done, down_done, out_done = (
            sem(k) for k in ("ss_done", "hm_done", "hg_done", "hn_done", "mh_done", "hr_done", "hq_done", "down_done", "out_done"))
        dve_steps, pool_steps = sem("dve_steps"), sem("pool_steps")

        def stage(b, k):
            return not isinstance(b, int) or 0 <= b - k < B

        def before(kind, b):
            i = kinds.index(kind)
            while True:
                i -= 2
                if i < 0:
                    i, b = i + len(kinds), b - 1
                if stage(b, delay[kinds[i]]) or (isinstance(b, int) and b < 0):
                    return kinds[i], b

        def tbank(kind):
            return T[kinds.index(kind) % 2]

        block = stack.enter_context(nc.Block())

        @block.sync
        def _(sp):
            sp.dma_start(g1[:], gnorm.rearrange("(a n) -> a n", a=1).broadcast_to([P, H])).then_inc(ld_g, 16)
            sp.dma_start(g2[:], dnorm.rearrange("(a n) -> a n", a=1).broadcast_to([P, INTER])).then_inc(ld_g, 16)

            def body(b, p, j):
                if stage(b, 4):
                    sp.wait_ge(out_done, b - 3)
                    sp.dma_start(out[bass.ds(b - 4, 1)].rearrange("o p d -> (o p) d"), xo[:, p, :]
                                 ).then_inc(stored[p], 16)

            bodies(sp, NB, body, head=2, tail=3)
            for p in range(2):
                sp.wait_ge(stored[p], 16 * B // 2)

        @block.gpsimd
        def _(pool):
            step = Steps(pool, pool_steps, alone=True)

            def gather(b, p):
                need(pool, x3_done, b - 1, True)
                pool.tensor_copy(slot[:, p, :], m["pos"][:, :, bass.ds(b, 1)].rearrange("p c o -> p (c o)")
                                 ).then_inc(slot_set, 1)
                need(pool, slot_set, b + 1, True)
                for c in range(2):
                    pool.indirect_dma_start(out=yg[:, p, c, :], out_offset=None, in_=slots_out,
                                            in_offset=bass.IndirectOffsetOnAxis(
                                                ap=slot[:, p, c:c + 1], axis=0)).then_inc(gathered[p], 16)

            def residual(b, k):
                need(pool, o_done, 2 * b - 1 + k, True)
                xb = X[:, b - 1, k * 256:(k + 1) * 256] if isinstance(b, int) else (
                    X[:, bass.ds(b - 1, 1), k * 256:(k + 1) * 256].rearrange("p o n -> p (o n)"))
                pool.tensor_tensor(xb, xb, On[:, k * 256:(k + 1) * 256], ALU.add).then_inc(x4_done, 1)

            def weighted(b, n):
                lo, size = CHUNKS[n]
                need(pool, h_done, 3 * (b - 2) + n + 1, True)
                if n == 0:
                    need(pool, hq_done, b - 2, True)
                pool.tensor_tensor(hg[:, lo:lo + size], h[:, lo:lo + size], g2[:, lo:lo + size],
                                   ALU.mult).then_inc(hg_done, 1)

            pool.memset(nround[:], -ROUND).then_inc(v_set, 1)
            pool.memset(V[:], 0.0).then_inc(v_set, 1)
            pool.memset(xn[:], 0.0).then_inc(v_set, 1)
            pool.wait_ge(v_set, 3)
            pool.memset(V[:, :, :, HD1:HV], 1.0).then_inc(v_set, 1)
            pool.wait_ge(v_set, 4)
            gather(0, 0)

            def front(b):
                need(pool, stats3, b + 1, True)
                need(pool, xn_done, b, True)
                step.then(pool.tensor_scalar(rs3[:, 0:1], mv3[:, 1:2], EPS, None, ALU.add))
                step.then(pool.tensor_tensor(rs3[:, 0:1], rs3[:, 0:1], half[:], ALU.pow))
                pool.tensor_scalar(rs3[:, 1:2], mv3[:, 0:1], rs3[:, 0:1], -1.0, ALU.mult, ALU.mult
                                   ).then_inc(rs3_done, 1)

            front(0)
            step.loop(12)

            def body(b, p, j):
                f, a, u, d, e = (stage(b, k) for k in range(5))
                step.body(b)
                if f:
                    need(pool, pv_done, 8 * b - 8, True)
                    pool.tensor_copy(V[:, p, :, 0:HD1],
                                     at(CTX, b).rearrange("p (k d) -> p k d", d=HD1)).then_inc(v_done, 1)
                if u:
                    need(pool, stats4, b - 1, True)
                    need(pool, mq_done, b - 2, True)
                    r, v, f3, g = (nrm[:, k:k + 1] for k in range(4))
                    step.then(pool.tensor_scalar(v, mv4[:, 1:2], EPS, None, ALU.add))
                    step.then(pool.tensor_tensor(r, v, half[:], ALU.pow))
                    step.then(pool.tensor_tensor(f3, r, r, ALU.mult))
                    step.then(pool.tensor_scalar(f3, f3, mv4[:, 1:2], EPS, ALU.mult, ALU.add))
                    step.then(pool.tensor_tensor(f3, f3, half[:], ALU.pow))
                    pool.tensor_tensor(g, r, f3, ALU.mult).then_inc(nrm_done, 1)
                if d:
                    c2, v2, r2, f2 = (hn[:, k:k + 1] for k in range(4))
                    need(pool, mh_done, b - 3, True)
                    step.then(pool.tensor_tensor(c2, dqg[:, 1 - p, 0:1], dqg[:, 1 - p, 1:2], ALU.mult))
                    step.then(pool.tensor_tensor(v2, c2, c2, ALU.mult))
                    need(pool, ss_done, b - 2, True)
                    step.then(pool.tensor_scalar(v2, v2, ss[:], 1.0 / INTER, ALU.mult, ALU.mult))
                    step.then(pool.tensor_scalar(v2, v2, EPS, None, ALU.add))
                    step.then(pool.tensor_tensor(r2, v2, half[:], ALU.pow))
                    pool.tensor_tensor(f2, r2, c2, ALU.mult).then_inc(hn_done, 1)
                if d:
                    need(pool, mh_done, b - 2, True)
                    pool.tensor_scalar(hg[:], hg[:], ah[:, 2:3], ROUND, ALU.mult, ALU.add).then_inc(hr_done, 1)
                if stage(b + 1, 0):
                    gather(b + 1, 1 - p)
                if u:
                    weighted(b, 0)
                if a:
                    residual(b, 0)
                if stage(b + 1, 0):
                    front(b + 1)
                if u:
                    weighted(b, 1)
                    weighted(b, 2)
                if a:
                    residual(b, 1)
                step.end()

            bodies(pool, NB, body, head=2, tail=3)

        @block.tensor
        def _(pe):
            def free(kind, b):
                k, bb = before(kind, b)
                need(pe, evac[k], bb - delay[k] + 1)

            def scores(b, p, g):
                q = 1 - p
                n = 8 * b - 8 + g
                need(pe, s_sub, n - 1)
                if g == 0:
                    pe.wait_ge(evac["q1"], b)
                    pe.wait_ge(evac["kT"], b)
                r = SLOT * (g % 4)
                for j in range(HG):
                    last = pe.matmul(S[g % 2][:, j * P:(j + 1) * P], qT[r:r + HD1, q, j, g // 4, :],
                                     kT[r:r + HD1, q, g // 4, :], start=True, stop=True, tile_position=(r, 0))
                last.then_inc(s_done, 1)

            def probs_t(b, p, g):
                pe.wait_ge(s_exp, 8 * b - 7 + g)
                free(f"T{g}", b)
                for j in range(HG):
                    last = pe.transpose(tbank(f"T{g}")[:, j * P:(j + 1) * P], PB[:, g % 2, j, :], ident[:])
                last.then_inc(ready[f"T{g}"], 1)

            def pv(b, p, g):
                q = 1 - p
                pe.wait_ge(evac[f"T{g}"], b)
                if g == 0:
                    pe.wait_ge(v_done, b)
                if g % 4 == 0:
                    need(pe, o_done, 2 * b - 3 + g // 4)
                for j in range(HG):
                    c = (HG * g + j) % OH * HV
                    last = pe.matmul(O[g // 4][:, c:c + HV], PT[:, g % 2, j, :], V[:, q, g, 0:HV],
                                     start=True, stop=True)
                last.then_inc(pv_done, 1)

            def transposes(kind, b, src, dt, idn, wait, value):
                pe.wait_ge(wait, value)
                free(kind, b)
                bk = tbank(kind)[:].bitcast(dt)
                for c, s in enumerate(src):
                    last = pe.transpose(bk[:, c * P:(c + 1) * P], s, idn[:])
                last.then_inc(ready[kind], 1)

            def gate_up(b, n):
                lo, size = CHUNKS[n]
                if n == 0:
                    pe.wait_ge(evac["xqT"], b - 1)
                for bk, first in ((GB, lo), (UB, INTER + lo)):
                    if bk is GB:
                        need(pe, ga_done, 3 * (b - 2) + n)
                    else:
                        need(pe, h_done, 3 * (b - 2) + n)
                        if n == 0 and stage(b, 4):
                            pe.wait_ge(out_done, b - 3)
                    for c in range(HC):
                        last = pe.matmul(bk[:, 0:size], xqT[:, c, :], gateT[:, c, first:first + size],
                                         start=(c == 0), stop=(c == HC - 1))
                last.then_inc(gu_done, 1)

            def down(b):
                pe.wait_ge(evac["hTb"], b - 3)
                pe.wait_ge(h_done, 3 * (b - 2) if stage(b, 3) else 3 * B)
                need(pe, out_done, b - 4)
                for c in range(IC):
                    last = pe.matmul(UB[:], hT[:, c, :], downT[:, c, :], start=(c == 0), stop=(c == IC - 1))
                last.then_inc(down_done, 1)

            def body(b, p, j):
                f, a, u, d, e = (stage(b, k) for k in range(5))

                def cols(t, lo, hi):
                    return [t[:, c * P:(c + 1) * P] for c in range(lo, hi)]

                def slot_of(g):
                    if g + 2 < KVH:
                        if a:
                            scores(b, p, g + 2)
                    elif f:
                        scores(b + 1, 1 - p, g + 2 - KVH)
                    if a:
                        if g > 0:
                            pv(b, p, g - 1)
                        probs_t(b, p, g)

                slot_of(0)
                slot_of(1)
                xv = xn[:].rearrange("p j k d -> p (j k d)")
                if f:
                    transposes("kT", b, cols(V[:, p].rearrange("p k d -> p (k d)"), 0, 2), F32, ident, v_done, b + 1)
                    transposes("q0", b, cols(xv, 0, 4), F32, ident, xn_done, b + 1)
                if e:
                    down(b)
                if f:
                    transposes("q1", b, cols(xv, 4, 8), F32, ident, xn_done, b + 1)
                slot_of(2)
                if u:
                    transposes("xqT", b, cols(xq, 0, HC), BF16, identb, xq_done, b - 1)
                slot_of(3)
                if u:
                    gate_up(b, 0)
                slot_of(4)
                if d:
                    transposes("hTa", b, cols(hq, 0, 8), BF16, identb, hq_done, b - 2)
                if u:
                    gate_up(b, 1)
                slot_of(5)
                if d:
                    transposes("hTb", b, cols(hq, 8, IC), BF16, identb, hq_done, b - 2)
                slot_of(6)
                slot_of(7)
                if u:
                    gate_up(b, 2)
                if a:
                    pv(b, p, 7)

            bodies(pe, NB, body, head=2, tail=3)

        @block.scalar
        def _(act):
            act.wait_ge(v_set, 4)

            def take(kind, b, dst, src):
                act.wait_ge(ready[kind], b - delay[kind] + 1)
                act.copy(dst, src).then_inc(evac[kind], 1)

            def view(kind, dt, n):
                return tbank(kind)[:].bitcast(dt)[:, 0:n * P].rearrange("p (c n) -> p c n", n=P)

            def body(b, p, j):
                f, a, u, d, e = (stage(b, k) for k in range(5))

                def exps(g):
                    if not (a if g < KVH else f):
                        return
                    n = 8 * b - 8 + g
                    act.wait_ge(s_sub, n + 1)
                    if g >= 2:
                        if a:
                            act.wait_ge(ready[f"T{g - 2}"], b)
                    else:
                        need(act, ready[f"T{g + 6}"], b - 1)
                    act.activation(PB[:, g % 2], D[:, g % 2], ACT.Exp, scale=SCALE).then_inc(s_exp, 1)

                def probs(g):
                    if a:
                        need(act, pv_done, 8 * b - 8 + g - 1)
                        take(f"T{g}", b, PT[:, g % 2], view(f"T{g}", F32, HG))

                def gates(n):
                    if u:
                        lo, size = CHUNKS[n]
                        act.wait_ge(gu_done, 3 * (b - 2) + n + 1)
                        need(act, ga_done, 3 * (b - 2) + n)
                        act.activation(th[:, 0:size], GB[:, 0:size], ACT.Tanh, scale=dqg[:, p, 1:2]).then_inc(th_done, 1)

                probs(0)
                if f:
                    need(act, rs3_done, b + 1, True)
                    need(act, ready["q1"], b, True)
                    act.activation(xn[:, :, :, 0:HD1].rearrange("p j k d -> p k j d"),
                                   at(X, b).rearrange("p (k j d) -> p k j d", k=KVH, j=GROUP), ACT.Identity,
                                   bias=rs3[:, 1:2], scale=rs3[:, 0:1]).then_inc(xn_done, 1)
                if d:
                    need(act, hn_done, b - 3)
                    act.wait_ge(h_done, 3 * (b - 2))
                    act.activation(junk[:], h[:], ACT.Square, accum_out=ss[:]).then_inc(ss_done, 1)
                exps(2)
                probs(1)
                if f:
                    take("kT", b, kT[:, p], view("kT", F32, 2))
                    take("q0", b, qT[:, p, 0:2].rearrange("p j c n -> p (j c) n"), view("q0", F32, 4))
                exps(3)
                if f:
                    take("q1", b, qT[:, p, 2:4].rearrange("p j c n -> p (j c) n"), view("q1", F32, 4))
                probs(2)
                if u:
                    need(act, gu_done, 3 * (b - 2))
                    take("xqT", b, xqT[:], view("xqT", BF16, HC))
                exps(4)
                if d:
                    act.wait_ge(hr_done, b - 2)
                    need(act, ready["hTb"], b - 3)
                    act.activation(hq[:], hg[:], ACT.Identity, bias=nround[:]).then_inc(hq_done, 1)
                probs(3)
                gates(0)
                exps(5)
                probs(4)
                if d:
                    need(act, down_done, b - 3)
                    take("hTa", b, hT[:, 0:8, :], view("hTa", BF16, 8))
                exps(6)
                probs(5)
                if d:
                    take("hTb", b, hT[:, 8:IC, :], view("hTb", BF16, IC - 8))
                gates(1)
                exps(7)
                probs(6)
                exps(8)
                probs(7)
                exps(9)
                gates(2)

            bodies(act, NB, body, head=2, tail=3)

        @block.vector
        def _(dve):
            step = Steps(dve, dve_steps, alone=True)
            dve.wait_ge(ld_g, 32)

            def front(b, p, j):
                xf = at(X, b)
                dve.wait_ge(gathered[p], 32 * (j + 1))
                dve.scalar_tensor_tensor(xf, yg[:, p, 0, :], m["wt"][:, 0, bass.ds(b, 1)], xf, ALU.mult,
                                         ALU.add).then_inc(x3_a, 1)
                dve.wait_ge(x3_a, b + 1)
                dve.scalar_tensor_tensor(xf, yg[:, p, 1, :], m["wt"][:, 1, bass.ds(b, 1)], xf, ALU.mult,
                                         ALU.add).then_inc(x3_done, 1)
                need(dve, x3_done, b + 1, True)
                step.then(dve.bn_stats(st[:, 1, :], xf))
                need(dve, rs3_done, b, True)
                dve.bn_aggr(mv3[:], st[:, 1, :]).then_inc(stats3, 1)

            front(0, 0, 0)
            step.loop(15)

            def body(b, p, j):
                f, a, u, d, e = (stage(b, k) for k in range(5))
                step.body(b)

                def softmax_head(g):
                    if not (a if g < KVH else f):
                        return
                    n = 8 * b - 8 + g
                    dve.wait_ge(s_done, n + 1)
                    bk = S[g % 2][:].rearrange("p (h k) -> p h k", h=HG)
                    dve.tensor_reduce(mx[:, g % 2, :], bk, AX.X, ALU.max).then_inc(s_max, 1)
                    dve.wait_ge(s_max, n + 1)
                    need(dve, s_exp, n - 1)
                    dve.tensor_tensor(D[:, g % 2], bk, mx[:, g % 2, :, None].broadcast_to([P, HG, P]),
                                      ALU.subtract).then_inc(s_sub, 1)

                def out_half(k):
                    if not a:
                        return
                    dve.wait_ge(pv_done, 8 * b - 8 + 4 * (k + 1))
                    bk = O[k][:, 0:OH * HV].rearrange("p (h d) -> p h d", h=OH)
                    step.then(dve.reciprocal(rden[:, k, :], bk[:, :, HD1]))
                    need(dve, x4_done, 2 * b - 3 + k)
                    dve.tensor_tensor(On[:, k * 256:(k + 1) * 256].rearrange("p (h d) -> p h d", h=OH),
                                      bk[:, :, 0:HD1], rden[:, k, :, None].broadcast_to([P, OH, HD1]),
                                      ALU.mult).then_inc(o_done, 1)

                def gated(n):
                    if not u:
                        return
                    lo, size = CHUNKS[n]
                    k = 3 * (b - 2) + n
                    dve.wait_ge(th_done, k + 1)
                    need(dve, h_done, k)
                    if n == 0 and d:
                        dve.wait_ge(ss_done, b - 2)
                        dve.wait_ge(hg_done, 3 * (b - 2))
                    dve.scalar_tensor_tensor(ga[:, 0:size], th[:, 0:size], 1.0, GB[:, 0:size], ALU.add,
                                             ALU.mult).then_inc(ga_done, 1)
                    dve.wait_ge(ga_done, k + 1)
                    dve.tensor_tensor(h[:, lo:lo + size], UB[:, 0:size], ga[:, 0:size], ALU.mult).then_inc(h_done, 1)

                def chunk_max(b, n):
                    lo, size = CHUNKS[n]
                    dve.wait_ge(hg_done, 3 * (b - 2) + n + 1)
                    dve.tensor_reduce(hm[:, n:n + 1], hg[:, lo:lo + size], AX.X, ALU.max,
                                      apply_absolute_value=True).then_inc(hm_done, 1)

                softmax_head(2)
                a0, a1, a2 = (am[:, k:k + 1] for k in range(3))
                b0, b1, b2, b3 = (ah[:, k:k + 1] for k in range(4))
                if u:
                    xb = at(X, b - 2)
                    need(dve, x4_done, 2 * (b - 1), True)
                    step.then(dve.bn_stats(st[:, 0, :], xb))
                    dve.bn_aggr(mv4[:], st[:, 0, :]).then_inc(stats4, 1)
                if u:
                    need(dve, stats4, b - 1, True)
                    t1_done = step.mark(dve.scalar_tensor_tensor(t1[:], xb, mv4[:, 0:1], g1[:], ALU.subtract, ALU.mult))
                if d:
                    chunk_max(b - 1, 2)
                if u:
                    dve.wait_ge(dve_steps, t1_done)
                    a0_done = step.mark(dve.tensor_reduce(a0, t1[:], AX.X, ALU.max, apply_absolute_value=True))
                if d:
                    dve.wait_ge(hm_done, 3 * (b - 2))
                    b0_done = step.mark(dve.tensor_reduce(b0, hm[:], AX.X, ALU.max))
                softmax_head(3)
                if d:
                    dve.wait_ge(hn_done, b - 2)
                    dve.wait_ge(dve_steps, b0_done)
                    b1_done = step.mark(dve.tensor_scalar(b1, b0, hn[:, 3:4], 1e-5, ALU.mult, ALU.max))
                if u:
                    dve.wait_ge(nrm_done, b - 1)
                    dve.wait_ge(dve_steps, a0_done)
                    a1_done = step.mark(dve.tensor_scalar(a1, a0, nrm[:, 3:4], 1e-5, ALU.mult, ALU.max))
                if d:
                    dve.wait_ge(dve_steps, b1_done)
                    b3_done = step.mark(dve.reciprocal(b3, b1))
                if u:
                    dve.wait_ge(dve_steps, a1_done)
                    a2_done = step.mark(dve.reciprocal(a2, a1))
                if d:
                    dve.wait_ge(dve_steps, b3_done)
                    need(dve, hr_done, b - 3)
                    dve.tensor_scalar(b2, b3, 127.0, hn[:, 3:4], ALU.mult, ALU.mult).then_inc(mh_done, 1)
                if u:
                    dve.wait_ge(dve_steps, a2_done)
                    dve.tensor_scalar(mq[:], a2, 127.0, nrm[:, 3:4], ALU.mult, ALU.mult).then_inc(mq_done, 1)
                    need(dve, hn_done, b - 3)
                    dqg_done = step.mark(dve.tensor_scalar(dqg[:, p, 0:1], a1, 1.0 / 127.0, m["wmean"][:, 0:1],
                                                           ALU.mult, ALU.mult))
                if d:
                    step.mark(dve.tensor_scalar(dqd[:, p:p + 1], b1, 1.0 / 127.0, m["wmean"][:, 1:2], ALU.mult, ALU.mult))
                if u:
                    dve.wait_ge(mq_done, b - 1)
                    tr_done = step.mark(dve.tensor_scalar(t1[:], t1[:], mq[:], ROUND, ALU.mult, ALU.add))
                    dve.wait_ge(dve_steps, dqg_done)
                    step.mark(dve.tensor_scalar(dqg[:, p, 1:2], dqg[:, p, 0:1], 0.5, None, ALU.mult))
                    dve.wait_ge(dve_steps, tr_done)
                    need(dve, ready["xqT"], b - 2)
                    dve.tensor_scalar(xq[:], t1[:], -ROUND, None, ALU.add).then_inc(xq_done, 1)
                softmax_head(4)
                if e:
                    dve.wait_ge(down_done, b - 3)
                    need(dve, stored[p], 16 * (j - 2))
                    dve.scalar_tensor_tensor(xo[:, p, :], UB[:], dqd[:, 1 - p:2 - p], at(X, b - 4), ALU.mult,
                                             ALU.add).then_inc(out_done, 1)
                softmax_head(5)
                gated(0)
                softmax_head(6)
                out_half(0)
                if u:
                    chunk_max(b, 0)
                softmax_head(7)
                if stage(b + 1, 0):
                    front(b + 1, 1 - p, j + p)
                gated(1)
                softmax_head(8)
                softmax_head(9)
                if u:
                    chunk_max(b, 1)
                gated(2)
                out_half(1)
                step.end()

            bodies(dve, NB, body, head=2, tail=3)


_INS = ['x', 'ctx_512', 'L0_xattn_Wq', 'L0_xattn_Wkv_expand', 'L0_xattn_Wout', 'L0_ffn_Wg', 'L0_ffn_W1', 'L0_ffn_W2',
        'L0_ffn_W3', 'L0_ffn_bias', 'L1_ffn_gate_w', 'L1_ffn_down_w', 'L1_ffn_gate_norm_w', 'L1_ffn_down_norm_w']


def kernel(**inputs):
    import numpy as np
    import concourse.bacc as bacc
    from concourse import mybir as _mybir
    from concourse.bass_utils import run_bass_kernel_spmd

    nc = bacc.Bacc("TRN2", target_bir_lowering=False, num_devices=1)
    arrays, args = {}, {}
    for name in _INS:
        a = np.ascontiguousarray(inputs[name])
        arrays[f"in_{name}"] = a
        args[name] = nc.dram_tensor(f"in_{name}", a.shape, _mybir.dt.from_np(a.dtype), kind="ExternalInput").ap()
    out = nc.dram_tensor("out", (B, P, H), _mybir.dt.float32, kind="ExternalOutput").ap()
    decoder_kernel(nc, args["x"], args["ctx_512"], args["L0_xattn_Wq"], args["L0_xattn_Wkv_expand"],
                   args["L0_xattn_Wout"], args["L0_ffn_Wg"], args["L0_ffn_W1"], args["L0_ffn_W2"],
                   args["L0_ffn_W3"], args["L0_ffn_bias"], args["L1_ffn_gate_w"], args["L1_ffn_down_w"],
                   args["L1_ffn_gate_norm_w"], args["L1_ffn_down_norm_w"], out)
    r = run_bass_kernel_spmd(nc, [arrays], core_ids=[0])
    return r.results[0]["out"]
```

```python
from contextlib import ExitStack

import concourse.bass as bass
from concourse import mybir

P = 128
ALU = mybir.AluOpType
ACT = mybir.ActivationFunctionType
AX = mybir.AxisListType
F32 = mybir.dt.float32
BF16 = mybir.dt.bfloat16
I32 = mybir.dt.int32
U32 = mybir.dt.uint32

B = 16
H = 512
HC = H // P
L = 128
EPS = 1e-5
NH0, HD0 = 16, 32
E, FF = 8, 256
FC = FF // P
QH, KVH, HD1 = 32, 8, 16
GROUP = QH // KVH
INTER = 1408
IC = INTER // P
GATE_TILES = 2 * INTER // P
SLOT_TILES = (2 * B * P + E * (P - 1)) // P
SLOTS = SLOT_TILES * P
REGION = B * P + P
ZERO_ROW = E * REGION
NEG = -3.0e38
BIG = 3.0e38
ROUND = 12582912.0
GATE_ABS = GATE_TILES * H // B
DOWN_ABS = HC * INTER // B
CHUNKS = [(0, 512), (512, 512), (1024, 384)]
HG = 4


def need(eng, sem, value, alone=False):
    if isinstance(value, int) and value <= 0:
        return
    eng.wait_ge(sem, value)
    if alone and not isinstance(value, int):
        eng.nop(nofuse=True)


def at(t, i, *rest):
    if isinstance(i, int):
        return t[(slice(None), i) + rest]
    ap = t[(slice(None), bass.ds(i, 1)) + rest]
    n = len(ap.shape)
    names = " ".join("abcdef"[k] for k in range(n - 2))
    return ap.rearrange(f"p o {names} -> p (o a) {names[2:]}" if n > 2 else "p o -> p o")


def bodies(eng, count, body, head=1, tail=1):
    for b in range(2 * head):
        body(b, b % 2, b // 2)
    with eng.Fori(head, count // 2 - tail) as j:
        for p in range(2):
            body(j * 2 + p, p, j)
    for b in range(count - 2 * tail, count):
        body(b, b % 2, b // 2)


class Steps:

    def __init__(self, eng, sem, per=0, alone=False):
        self.eng, self.sem, self.per, self.alone, self.first, self.base, self.n = eng, sem, per, alone, 0, 0, 0

    def loop(self, per):
        self.first, self.per, self.alone = self.n, per, True

    def body(self, b):
        self.base, self.n = b * self.per + self.first, 0

    def mark(self, ins):
        ins.then_inc(self.sem, 1)
        self.n += 1
        return self.base + self.n

    def then(self, ins):
        need(self.eng, self.sem, self.mark(ins), self.alone)

    def end(self):
        rest = self.per - self.n
        assert rest >= 0, (self.n, self.per)
        if rest:
            self.eng.drain().then_inc(self.sem, rest)
        self.n = self.per
        self.eng.wait_ge(self.sem, self.base + self.n)


def decoder_kernel(nc, x, ctx, Wq, Wkv, Wout, Wg, W1, W2, W3, bias, gate_w, down_w, gnorm, dnorm, out):
    slots_in = nc.dram_tensor("slots_in", [ZERO_ROW + P, H], F32, kind="Internal").ap()
    slots_out = nc.dram_tensor("slots_out", [SLOTS, H], F32, kind="Internal").ap()
    with ExitStack() as stack:
        def sb(name, shape, dt=F32):
            return stack.enter_context(nc.sbuf_tensor(name, shape, dt))

        def sem(name):
            return stack.enter_context(nc.semaphore(name))

        m = {}
        m["X"] = sb("X", [P, B, H])
        m["CTX"] = sb("CTX", [P, B, L])
        m["ident"] = sb("ident", [P, P])
        m["identb"] = sb("identb", [P, P], BF16)
        m["absum"] = sb("absum", [P, 2, B])
        m["ones"] = sb("ones", [P, P])
        m["half"] = sb("half", [P, 1])
        m["pos"] = sb("pos", [P, 2, B], U32)
        m["wt"] = sb("wt", [P, 2, B])
        m["wmean"] = sb("wmean", [P, 2])
        m["wscale"] = sb("wscale", [P, 2])
        m["R"] = sb("R", [P, HC * 2 * INTER + IC * H], BF16)
        m["sent"] = [sem("sent0"), sem("sent1")]
        with ExitStack() as moe:
            m["first"] = []
            m["sem"] = lambda name: m["first"].append(moe.enter_context(nc.semaphore(name))) or m["first"][-1]
            m["W13T"] = moe.enter_context(nc.sbuf_tensor("W13T", [P, E, HC, 2 * FF], F32))
            m["W2T"] = moe.enter_context(nc.sbuf_tensor("W2T", [P, E, FC, H], F32))
            for name, shape, dt in (
                    ("prob", [P, B, E], F32),
                    ("pick", [P, 2, B, E], F32),
                    ("row_in", [P, 2, B], F32),
                    ("cum", [P, E], BF16),
                    ("tri", [P, P], BF16), ("onesb", [P, P], BF16),
                    ("iota", [P, SLOT_TILES], F32), ("ebase", [P, E], F32)):
                m[name] = moe.enter_context(nc.sbuf_tensor(name, shape, dt))
            layer0_attention(nc, m, x, ctx, Wq, Wkv, Wout, Wg, W1, W2, W3, bias, gate_w, down_w, slots_in)
            m["sem"] = sem
            experts(nc, m, gate_w, down_w, slots_in, slots_out)
        layer1(nc, m, slots_out, gnorm, dnorm, out)


def layer0_attention(nc, m, x, ctx, Wq, Wkv, Wout, Wg, W1, W2, W3, bias, gate_w, down_w, slots_in):
    X, CTX, ident, identb = m["X"], m["CTX"], m["ident"], m["identb"]
    W13T, W2T, ones, half = m["W13T"], m["W2T"], m["ones"], m["half"]
    tri, onesb, cum, iota, ebase = m["tri"], m["onesb"], m["cum"], m["iota"], m["ebase"]
    SCALE = float(HD0) ** -0.5
    NB = B + 4
    RANK = 64
    with ExitStack() as stack:
        def sb(name, shape, dt=F32):
            return stack.enter_context(nc.sbuf_tensor("a_" + name, shape, dt))

        def sem(name):
            return m["sem"]("a_" + name)

        def bank(name):
            return stack.enter_context(nc.psum_tensor("a_" + name, [P, 512], F32))

        reg = m["R"][:, 0:2 * (2 * HC * H + 2 * H)].bitcast(F32)
        WqT = reg[:, 0:HC * H].rearrange("p (c f) -> p c f", c=HC)
        WoutT = reg[:, HC * H:2 * HC * H].rearrange("p (c f) -> p c f", c=HC)
        WkvT = reg[:, 2 * HC * H:2 * HC * H + 2 * H]
        WgT = sb("WgT", [P, HC, E])
        mask4 = sb("mask4", [P, HG, P], BF16)
        wn = sb("wn", [P, 3, H])
        pre = W13T[:, 0:2, :, :].rearrange("p e c n -> p (e c) n")
        prekv = W13T[:, 2, 0:2, :].rearrange("p c (t n) -> p (c t) n", n=P)
        preg = W13T[0:E, 3, 0, :]
        zero = W2T[:, E - 1, FC - 1, :]
        absn = sb("absn", [P, GATE_ABS + DOWN_ABS])
        xn = sb("xn", [P, H])
        xn2 = sb("xn2", [P, 2, H])
        brow = sb("brow", [P, E])
        order = sb("order", [P, E])
        ex = sb("ex", [P, E])
        rk = sb("rk", [P, E])
        pr = sb("pr", [P, E])
        score = sb("score", [P, E])
        mark = sb("mark", [P, E])
        best = sb("best", [P, 1])
        pk = sb("pk", [P, 2, E])
        both = sb("both", [P, E], BF16)
        row = sb("row", [P, 2, E])
        rowf = sb("rowf", [P, 2])
        slot = sb("slot", [P, 2, 2], U32)
        xT = sb("xT", [P, HC, P])
        x2T = sb("x2T", [P, HC, P])
        qT = sb("qT", [P, 2, HC, P])
        kT = sb("kT", [P, 2, HC, P])
        V = sb("V", [P, 2, NH0, HD0 + 1])
        mx = sb("mx", [P, 2, HG])
        spare = m["R"][:, 2 * (2 * HC * H + 2 * H):][:, 0:12 * H + 4 * P].bitcast(F32)
        D = spare[:, 0:2 * H].rearrange("p (g h k) -> p g h k", g=2, h=HG)
        PT = spare[:, 2 * H:4 * H].rearrange("p (g h k) -> p g h k", g=2, h=HG)
        On = spare[:, 4 * H:5 * H]
        OT = spare[:, 5 * H:6 * H].rearrange("p (c n) -> p c n", c=HC)
        cx = spare[:, 6 * H:6 * H + P]
        ctxT = spare[:, 6 * H + P:6 * H + 2 * P]
        rden = sb("rden", [P, 2, 8])
        st = sb("st", [P, 2, 6])
        mv1 = sb("mv1", [P, 2])
        rs1 = sb("rs1", [P, 1])
        mv2 = sb("mv2", [P, 2])
        rs2 = sb("rs2", [P, 1])

        S = [bank("S0"), bank("S1")]
        T = [bank("T0"), bank("T1")]
        Fb = bank("F")
        Dk = bank("Dk")
        O = [bank("O0"), bank("O1")]

        ld_x, ld_ctx = [sem("ld_x0"), sem("ld_x1")], [sem("ld_ctx0"), sem("ld_ctx1")]
        ld_wq, ld_wkv, ld_w = sem("ld_wq"), sem("ld_wkv"), sem("ld_w")
        ld_stage, ld_abs = sem("ld_stage"), sem("ld_abs")
        zeroed, filled = sem("zeroed"), sem("filled")
        consts, consts_dve = sem("consts"), sem("consts_dve")
        pre_t, pre_e = sem("pre_t"), sem("pre_e")
        front = ["xT", "cT", "K", "Q", "V"]
        att = ["T0", "T1", "T2", "T3", "W0", "W1", "W2"]
        tail = ["OT", "x2T"]
        ready = {k: sem("ready_" + k) for k in front + att + tail}
        evac = {k: sem("evac_" + k) for k in front + att + tail}
        s_done, s_max, s_sub, s_exp = sem("s_done"), sem("s_max"), sem("s_sub"), sem("s_exp")
        pv_done, o_done = sem("pv_done"), sem("o_done")
        rstd1_done, rstd2_done = sem("rstd1_done"), sem("rstd2_done")
        stats1, stats2, xn_done, xn2_done = sem("stats1"), sem("stats2"), sem("xn_done"), sem("xn2_done")
        y_done, x2_done, r_done = sem("y_done"), sem("x2_done"), sem("r_done")
        abs_done, cx_done = sem("abs_done"), sem("cx_done")
        ex_done, rank_done, rk_done, both_done, counted, kept, row_done, slot_done = (
            sem(k) for k in ("ex_done", "rank_done", "rk_done", "both_done", "counted", "kept", "row_done",
                             "slot_done"))
        sent = m["sent"]
        dve_steps, pool_steps = sem("dve_steps"), sem("pool_steps")

        def count(kind, b):
            return b + 1 if kind in front else b if kind in att else b - 1

        def routed(b, k):
            return not isinstance(b, int) or 0 <= b - k < B

        def has(kind, b):
            if not isinstance(b, int):
                return True
            return 0 <= count(kind, b) - 1 < B

        ring = {"T": ["T0", "xT", "T1", "OT", "T2", "T3", "x2T"], "F": ["cT", "K", "Q", "W0", "V", "W1", "W2"]}
        where = {k: (r, i) for r, ks in ring.items() for i, k in enumerate(ks)}

        def before(kind, b):
            r, i = where[kind]
            ks, back = ring[r], 2 if r == "T" else 1
            while True:
                i -= back
                if i < 0:
                    i, b = i + len(ks), b - 1
                if has(ks[i], b) or (isinstance(b, int) and b < 0):
                    return ks[i], b

        def tbank(kind, p):
            return T[(p * len(ring["T"]) + where[kind][1]) % 2]

        pre_jobs = [("q", r) for r in range(HC)] + [("kv", r) for r in range(2)] + [("o", r) for r in range(HC)] \
            + [("g", 0)]

        block = stack.enter_context(nc.Block())

        @block.sync
        def _(sp):
            sp.dma_start(X[:, 0:2, :], x[0:2].rearrange("b p d -> p b d")).then_inc(ld_x[0], 16)
            sp.dma_start(pre[:, 0:HC, :], Wq.rearrange("(t p) n -> p t n", p=P)).then_inc(ld_wq, 16)
            sp.dma_start(prekv, Wkv.rearrange("(t p) n -> p t n", p=P)).then_inc(ld_wkv, 16)
            sp.dma_start(CTX[:, 0:1, :], ctx[0:1].rearrange("b p d -> p b d")).then_inc(ld_ctx[0], 16)
            sp.dma_start(pre[:, HC:2 * HC, :], Wout.rearrange("(t p) n -> p t n", p=P)).then_inc(ld_w, 16)
            sp.dma_start(preg, Wg).then_inc(ld_w, 16)
            sp.dma_start(brow[:], bias.rearrange("(a n) -> a n", a=1).broadcast_to([P, E])).then_inc(ld_w, 16)
            sp.dma_start(CTX[:, 1:B, :], ctx[1:B].rearrange("b p d -> p b d")).then_inc(ld_ctx[1], 16)
            sp.dma_start(X[:, 2:B, :], x[2:B].rearrange("b p d -> p b d")).then_inc(ld_x[1], 16)

            def body(b, p, j):
                e, e_half = j - 1 + p, 1 - p
                if has("W0", b):
                    need(sp, ready["W2"], b - 1)
                    rows = slice(e_half * P, (e_half + 1) * P)
                    if isinstance(e, int):
                        w1, w3, w2 = W1[e], W3[e], W2[e]
                    else:
                        w1, w3, w2 = (w[bass.ds(e, 1)].rearrange("o a b -> (o a) b") for w in (W1, W3, W2))
                    sp.dma_start(wn[:, 0, :], w1[rows, :]).then_inc(ld_stage, 16)
                    sp.dma_start(wn[:, 1, :], w3[rows, :]).then_inc(ld_stage, 16)
                    sp.dma_start(wn[:, 2, :].rearrange("p (t n) -> p t n", n=P),
                                 w2[:, rows].rearrange("(t p) n -> p t n", p=P)).then_inc(ld_stage, 16)
                if has("xT", b):
                    need(sp, abs_done, b)
                    gf = gate_w.rearrange("(p a) b -> p (a b)", p=P)
                    df = down_w.rearrange("(p a) b -> p (a b)", p=P)
                    sp.dma_start(absn[:, 0:GATE_ABS], gf[:, bass.ds(b * GATE_ABS, GATE_ABS)]).then_inc(ld_abs, 16)
                    sp.dma_start(absn[:, GATE_ABS:], df[:, bass.ds(b * DOWN_ABS, DOWN_ABS)]).then_inc(ld_abs, 16)
                if isinstance(b, int) and b == 1:
                    sp.wait_ge(zeroed, 1)
                    sp.dma_start(slots_in[ZERO_ROW:ZERO_ROW + P, :], zero).then_inc(filled, 16)

            bodies(sp, NB, body, head=2, tail=3)
            sp.wait_ge(filled, 16)

        @block.gpsimd
        def _(pool):
            step = Steps(pool, pool_steps)
            step.then(pool.memset(ident[:], 0.0))
            pool.affine_select(out=ident[:], in_=ident[:], compare_op=ALU.not_equal, fill=1.0, base=0,
                               pattern=[[-1, P]], channel_multiplier=1).then_inc(consts, 1)
            step.then(pool.memset(mask4[:], 0.0))
            pool.affine_select(out=mask4[:], in_=mask4[:], compare_op=ALU.is_ge, fill=NEG, base=0,
                               pattern=[[0, HG], [-1, P]], channel_multiplier=1).then_inc(consts, 1)
            pool.memset(half[:], -0.5).then_inc(consts, 1)
            pool.memset(V[:, :, :, HD0:HD0 + 1], 1.0).then_inc(consts, 1)
            pool.memset(ones[:], 1.0).then_inc(consts, 1)
            pool.memset(zero, 0.0).then_inc(zeroed, 1)
            pool.wait_ge(consts, 5)
            pool.tensor_copy(identb[:], ident[:]).then_inc(consts, 1)
            pool.memset(onesb[:], 1.0).then_inc(consts, 1)
            pool.memset(cum[:], 0.0).then_inc(consts, 1)
            pool.wait_ge(consts, 8)
            pool.affine_select(out=tri[:], in_=onesb[:], compare_op=ALU.is_ge, fill=0.0, base=-1,
                               pattern=[[1, P]], channel_multiplier=-1).then_inc(consts, 1)
            pool.wait_ge(consts, 9)

            def front(b):
                need(pool, ready["cT"], b, True)
                pool.tensor_copy(cx[:], at(CTX, b)).then_inc(cx_done, 1)
                need(pool, stats1, b + 1, True)
                need(pool, xn_done, b, True)
                step.then(pool.tensor_scalar(rs1[:], mv1[:, 1:2], EPS, None, ALU.add))
                pool.tensor_tensor(rs1[:], rs1[:], half[:], ALU.pow).then_inc(rstd1_done, 1)

            pool.wait_ge(ld_ctx[0], 16)
            front(0)
            pool.wait_ge(ld_ctx[1], 16)
            step.loop(4)

            def body(b, p, j):
                step.body(b)
                if routed(b, 4):
                    need(pool, rk_done, b - 3, True)
                    pool.tensor_tensor(cum[:], cum[:], both[:], ALU.add).then_inc(counted, 1)
                    need(pool, row_done, b - 3, True)
                    need(pool, sent[p], 32 * (j - 2), True)
                    step.then(pool.tensor_copy(slot[:, p, :], rowf[:]))
                    for c in range(2):
                        pool.indirect_dma_start(out=slots_in, out_offset=bass.IndirectOffsetOnAxis(
                            ap=slot[:, p, c:c + 1], axis=0), in_=xn2[:, p, :], in_offset=None).then_inc(sent[p], 16)
                    pool.tensor_copy(m["row_in"][:, :, bass.ds(b - 4, 1)].rearrange("p c o -> p (c o)"), rowf[:]
                                     ).then_inc(slot_done, 1)
                if has("xT", b + 1):
                    front(b + 1)
                if has("OT", b):
                    need(pool, stats2, b - 1, True)
                    need(pool, xn2_done, b - 2, True)
                    step.then(pool.tensor_scalar(rs2[:], mv2[:, 1:2], EPS, None, ALU.add))
                    pool.tensor_tensor(rs2[:], rs2[:], half[:], ALU.pow).then_inc(rstd2_done, 1)
                if routed(b, 3):
                    need(pool, both_done, b - 2, True)
                    pool.tensor_copy(m["pick"][:, :, bass.ds(b - 3, 1), :].rearrange("p c o e -> p c (o e)"), pk[:]
                                     ).then_inc(kept, 1)
                    pool.tensor_copy(at(m["prob"], b - 3), pr[:]).then_inc(kept, 1)
                step.end()

            bodies(pool, NB, body, head=2, tail=3)
            for q in range(2):
                pool.wait_ge(sent[q], 32 * B // 2)

        @block.tensor
        def _(pe):
            pe.wait_ge(consts, 9)
            for n, (kind, r) in enumerate(pre_jobs):
                if r == 0 and kind != "g":
                    pe.wait_ge(*{"q": (ld_wq, 16), "kv": (ld_wkv, 16), "o": (ld_w, 48)}[kind])
                if n >= 2:
                    pe.wait_ge(pre_e, n - 1)
                bk = T[n % 2]
                if kind == "g":
                    for c in range(HC):
                        last = pe.transpose(bk[:, c * E:(c + 1) * E], preg[:, c * P:(c + 1) * P], ident[0:E, 0:E])
                else:
                    for c in range(4):
                        src = (pre[:, r, c * P:(c + 1) * P] if kind == "q" else prekv[:, 4 * r + c, :] if kind == "kv"
                               else pre[:, HC + r, c * P:(c + 1) * P])
                        last = pe.transpose(bk[:, c * P:(c + 1) * P], src, ident[:])
                last.then_inc(pre_t, 1)
            pe.wait_ge(pre_e, len(pre_jobs))

            def free(kind, b):
                k, bb = before(kind, b)
                need(pe, evac[k], count(k, bb))

            def scores(b, p, g):
                q = 1 - p
                n = 4 * b - 4 + g
                need(pe, s_sub, n - 1)
                if g == 0:
                    pe.wait_ge(evac["Q"], b)
                    pe.wait_ge(evac["K"], b)
                bk, rows = S[g % 2], slice(HD0 * g, HD0 * (g + 1))
                pe.matmul(bk[:], identb[:], mask4[:].rearrange("p a b -> p (a b)"), start=True, stop=False)
                for c in range(HG):
                    last = pe.matmul(bk[:, c * P:(c + 1) * P], qT[rows, q, c, :], kT[rows, q, c, :],
                                     start=False, stop=(c == HG - 1), tile_position=(HD0 * g, 0))
                last.then_inc(s_done, 1)

            def probs_t(b, p, g):
                pe.wait_ge(s_exp, 4 * b - 3 + g)
                free(f"T{g}", b)
                bk = tbank(f"T{g}", p)
                for j in range(HG):
                    last = pe.transpose(bk[:, j * P:(j + 1) * P], D[:, g % 2, j, :], ident[:])
                last.then_inc(ready[f"T{g}"], 1)

            def pv(b, p, g):
                q = 1 - p
                pe.wait_ge(evac[f"T{g}"], b)
                if g == 0:
                    pe.wait_ge(evac["V"], b)
                if g % 2 == 0:
                    need(pe, o_done, 2 * b - 3 + g // 2)
                for j in range(HG):
                    c = (4 * (g % 2) + j) * (HD0 + 1)
                    last = pe.matmul(O[g // 2][:, c:c + HD0 + 1], PT[:, g % 2, j, :], V[:, q, 4 * j + g, :],
                                     start=True, stop=True)
                last.then_inc(pv_done, 1)

            def four(kind, b, p, src, wait, value):
                need(pe, wait, value)
                free(kind, b)
                bk = tbank(kind, p)
                for c in range(HC):
                    last = pe.transpose(bk[:, c * P:(c + 1) * P], src[:, c * P:(c + 1) * P], ident[:])
                last.then_inc(ready[kind], 1)

            def weights(b, p, j, k):
                if k == 0:
                    pe.wait_ge(ld_stage, 48 * b)
                free(f"W{k}", b)
                for c in range(4):
                    last = pe.transpose(Fb[:, c * P:(c + 1) * P], wn[:, k, c * P:(c + 1) * P], ident[:])
                last.then_inc(ready[f"W{k}"], 1)

            def body(b, p, j):
                a, f, t = has("T0", b), has("xT", b), has("OT", b)
                if a:
                    scores(b, p, 2)
                    probs_t(b, p, 0)
                if f:
                    four("xT", b, p, xn, xn_done, b + 1)
                    pe.wait_ge(cx_done, b + 1)
                    free("cT", b)
                    pe.transpose(Fb[:, 0:P], cx[:], ident[:]).then_inc(ready["cT"], 1)
                if a:
                    scores(b, p, 3)
                    pv(b, p, 0)
                    probs_t(b, p, 1)
                if f:
                    pe.wait_ge(evac["cT"], b + 1)
                    for g in range(HC):
                        last = pe.matmul(Fb[:, g * P:(g + 1) * P], WkvT[:, g * P:(g + 1) * P], ctxT[:],
                                         start=True, stop=True)
                    last.then_inc(ready["K"], 1)
                if t:
                    four("OT", b, p, On, o_done, 2 * b - 2)
                if a:
                    pv(b, p, 1)
                    probs_t(b, p, 2)
                if f:
                    pe.wait_ge(evac["xT"], b + 1)
                    free("Q", b)
                    for g in range(HC):
                        for c in range(HC):
                            last = pe.matmul(Fb[:, g * P:(g + 1) * P], WqT[:, c, g * P:(g + 1) * P], xT[:, c, :],
                                             start=(c == 0), stop=(c == HC - 1))
                    last.then_inc(ready["Q"], 1)
                if t:
                    pe.wait_ge(evac["OT"], b - 1)
                    need(pe, ex_done, b - 2)
                    need(pe, rk_done, b - 3)
                    for c in range(HC):
                        last = pe.matmul(Dk[:], OT[:, c, :], WoutT[:, c, :], start=(c == 0), stop=(c == HC - 1))
                    last.then_inc(y_done, 1)
                if a:
                    pv(b, p, 2)
                    probs_t(b, p, 3)
                    weights(b, p, j, 0)
                if f:
                    scores(b + 1, 1 - p, 0)
                    scores(b + 1, 1 - p, 1)
                    free("V", b)
                    pe.matmul(Fb[:], ctxT[:], WkvT[:, H:2 * H], start=True, stop=True).then_inc(ready["V"], 1)
                if t:
                    four("x2T", b, p, xn2[:, p, :], xn2_done, b - 1)
                if a:
                    pv(b, p, 3)
                    weights(b, p, j, 1)
                if routed(b, 3):
                    if t:
                        pe.wait_ge(x2_done, b - 1)
                    else:
                        pe.wait_ge(ex_done, b - 2)
                        pe.wait_ge(rk_done, b - 3)
                    pe.wait_ge(both_done, b - 2)
                    need(pe, counted, b - 3)
                    pe.matmul(Dk[:, RANK:RANK + E], tri[:], both[:], start=True, stop=False)
                    pe.matmul(Dk[:, RANK:RANK + E], onesb[:], cum[:], start=False, stop=True).then_inc(rank_done, 1)
                if t:
                    pe.wait_ge(evac["x2T"], b - 1)
                    pe.wait_ge(x2_done, b - 1)
                    for c in range(HC):
                        last = pe.matmul(Dk[:, 0:E], x2T[:, c, :], WgT[:, c, :], start=(c == 0), stop=(c == HC - 1))
                    last.then_inc(r_done, 1)
                if a:
                    weights(b, p, j, 2)

            bodies(pe, NB, body, head=2, tail=3)

        @block.scalar
        def _(act):
            for n, (kind, r) in enumerate(pre_jobs):
                act.wait_ge(pre_t, n + 1)
                bk = T[n % 2]
                if kind == "g":
                    dst, src = WgT[:], bk[:, 0:HC * E].rearrange("p (c e) -> p c e", c=HC)
                elif kind == "kv":
                    dst, src = WkvT[:, 4 * P * r:4 * P * (r + 1)], bk[:]
                else:
                    dst = (WqT if kind == "q" else WoutT)[:, :, r * P:(r + 1) * P]
                    src = bk[:].rearrange("p (c f) -> p c f", c=HC)
                act.copy(dst, src).then_inc(pre_e, 1)

            def take(kind, b, dst, src):
                act.wait_ge(ready[kind], count(kind, b))
                act.copy(dst, src).then_inc(evac[kind], 1)

            def chunked(bk):
                return bk[:].rearrange("p (c n) -> p c n", c=4)

            def exps(b, g):
                n = 4 * b - 4 + g
                act.wait_ge(s_sub, n + 1)
                act.activation(D[:, g % 2], D[:, g % 2], ACT.Exp, scale=SCALE).then_inc(s_exp, 1)

            def take_probs(b, p, g):
                n = 4 * b - 4 + g
                need(act, pv_done, n - 1)
                take(f"T{g}", b, PT[:, g % 2], chunked(tbank(f"T{g}", p)))

            def weights(b, p, j, k):
                e, half_e = j - 1 + p, 1 - p
                if k == 2 and isinstance(b, int) and b == B:
                    act.wait_ge(filled, 16)
                if k < 2:
                    lo = k * FF + half_e * P
                    take(f"W{k}", b, at(W13T, e, slice(None), slice(lo, lo + P)), chunked(Fb))
                else:
                    take("W2", b, at(W2T, e, half_e), Fb[:])

            def body(b, p, j):
                a, f, t = has("T0", b), has("xT", b), has("OT", b)
                q = 1 - p
                if a:
                    take_probs(b, p, 0)
                if f:
                    need(act, ready["Q"], b)
                    take("xT", b, xT[:], chunked(tbank("xT", p)))
                    need(act, ready["V"], b)
                    take("cT", b, ctxT[:], Fb[:, 0:P])
                if a:
                    exps(b, 2)
                    take_probs(b, p, 1)
                if f:
                    take("K", b, kT[:, p], chunked(Fb))
                if a:
                    exps(b, 3)
                if t:
                    need(act, y_done, b - 2)
                    take("OT", b, OT, chunked(tbank("OT", p)))
                if a:
                    take_probs(b, p, 2)
                if f:
                    take("Q", b, qT[:, p], chunked(Fb))
                if a:
                    take_probs(b, p, 3)
                    weights(b, p, j, 0)
                if f:
                    exps(b + 1, 0)
                    need(act, pv_done, 4 * b - 4)
                    take("V", b, V[:, p, :, 0:HD0], Fb[:].rearrange("p (h d) -> p h d", h=NH0))
                if t:
                    need(act, r_done, b - 2)
                    take("x2T", b, x2T[:], chunked(tbank("x2T", p)))
                if f:
                    exps(b + 1, 1)
                if a:
                    weights(b, p, j, 1)
                if t:
                    act.wait_ge(r_done, b - 1)
                if routed(b, 3):
                    act.wait_ge(rank_done, b - 2)
                    need(act, row_done, b - 3)
                    act.copy(rk[:], Dk[:, RANK:RANK + E]).then_inc(rk_done, 1)
                if t:
                    need(act, both_done, b - 2)
                    act.activation(ex[:], Dk[:, 0:E], ACT.Exp, scale=-1.0).then_inc(ex_done, 1)
                if a:
                    weights(b, p, j, 2)

            bodies(act, NB, body, head=2, tail=3)

        @block.vector
        def _(dve):
            step = Steps(dve, dve_steps, alone=True)

            def ln_stats(src, dst, k, signal):
                step.then(dve.bn_stats(st[:, k, :], src))
                dve.bn_aggr(dst, st[:, k, :]).then_inc(signal, 1)

            def normalise(dst, src, mv, rs, signal):
                dve.tensor_scalar(dst, src, mv[:, 0:1], rs[:], ALU.subtract, ALU.mult).then_inc(signal, 1)

            def softmax_head(b, g):
                n = 4 * b - 4 + g
                dve.wait_ge(s_done, n + 1)
                bk = S[g % 2][:].rearrange("p (h k) -> p h k", h=HG)
                dve.tensor_reduce(mx[:, g % 2, :], bk, AX.X, ALU.max).then_inc(s_max, 1)
                dve.wait_ge(s_max, n + 1)
                if g >= 2:
                    dve.wait_ge(ready[f"T{g - 2}"], b)
                else:
                    need(dve, ready[f"T{g + 2}"], b - 1)
                dve.tensor_tensor(D[:, g % 2], bk, mx[:, g % 2, :, None].broadcast_to([P, HG, P]),
                                  ALU.subtract).then_inc(s_sub, 1)

            def out_half(b, p, k):
                q = 1 - p
                dve.wait_ge(pv_done, 4 * b - 4 + 2 * k + 2)
                bk = O[k][:, 0:8 * (HD0 + 1)].rearrange("p (h d) -> p h d", h=8)
                step.then(dve.reciprocal(rden[:, k, :], bk[:, :, HD0]))
                need(dve, ready["OT"], b - 1)
                four = "p (g c) d -> p g c d"
                rd = rden[:, k, :, None].broadcast_to([P, 8, HD0])
                dve.tensor_tensor(On.rearrange("p (c g d) -> p g c d", g=HG, d=HD0)[:, 2 * k:2 * k + 2],
                                  bk[:, :, 0:HD0].rearrange(four, g=2), rd.rearrange(four, g=2),
                                  ALU.mult).then_inc(o_done, 1)

            def front(b):
                if isinstance(b, int) and b < 2:
                    dve.wait_ge(ld_x[b], 16)
                ln_stats(at(X, b), mv1[:], 0, stats1)

            def front_norm(b):
                need(dve, rstd1_done, b + 1)
                need(dve, ready["xT"], b)
                normalise(xn[:], at(X, b), mv1, rs1, xn_done)

            front(0)
            front_norm(0)
            dve.wait_ge(consts, 9)
            step.then(dve.tensor_tensor_scan(iota[:], ones[:, 0:SLOT_TILES], ones[:, 0:SLOT_TILES], -1.0,
                                             ALU.mult, ALU.add))
            step.then(dve.tensor_scalar(ebase[:], iota[:, 0:E], float(REGION), None, ALU.mult))
            dve.tensor_scalar(order[:], iota[:, 0:E], -1.0, float(E), ALU.mult, ALU.add).then_inc(consts_dve, 1)
            dve.wait_ge(ld_w, 48)
            step.loop(19)

            def pick(c):
                step.then(dve.tensor_reduce(best[:], score[:], AX.X, ALU.max))
                step.then(dve.scalar_tensor_tensor(mark[:], score[:], best[:], order[:], ALU.is_ge, ALU.mult))
                step.then(dve.tensor_reduce(best[:], mark[:], AX.X, ALU.max))
                step.then(dve.tensor_scalar(pk[:, c, :], mark[:], best[:], None, ALU.is_equal))

            def body(b, p, j):
                a, f, t, r = has("T0", b), has("xT", b), has("OT", b), routed(b, 3)
                step.body(b)
                if a:
                    softmax_head(b, 2)
                if routed(b, 4):
                    dve.wait_ge(rk_done, b - 3)
                    step.then(dve.tensor_tensor(rk[:], rk[:], ebase[:], ALU.add))
                    step.then(dve.tensor_tensor(row[:], pk[:], rk[:, None, :].broadcast_to([P, 2, E]), ALU.mult))
                    need(dve, slot_done, b - 4)
                    dve.tensor_reduce(rowf[:], row[:], AX.X, ALU.add).then_inc(row_done, 1)
                    dve.wait_ge(row_done, b - 3)
                if has("xT", b + 1):
                    need(dve, xn_done, b + 1)
                    front(b + 1)
                if r:
                    dve.wait_ge(ex_done, b - 2)
                    step.then(dve.tensor_scalar(mark[:], ex[:], 1.0, None, ALU.add))
                    need(dve, kept, 2 * (b - 3))
                    step.then(dve.reciprocal(pr[:], mark[:]))
                    step.then(dve.tensor_tensor(score[:], pr[:], brow[:], ALU.add))
                if a:
                    softmax_head(b, 3)
                if has("xT", b + 1):
                    front_norm(b + 1)
                if r:
                    pick(0)
                    step.then(dve.scalar_tensor_tensor(score[:], pk[:, 0, :], -BIG, score[:], ALU.mult, ALU.add))
                if f:
                    dve.wait_ge(ld_abs, 32 * (b + 1))
                    bb = bass.ds(b, 1)
                    step.mark(dve.tensor_reduce(m["absum"][:, 0, bb], absn[:, 0:GATE_ABS], AX.X, ALU.add,
                                                apply_absolute_value=True))
                    dve.tensor_reduce(m["absum"][:, 1, bb], absn[:, GATE_ABS:], AX.X, ALU.add,
                                      apply_absolute_value=True).then_inc(abs_done, 1)
                if a:
                    out_half(b, p, 0)
                if r:
                    pick(1)
                    need(dve, counted, b - 3)
                    dve.tensor_tensor(both[:], pk[:, 0, :], pk[:, 1, :], ALU.add).then_inc(both_done, 1)
                if t:
                    dve.wait_ge(y_done, b - 1)
                    xb = at(X, b - 2)
                    dve.tensor_tensor(xb, Dk[:], xb, ALU.add).then_inc(x2_done, 1)
                    need(dve, x2_done, b - 1, True)
                    ln_stats(xb, mv2[:], 1, stats2)
                if f:
                    softmax_head(b + 1, 0)
                if t:
                    need(dve, rstd2_done, b - 1)
                    need(dve, ready["x2T"], b - 2)
                    need(dve, sent[p], 32 * (j - 1))
                    normalise(xn2[:, p, :], xb, mv2, rs2, xn2_done)
                if f:
                    softmax_head(b + 1, 1)
                if a:
                    out_half(b, p, 1)
                step.end()

            bodies(dve, NB, body, head=2, tail=3)


def experts(nc, m, gate_w, down_w, slots_in, slots_out):
    W13T, W2T, ones = m["W13T"], m["W2T"], m["ones"]
    iota, ebase = m["iota"], m["ebase"]
    ident, identb = m["ident"], m["identb"]
    gateT = m["R"][:, 0:HC * 2 * INTER].rearrange("p (c n) -> p c n", c=HC)
    downT = m["R"][:, HC * 2 * INTER:].rearrange("p (c n) -> p c n", c=IC)
    NB = SLOT_TILES + 2
    with ExitStack() as stack:
        def sb(name, shape, dt=F32):
            return stack.enter_context(nc.sbuf_tensor("e_" + name, shape, dt))

        def sem(name):
            return m["sem"]("e_" + name)

        def bank(name, dt=F32):
            return stack.enter_context(nc.psum_tensor("e_" + name, [P, 2048 // mybir.dt.size(dt)], dt))

        tmp = sb("tmp", [P, B, E])
        den = sb("den", [P, B])
        rows = sb("rows", [P, B])
        pidx = sb("pidx", [P, 1])
        tiles = sb("tiles", [P, E])
        upto = sb("upto", [P, E])
        delta = sb("delta", [P, E])
        behind = sb("behind", [P, E])
        idx = sb("idx", [P, E], U32)
        zeros = sb("zeros", [P, H])
        over = sb("over", [1, SLOT_TILES, E])
        te = sb("te", [1, SLOT_TILES, E])
        who = sb("who", [1, SLOT_TILES])
        first = sb("first", [1, SLOT_TILES])
        start = sb("start", [1, SLOT_TILES], I32)
        which = sb("which", [1, SLOT_TILES], I32)
        asum = sb("asum", [P, 2])
        xg = sb("xg", [P, 2, H])
        y = sb("y", [P, 2, H])
        xT = sb("xT", [P, 2, HC, P])
        sg = sb("sg", [P, FF])
        g = sb("g", [P, 2, FF])
        gT = sb("gT", [P, FC, P])
        wst = sb("wst", [P, 2, H])
        wr = sb("wr", [P, H])
        wq = sb("wq", [P, 2, H], BF16)

        XB = [bank("X0"), bank("X1")]
        GB = bank("G")
        HB = [bank("H0"), bank("H1")]
        YB = [bank("Y0"), bank("Y1")]
        WB = bank("W", BF16)

        s_sum, s_cnt, s_rows, s_table, padded, steps = (
            sem(k) for k in ("sum", "cnt", "rows", "table", "padded", "steps"))
        ld_xg = [sem("ld_xg0"), sem("ld_xg1")]
        ld_wst = [sem("ld_wst0"), sem("ld_wst1")]
        x_t, x_e, h_done, silu_done, g_done, g_t, g_e, y_done, y_e = (
            sem(k) for k in ("x_t", "x_e", "h_done", "silu_done", "g_done", "g_t", "g_e", "y_done", "y_e"))
        stored = [sem("stored0"), sem("stored1")]
        wq_r, wq_m, wq_done, wq_t, wq_e = (sem(k) for k in ("wq_r", "wq_m", "wq_done", "wq_t", "wq_e"))

        def run(eng, body):
            jobs = GATE_TILES + IC
            assert GATE_TILES % 2 == 0 and jobs < SLOT_TILES
            for b in range(4):
                body(b, b % 2, b // 2, "gate")
            with eng.Fori(2, GATE_TILES // 2) as j:
                for p in range(2):
                    body(j * 2 + p, p, j, "gate")
            with eng.Fori(GATE_TILES // 2, jobs // 2) as j:
                for p in range(2):
                    body(j * 2 + p, p, j, "down")
            j = jobs // 2
            if jobs % 2:
                body(2 * j, 0, j, "down")
                body(2 * j + 1, 1, j, None)
                j += 1
            with eng.Fori(j, SLOT_TILES // 2) as j:
                for p in range(2):
                    body(j * 2 + p, p, j, None)
            for b in range(SLOT_TILES // 2 * 2, NB):
                body(b, b % 2, b // 2, None)

        def stage(b, k):
            return not isinstance(b, int) or 0 <= b - k < SLOT_TILES

        block = stack.enter_context(nc.Block())

        @block.sync
        def _(sp):
            for s in m["first"]:
                sp.sem_clear(s)

            def body(b, p, j, job):
                if job:
                    need(sp, wq_r, b - 1)
                    if job == "gate":
                        sp.dma_start(wst[:, p, :], gate_w[bass.ds(b * P, P), :]).then_inc(ld_wst[p], 16)
                    else:
                        sp.dma_start(wst[:, p, :].rearrange("p (t n) -> p t n", n=P),
                                     down_w[:, bass.ds((b - GATE_TILES) * P, P)].rearrange("(t p) n -> p t n", p=P)
                                     ).then_inc(ld_wst[p], 16)
                if stage(b, 0):
                    if isinstance(b, int) and b == 0:
                        sp.wait_ge(s_table, 2)
                        sp.wait_ge(padded, 16 * E)
                    need(sp, x_t, b - 1)
                    sp.nop(nofuse=True)
                    row = sp.value_load(start[0:1, bass.ds(b, 1)], min_val=0, max_val=ZERO_ROW)
                    sp.dma_start(xg[:, p, :], slots_in[bass.ds(row, P), :]).then_inc(ld_xg[p], 16)
                if stage(b, 3):
                    sp.wait_ge(y_e, b - 2)
                    sp.dma_start(slots_out[bass.ds((b - 3) * P, P), :], y[:, 1 - p, :]).then_inc(stored[1 - p], 16)

            run(sp, body)
            sp.wait_ge(y_e, SLOT_TILES)
            sp.dma_start(slots_out[(SLOT_TILES - 1) * P:, :], y[:, (SLOT_TILES - 1) % 2, :]
                         ).then_inc(stored[(SLOT_TILES - 1) % 2], 16)
            for p in range(2):
                sp.wait_ge(stored[p], 16 * len(range(p, SLOT_TILES, 2)))

        @block.gpsimd
        def _(pool):
            pool.memset(zeros[:], 0.0).then_inc(s_rows, 1)
            pool.wait_ge(s_rows, 2)
            for e in range(E):
                pool.indirect_dma_start(out=slots_in, out_offset=bass.IndirectOffsetOnAxis(
                    ap=idx[:, e:e + 1], axis=0), in_=zeros[:], in_offset=None).then_inc(padded, 16)
            pool.wait_ge(padded, 16 * E)

        @block.tensor
        def _(pe):
            pe.matmul(XB[1][:, 0:E], m["onesb"][:], m["cum"][:], start=True, stop=True).then_inc(s_cnt, 1)
            pe.wait_ge(s_sum, 1)
            pe.matmul(YB[0][:, 0:2], ones[:], asum[:], start=True, stop=True).then_inc(s_cnt, 1)
            pe.wait_ge(s_table, 1)

            def expert(i):
                pe.nop(nofuse=True)
                return pe.value_load(which[0:1, bass.ds(i, 1)], min_val=0, max_val=E - 1)

            def body(b, p, j, job):
                if stage(b, 2):
                    pe.wait_ge(g_done, b - 1)
                    need(pe, g_e, b - 2)
                    for c in range(FC):
                        last = pe.transpose(GB[:, c * P:(c + 1) * P], g[:, p, c * P:(c + 1) * P], ident[:])
                    last.then_inc(g_t, 1)
                if stage(b, 0):
                    pe.wait_ge(ld_xg[p], 16 * (j + 1))
                    need(pe, x_e, b - 1)
                    for c in range(HC):
                        last = pe.transpose(XB[p][:, c * P:(c + 1) * P], xg[:, p, c * P:(c + 1) * P], ident[:])
                    last.then_inc(x_t, 1)
                if stage(b, 1):
                    pe.wait_ge(x_e, b)
                    need(pe, g_done, b - 2)
                    e = expert(b - 1)
                    for c in range(HC):
                        last = pe.matmul(HB[1 - p][:], xT[:, 1 - p, c, :], at(W13T, e, c), start=(c == 0),
                                         stop=(c == HC - 1))
                    last.then_inc(h_done, 1)
                if job:
                    pe.wait_ge(wq_done, b + 1)
                    need(pe, wq_e, b)
                    for c in range(4):
                        last = pe.transpose(WB[:, c * P:(c + 1) * P], wq[:, p, c * P:(c + 1) * P], identb[:])
                    last.then_inc(wq_t, 1)
                if stage(b, 2):
                    pe.wait_ge(g_e, b - 1)
                    need(pe, y_e, b - 2)
                    e = expert(b - 2)
                    for c in range(FC):
                        last = pe.matmul(YB[p][:], gT[:, c, :], at(W2T, e, c), start=(c == 0), stop=(c == FC - 1))
                    last.then_inc(y_done, 1)

            run(pe, body)

        @block.scalar
        def _(act):
            def body(b, p, j, job):
                if stage(b, 2):
                    act.wait_ge(g_t, b - 1)
                    need(act, y_done, b - 2)
                    act.copy(gT[:], GB[:, 0:FF].rearrange("p (c n) -> p c n", c=FC)).then_inc(g_e, 1)
                if stage(b, 0):
                    act.wait_ge(x_t, b + 1)
                    need(act, h_done, b - 1)
                    act.copy(xT[:, p], XB[p][:].rearrange("p (c n) -> p c n", c=HC)).then_inc(x_e, 1)
                if stage(b, 1):
                    act.wait_ge(h_done, b)
                    need(act, g_done, b - 1)
                    act.activation(sg[:], HB[1 - p][:, 0:FF], ACT.Silu).then_inc(silu_done, 1)
                if job:
                    act.wait_ge(wq_t, b + 1)
                    src = WB[:, 0:H]
                    if job == "gate":
                        act.copy(gateT[:, :, bass.ds(b * P, P)], src.rearrange("p (c n) -> p c n", c=HC)).then_inc(wq_e, 1)
                    else:
                        act.copy(at(downT, b - GATE_TILES), src).then_inc(wq_e, 1)

            run(act, body)

        @block.vector
        def _(dve):
            step = Steps(dve, steps)
            then = step.then
            dve.tensor_reduce(asum[:], m["absum"][:], AX.X, ALU.add).then_inc(s_sum, 1)
            then(dve.tensor_reduce(pidx[:], m["tri"][:], AX.X, ALU.add))
            then(dve.tensor_scalar(pidx[:], pidx[:], -1.0, float(P - 1), ALU.mult, ALU.add))
            dve.wait_ge(s_cnt, 1)
            then(dve.tensor_tensor(behind[:], XB[1][:, 0:E], ebase[:], ALU.add))
            dve.tensor_scalar(idx[:], behind[:], pidx[:], None, ALU.add).then_inc(s_rows, 1)
            then(dve.tensor_scalar(tiles[:], XB[1][:, 0:E], P / 2 - 0.5, 1.0 / P, ALU.add, ALU.mult))
            then(dve.tensor_scalar(tiles[:], tiles[:], ROUND, -ROUND, ALU.add, ALU.add))
            then(dve.tensor_tensor_scan(upto[:], ones[:, 0:E], tiles[:], 0.0, ALU.mult, ALU.add))

            def over_tiles(t):
                return t[0:1, None, :].broadcast_to([1, SLOT_TILES, E])

            then(dve.tensor_tensor(over[:], over_tiles(upto), iota[0:1, :, None].broadcast_to([1, SLOT_TILES, E]),
                                   ALU.is_le))
            step.mark(dve.tensor_reduce(who[:], over[:], AX.X, ALU.add))
            then(dve.tensor_tensor(te[:], over[:], over_tiles(tiles), ALU.mult))
            dve.tensor_scalar(which[:], who[:], float(E - 1), None, ALU.min).then_inc(s_table, 1)
            then(dve.tensor_reduce(first[:], te[:], AX.X, ALU.add))
            then(dve.tensor_tensor(first[:], iota[0:1, :], first[:], ALU.subtract))
            then(dve.tensor_scalar(who[:], who[:], float(REGION), None, ALU.mult))
            then(dve.scalar_tensor_tensor(first[:], first[:], float(P), who[:], ALU.mult, ALU.add))
            dve.tensor_scalar(start[:], first[:], float(ZERO_ROW), None, ALU.min).then_inc(s_table, 1)
            dve.wait_ge(s_cnt, 2)
            for k, n in enumerate((2 * INTER * H, INTER * H)):
                step.mark(dve.tensor_scalar(m["wmean"][:, k:k + 1], YB[0][:, k:k + 1], 1.0 / n, 1e-5, ALU.mult, ALU.max))
            dve.wait_ge(steps, step.n)
            then(dve.reciprocal(m["wscale"][:], m["wmean"][:]))
            then(dve.tensor_tensor(delta[:], upto[:], tiles[:], ALU.subtract))
            then(dve.scalar_tensor_tensor(delta[:], delta[:], float(P), ebase[:], ALU.mult, ALU.subtract))
            for c in range(2):
                then(dve.tensor_tensor(tmp[:], m["pick"][:, c], delta[:, None, :].broadcast_to([P, B, E]), ALU.mult))
                then(dve.tensor_reduce(rows[:], tmp[:], AX.X, ALU.add))
                then(dve.tensor_tensor(m["pos"][:, c, :], rows[:], m["row_in"][:, c, :], ALU.add))
                then(dve.tensor_tensor(tmp[:], m["prob"][:], m["pick"][:, c], ALU.mult))
                then(dve.tensor_reduce(m["wt"][:, c, :], tmp[:], AX.X, ALU.add))
            then(dve.tensor_tensor(den[:], m["wt"][:, 0, :], m["wt"][:, 1, :], ALU.add))
            then(dve.reciprocal(den[:], den[:]))
            then(dve.tensor_tensor(m["wt"][:], m["wt"][:], den[:, None, :].broadcast_to([P, 2, B]), ALU.mult))

            def body(b, p, j, job):
                if job:
                    k = 0 if job == "gate" else 1
                    dve.wait_ge(ld_wst[p], 16 * (j + 1))
                    need(dve, wq_done, b)
                    dve.tensor_scalar(wr[:], wst[:, p, :], m["wscale"][:, k:k + 1], ROUND, ALU.mult,
                                      ALU.add).then_inc(wq_r, 1)
                    dve.wait_ge(wq_r, b + 1)
                    need(dve, wq_t, b - 1)
                    dve.tensor_scalar(wr[:], wr[:], -ROUND, 1.0, ALU.add, ALU.min).then_inc(wq_m, 1)
                    dve.wait_ge(wq_m, b + 1)
                    dve.tensor_scalar(wq[:, p, :], wr[:], -1.0, None, ALU.max).then_inc(wq_done, 1)
                if stage(b, 1):
                    dve.wait_ge(silu_done, b)
                    need(dve, g_t, b - 2)
                    dve.tensor_tensor(g[:, 1 - p, :], HB[1 - p][:, FF:2 * FF], sg[:], ALU.mult).then_inc(g_done, 1)
                if stage(b, 2):
                    dve.wait_ge(y_done, b - 1)
                    need(dve, stored[p], 16 * (j - 1))
                    dve.tensor_copy(y[:, p, :], YB[p][:]).then_inc(y_e, 1)

            run(dve, body)


def layer1(nc, m, slots_out, gnorm, dnorm, out):
    X, CTX, ident, identb, half = m["X"], m["CTX"], m["ident"], m["identb"], m["half"]
    gateT = m["R"][:, 0:HC * 2 * INTER].rearrange("p (c n) -> p c n", c=HC)
    downT = m["R"][:, HC * 2 * INTER:].rearrange("p (c n) -> p c n", c=IC)
    SCALE = float(HD1) ** -0.5
    NB = B + 4
    SLOT = 32
    HV = HD1 + 1
    OH = QH // 2
    with ExitStack() as stack:
        def sb(name, shape, dt=F32):
            return stack.enter_context(nc.sbuf_tensor("c_" + name, shape, dt))

        def sem(name):
            return m["sem"]("c_" + name)

        def bank(name):
            return stack.enter_context(nc.psum_tensor("c_" + name, [P, 512], F32))

        g1 = sb("g1", [P, H])
        g2 = sb("g2", [P, INTER])
        nround = sb("nround", [P, 1])
        yg = sb("yg", [P, 2, 2, H])
        slot = sb("slot", [P, 2, 2], U32)
        xn = sb("xn", [P, GROUP, KVH, SLOT])
        qT = sb("qT", [P, 2, GROUP, 2, P])
        kT = sb("kT", [P, 2, 2, P])
        V = sb("V", [P, 2, KVH, SLOT])
        D = sb("D", [P, 2, HG, P])
        mx = sb("mx", [P, 2, HG])
        PB = sb("PB", [P, 2, HG, P])
        PT = sb("PT", [P, 2, HG, P])
        On = sb("On", [P, H])
        rden = sb("rden", [P, 2, OH])
        st = sb("st", [P, 2, 6])
        mv3 = sb("mv3", [P, 2])
        rs3 = sb("rs3", [P, 2])
        mv4 = sb("mv4", [P, 2])
        nrm = sb("nrm", [P, 4])
        t1 = sb("t1", [P, H])
        am = sb("am", [P, 4])
        mq = sb("mq", [P, 1])
        dqg = sb("dqg", [P, 2, 2])
        xq = sb("xq", [P, H], BF16)
        xqT = sb("xqT", [P, HC, P], BF16)
        th = sb("th", [P, H])
        ga = sb("ga", [P, H])
        h = sb("h", [P, INTER])
        hg = sb("hg", [P, INTER])
        junk = sb("junk", [P, INTER], BF16)
        ss = sb("ss", [P, 1])
        hn = sb("hn", [P, 4])
        ah = sb("ah", [P, 4])
        hm = sb("hm", [P, 3])
        dqd = sb("dqd", [P, 2])
        hq = sb("hq", [P, INTER], BF16)
        hT = sb("hT", [P, IC, P], BF16)
        xo = sb("xo", [P, 2, H])

        S = [bank("S0"), bank("S1")]
        T = [bank("T0"), bank("T1")]
        O = [bank("O0"), bank("O1")]
        GB, UB = bank("G"), bank("U")

        ld_g = sem("ld_g")
        gathered = [sem("gathered0"), sem("gathered1")]
        stored = [sem("stored0"), sem("stored1")]
        kinds = ["T0", "T1", "kT", "q0", "T2", "q1", "xqT", "T3", "T4", "hTa", "T5", "hTb", "T6", "T7"]
        delay = {k: 1 for k in kinds}
        delay.update(hTa=3, hTb=3, xqT=2, q0=0, q1=0, kT=0)
        ready = {k: sem("ready_" + k) for k in kinds}
        evac = {k: sem("evac_" + k) for k in kinds}
        s_done, s_max, s_sub, s_exp, pv_done, o_done = (
            sem(k) for k in ("s_done", "s_max", "s_sub", "s_exp", "pv_done", "o_done"))
        slot_set = sem("slot_set")
        v_set, x3_a, x3_done, stats3, rs3_done, xn_done, v_done = (
            sem(k) for k in ("v_set", "x3_a", "x3_done", "stats3", "rs3_done", "xn_done", "v_done"))
        x4_done, stats4, nrm_done, mq_done, xq_done = (
            sem(k) for k in ("x4_done", "stats4", "nrm_done", "mq_done", "xq_done"))
        g_done, u_done, th_done, ga_done, h_done = (sem(k) for k in ("g_done", "u_done", "th_done", "ga_done", "h_done"))
        ss_done, hm_done, hg_done, hn_done, mh_done, hr_done, hq_done, down_done, out_done = (
            sem(k) for k in ("ss_done", "hm_done", "hg_done", "hn_done", "mh_done", "hr_done", "hq_done", "down_done", "out_done"))
        dve_steps, pool_steps = sem("dve_steps"), sem("pool_steps")

        def stage(b, k):
            return not isinstance(b, int) or 0 <= b - k < B

        def before(kind, b):
            i = kinds.index(kind)
            while True:
                i -= 2
                if i < 0:
                    i, b = i + len(kinds), b - 1
                if stage(b, delay[kinds[i]]) or (isinstance(b, int) and b < 0):
                    return kinds[i], b

        def tbank(kind):
            return T[kinds.index(kind) % 2]

        block = stack.enter_context(nc.Block())

        @block.sync
        def _(sp):
            sp.wait_ge(gathered[0], 32)
            sp.dma_start(g1[:], gnorm.rearrange("(a n) -> a n", a=1).broadcast_to([P, H])).then_inc(ld_g, 16)
            sp.dma_start(g2[:], dnorm.rearrange("(a n) -> a n", a=1).broadcast_to([P, INTER])).then_inc(ld_g, 16)

            def body(b, p, j):
                if stage(b, 4):
                    sp.wait_ge(out_done, b - 3)
                    sp.dma_start(out[bass.ds(b - 4, 1)].rearrange("o p d -> (o p) d"), xo[:, p, :]
                                 ).then_inc(stored[p], 16)

            bodies(sp, NB, body, head=2, tail=3)
            for p in range(2):
                sp.wait_ge(stored[p], 16 * B // 2)

        @block.gpsimd
        def _(pool):
            step = Steps(pool, pool_steps, alone=True)

            def gather(b, p):
                need(pool, x3_done, b - 1, True)
                pool.tensor_copy(slot[:, p, :], m["pos"][:, :, bass.ds(b, 1)].rearrange("p c o -> p (c o)")
                                 ).then_inc(slot_set, 1)
                need(pool, slot_set, b + 1, True)
                for c in range(2):
                    pool.indirect_dma_start(out=yg[:, p, c, :], out_offset=None, in_=slots_out,
                                            in_offset=bass.IndirectOffsetOnAxis(
                                                ap=slot[:, p, c:c + 1], axis=0)).then_inc(gathered[p], 16)

            def residual(b, k):
                need(pool, o_done, 2 * b - 1 + k, True)
                xb = X[:, b - 1, k * 256:(k + 1) * 256] if isinstance(b, int) else (
                    X[:, bass.ds(b - 1, 1), k * 256:(k + 1) * 256].rearrange("p o n -> p (o n)"))
                pool.tensor_tensor(xb, xb, On[:, k * 256:(k + 1) * 256], ALU.add).then_inc(x4_done, 1)

            def weighted(b, n):
                lo, size = CHUNKS[n]
                need(pool, h_done, 3 * (b - 2) + n + 1, True)
                if n == 0:
                    need(pool, hq_done, b - 2, True)
                pool.tensor_tensor(hg[:, lo:lo + size], h[:, lo:lo + size], g2[:, lo:lo + size],
                                   ALU.mult).then_inc(hg_done, 1)

            gather(0, 0)
            pool.memset(nround[:], -ROUND).then_inc(v_set, 1)
            pool.memset(V[:], 0.0).then_inc(v_set, 1)
            pool.memset(xn[:], 0.0).then_inc(v_set, 1)
            pool.wait_ge(v_set, 3)
            pool.memset(V[:, :, :, HD1:HV], 1.0).then_inc(v_set, 1)
            pool.wait_ge(v_set, 4)

            def front(b):
                need(pool, stats3, b + 1, True)
                need(pool, xn_done, b, True)
                step.then(pool.tensor_scalar(rs3[:, 0:1], mv3[:, 1:2], EPS, None, ALU.add))
                step.then(pool.tensor_tensor(rs3[:, 0:1], rs3[:, 0:1], half[:], ALU.pow))
                pool.tensor_scalar(rs3[:, 1:2], mv3[:, 0:1], rs3[:, 0:1], -1.0, ALU.mult, ALU.mult
                                   ).then_inc(rs3_done, 1)

            front(0)
            step.loop(12)

            def body(b, p, j):
                f, a, u, d, e = (stage(b, k) for k in range(5))
                step.body(b)
                if f:
                    need(pool, pv_done, 8 * b - 8, True)
                    pool.tensor_copy(V[:, p, :, 0:HD1],
                                     at(CTX, b).rearrange("p (k d) -> p k d", d=HD1)).then_inc(v_done, 1)
                if d:
                    c2, v2, r2, f2 = (hn[:, k:k + 1] for k in range(4))
                    need(pool, mh_done, b - 3, True)
                    step.then(pool.tensor_tensor(c2, dqg[:, 1 - p, 0:1], dqg[:, 1 - p, 1:2], ALU.mult))
                    step.then(pool.tensor_tensor(v2, c2, c2, ALU.mult))
                if u:
                    need(pool, stats4, b - 1, True)
                    need(pool, mq_done, b - 2, True)
                    r, v, f3, g = (nrm[:, k:k + 1] for k in range(4))
                    step.then(pool.tensor_scalar(v, mv4[:, 1:2], EPS, None, ALU.add))
                    step.then(pool.tensor_tensor(r, v, half[:], ALU.pow))
                    step.then(pool.tensor_tensor(f3, r, r, ALU.mult))
                    step.then(pool.tensor_scalar(f3, f3, mv4[:, 1:2], EPS, ALU.mult, ALU.add))
                    step.then(pool.tensor_tensor(f3, f3, half[:], ALU.pow))
                    pool.tensor_tensor(g, r, f3, ALU.mult).then_inc(nrm_done, 1)
                if d:
                    need(pool, ss_done, b - 2, True)
                    step.then(pool.tensor_scalar(v2, v2, ss[:], 1.0 / INTER, ALU.mult, ALU.mult))
                    step.then(pool.tensor_scalar(v2, v2, EPS, None, ALU.add))
                    step.then(pool.tensor_tensor(r2, v2, half[:], ALU.pow))
                    pool.tensor_tensor(f2, r2, c2, ALU.mult).then_inc(hn_done, 1)
                if d:
                    need(pool, mh_done, b - 2, True)
                    pool.tensor_scalar(hg[:], hg[:], ah[:, 2:3], ROUND, ALU.mult, ALU.add).then_inc(hr_done, 1)
                if stage(b + 1, 0):
                    gather(b + 1, 1 - p)
                if u:
                    weighted(b, 0)
                if a:
                    residual(b, 0)
                if u:
                    weighted(b, 1)
                if stage(b + 1, 0):
                    front(b + 1)
                if u:
                    weighted(b, 2)
                if a:
                    residual(b, 1)
                step.end()

            bodies(pool, NB, body, head=2, tail=3)

        @block.tensor
        def _(pe):
            def free(kind, b):
                k, bb = before(kind, b)
                need(pe, evac[k], bb - delay[k] + 1)

            def scores_wait(b, p, g):
                n = 8 * b - 8 + g
                need(pe, s_sub, n - 1)
                if g == 0:
                    pe.wait_ge(evac["q1"], b)
                    pe.wait_ge(evac["kT"], b)

            def score(p, g, j):
                r = SLOT * (g % 4)
                ins = pe.matmul(S[g % 2][:, j * P:(j + 1) * P], qT[r:r + HD1, 1 - p, j, g // 4, :],
                                kT[r:r + HD1, 1 - p, g // 4, :], start=True, stop=True, tile_position=(r, 0))
                if j == HG - 1:
                    ins.then_inc(s_done, 1)

            def probs_t(b, p, g):
                pe.wait_ge(s_exp, 8 * b - 7 + g)
                free(f"T{g}", b)
                for j in range(HG):
                    last = pe.transpose(tbank(f"T{g}")[:, j * P:(j + 1) * P], PB[:, g % 2, j, :], ident[:])
                last.then_inc(ready[f"T{g}"], 1)

            def pv_wait(b, g):
                pe.wait_ge(evac[f"T{g}"], b)
                if g == 0:
                    pe.wait_ge(v_done, b)
                if g % 4 == 0:
                    need(pe, o_done, 2 * b - 3 + g // 4)

            def pv(p, g, j):
                c = (HG * g + j) % OH * HV
                ins = pe.matmul(O[g // 4][:, c:c + HV], PT[:, g % 2, j, :], V[:, 1 - p, g, 0:HV],
                                start=True, stop=True)
                if j == HG - 1:
                    ins.then_inc(pv_done, 1)

            def transposes(kind, b, src, dt, idn, wait, value):
                pe.wait_ge(wait, value)
                free(kind, b)
                bk = tbank(kind)[:].bitcast(dt)
                for c, s in enumerate(src):
                    last = pe.transpose(bk[:, c * P:(c + 1) * P], s, idn[:])
                last.then_inc(ready[kind], 1)

            def gate(b, n):
                lo, size = CHUNKS[n]
                if n == 0:
                    pe.wait_ge(evac["xqT"], b - 1)
                need(pe, ga_done, 3 * (b - 2) + n)
                for c in range(HC):
                    last = pe.matmul(GB[:, 0:size], xqT[:, c, :], gateT[:, c, lo:lo + size],
                                     start=(c == 0), stop=(c == HC - 1))
                last.then_inc(g_done, 1)

            def up(b, n):
                lo, size = CHUNKS[n]
                need(pe, h_done, 3 * (b - 2) + n)
                if n == 0 and stage(b, 4):
                    pe.wait_ge(out_done, b - 3)
                for c in range(HC):
                    last = pe.matmul(UB[:, 0:size], xqT[:, c, :], gateT[:, c, INTER + lo:INTER + lo + size],
                                     start=(c == 0), stop=(c == HC - 1))
                last.then_inc(u_done, 1)

            def down(b, first, end):
                if first == 0:
                    pe.wait_ge(evac["hTb"], b - 3)
                    pe.wait_ge(h_done, 3 * (b - 2) if stage(b, 3) else 3 * B)
                    need(pe, out_done, b - 4)
                for c in range(first, end):
                    last = pe.matmul(UB[:], hT[:, c, :], downT[:, c, :], start=(c == 0), stop=(c == IC - 1))
                if end == IC:
                    last.then_inc(down_done, 1)

            def body(b, p, j):
                f, a, u, d, e = (stage(b, k) for k in range(5))

                def cols(t, lo, hi):
                    return [t[:, c * P:(c + 1) * P] for c in range(lo, hi)]

                def slot_of(g):
                    if g + 2 < KVH:
                        ahead = (b, p, g + 2) if a else None
                    else:
                        ahead = (b + 1, 1 - p, g + 2 - KVH) if f else None
                    outputs = a and g > 0
                    if ahead:
                        scores_wait(*ahead)
                    if outputs:
                        pv_wait(b, g - 1)
                    if ahead:
                        for j in range(HG):
                            score(ahead[1], ahead[2], j)
                    if outputs:
                        for j in range(HG):
                            pv(p, g - 1, j)
                    if a:
                        probs_t(b, p, g)

                xv = xn[:].rearrange("p j k d -> p (j k d)")
                slot_of(0)
                if e:
                    down(b, 0, IC // 2)
                slot_of(1)
                if f:
                    transposes("kT", b, cols(V[:, p].rearrange("p k d -> p (k d)"), 0, 2), F32, ident, v_done, b + 1)
                if e:
                    down(b, IC // 2, IC)
                if f:
                    transposes("q0", b, cols(xv, 0, 4), F32, ident, xn_done, b + 1)
                slot_of(2)
                if f:
                    transposes("q1", b, cols(xv, 4, 8), F32, ident, xn_done, b + 1)
                if u:
                    transposes("xqT", b, cols(xq, 0, HC), BF16, identb, xq_done, b - 1)
                slot_of(3)
                if u:
                    gate(b, 0)
                    up(b, 0)
                slot_of(4)
                if d:
                    transposes("hTa", b, cols(hq, 0, 8), BF16, identb, hq_done, b - 2)
                if u:
                    gate(b, 1)
                slot_of(5)
                if d:
                    transposes("hTb", b, cols(hq, 8, IC), BF16, identb, hq_done, b - 2)
                if u:
                    up(b, 1)
                slot_of(6)
                if u:
                    gate(b, 2)
                slot_of(7)
                if u:
                    up(b, 2)
                if a:
                    pv_wait(b, 7)
                    for j in range(HG):
                        pv(p, 7, j)

            bodies(pe, NB, body, head=2, tail=3)

        @block.scalar
        def _(act):
            act.wait_ge(v_set, 4)

            def take(kind, b, dst, src):
                act.wait_ge(ready[kind], b - delay[kind] + 1)
                act.copy(dst, src).then_inc(evac[kind], 1)

            def view(kind, dt, n):
                return tbank(kind)[:].bitcast(dt)[:, 0:n * P].rearrange("p (c n) -> p c n", n=P)

            def body(b, p, j):
                f, a, u, d, e = (stage(b, k) for k in range(5))

                def exps(g):
                    if not (a if g < KVH else f):
                        return
                    n = 8 * b - 8 + g
                    act.wait_ge(s_sub, n + 1)
                    if g >= 2:
                        if a:
                            act.wait_ge(ready[f"T{g - 2}"], b)
                    else:
                        need(act, ready[f"T{g + 6}"], b - 1)
                    act.activation(PB[:, g % 2], D[:, g % 2], ACT.Exp, scale=SCALE).then_inc(s_exp, 1)

                def probs(g):
                    if a:
                        need(act, pv_done, 8 * b - 8 + g - 1)
                        take(f"T{g}", b, PT[:, g % 2], view(f"T{g}", F32, HG))

                def gates(n):
                    if u:
                        lo, size = CHUNKS[n]
                        act.wait_ge(g_done, 3 * (b - 2) + n + 1)
                        need(act, ga_done, 3 * (b - 2) + n)
                        act.activation(th[:, 0:size], GB[:, 0:size], ACT.Tanh, scale=dqg[:, p, 1:2]).then_inc(th_done, 1)

                probs(0)
                if f:
                    need(act, rs3_done, b + 1, True)
                    need(act, ready["q1"], b, True)
                    act.activation(xn[:, :, :, 0:HD1].rearrange("p j k d -> p k j d"),
                                   at(X, b).rearrange("p (k j d) -> p k j d", k=KVH, j=GROUP), ACT.Identity,
                                   bias=rs3[:, 1:2], scale=rs3[:, 0:1]).then_inc(xn_done, 1)
                if d:
                    need(act, hn_done, b - 3)
                    act.wait_ge(h_done, 3 * (b - 2))
                    act.activation(junk[:], h[:], ACT.Square, accum_out=ss[:]).then_inc(ss_done, 1)
                exps(2)
                probs(1)
                if f:
                    take("kT", b, kT[:, p], view("kT", F32, 2))
                    take("q0", b, qT[:, p, 0:2].rearrange("p j c n -> p (j c) n"), view("q0", F32, 4))
                exps(3)
                probs(2)
                if f:
                    take("q1", b, qT[:, p, 2:4].rearrange("p j c n -> p (j c) n"), view("q1", F32, 4))
                if u:
                    need(act, u_done, 3 * (b - 2))
                    take("xqT", b, xqT[:], view("xqT", BF16, HC))
                exps(4)
                if d:
                    act.wait_ge(hr_done, b - 2)
                    need(act, ready["hTb"], b - 3)
                    act.activation(hq[:], hg[:], ACT.Identity, bias=nround[:]).then_inc(hq_done, 1)
                probs(3)
                gates(0)
                exps(5)
                probs(4)
                if d:
                    need(act, down_done, b - 3)
                    take("hTa", b, hT[:, 0:8, :], view("hTa", BF16, 8))
                gates(1)
                exps(6)
                probs(5)
                if d:
                    take("hTb", b, hT[:, 8:IC, :], view("hTb", BF16, IC - 8))
                exps(7)
                probs(6)
                gates(2)
                probs(7)
                exps(8)
                exps(9)

            bodies(act, NB, body, head=2, tail=3)

        @block.vector
        def _(dve):
            step = Steps(dve, dve_steps, alone=True)
            def front(b, p, j):
                xf = at(X, b)
                dve.wait_ge(gathered[p], 32 * (j + 1))
                dve.scalar_tensor_tensor(xf, yg[:, p, 0, :], m["wt"][:, 0, bass.ds(b, 1)], xf, ALU.mult,
                                         ALU.add).then_inc(x3_a, 1)
                dve.wait_ge(x3_a, b + 1)
                dve.scalar_tensor_tensor(xf, yg[:, p, 1, :], m["wt"][:, 1, bass.ds(b, 1)], xf, ALU.mult,
                                         ALU.add).then_inc(x3_done, 1)
                need(dve, x3_done, b + 1, True)
                step.then(dve.bn_stats(st[:, 1, :], xf))
                need(dve, rs3_done, b, True)
                dve.bn_aggr(mv3[:], st[:, 1, :]).then_inc(stats3, 1)

            front(0, 0, 0)
            dve.wait_ge(ld_g, 32)
            step.loop(15)

            def body(b, p, j):
                f, a, u, d, e = (stage(b, k) for k in range(5))
                step.body(b)

                def softmax_head(g):
                    if not (a if g < KVH else f):
                        return
                    n = 8 * b - 8 + g
                    dve.wait_ge(s_done, n + 1)
                    bk = S[g % 2][:].rearrange("p (h k) -> p h k", h=HG)
                    dve.tensor_reduce(mx[:, g % 2, :], bk, AX.X, ALU.max).then_inc(s_max, 1)
                    dve.wait_ge(s_max, n + 1)
                    need(dve, s_exp, n - 1)
                    dve.tensor_tensor(D[:, g % 2], bk, mx[:, g % 2, :, None].broadcast_to([P, HG, P]),
                                      ALU.subtract).then_inc(s_sub, 1)

                def out_half(k):
                    if not a:
                        return
                    dve.wait_ge(pv_done, 8 * b - 8 + 4 * (k + 1))
                    bk = O[k][:, 0:OH * HV].rearrange("p (h d) -> p h d", h=OH)
                    step.then(dve.reciprocal(rden[:, k, :], bk[:, :, HD1]))
                    need(dve, x4_done, 2 * b - 3 + k)
                    dve.tensor_tensor(On[:, k * 256:(k + 1) * 256].rearrange("p (h d) -> p h d", h=OH),
                                      bk[:, :, 0:HD1], rden[:, k, :, None].broadcast_to([P, OH, HD1]),
                                      ALU.mult).then_inc(o_done, 1)

                def gated(n):
                    if not u:
                        return
                    lo, size = CHUNKS[n]
                    k = 3 * (b - 2) + n
                    dve.wait_ge(th_done, k + 1)
                    need(dve, h_done, k)
                    if n == 0 and d:
                        dve.wait_ge(ss_done, b - 2)
                        dve.wait_ge(hg_done, 3 * (b - 2))
                    dve.scalar_tensor_tensor(ga[:, 0:size], th[:, 0:size], 1.0, GB[:, 0:size], ALU.add,
                                             ALU.mult).then_inc(ga_done, 1)
                    dve.wait_ge(ga_done, k + 1)
                    dve.wait_ge(u_done, k + 1)
                    dve.tensor_tensor(h[:, lo:lo + size], UB[:, 0:size], ga[:, 0:size], ALU.mult).then_inc(h_done, 1)

                def chunk_max(b, n):
                    lo, size = CHUNKS[n]
                    dve.wait_ge(hg_done, 3 * (b - 2) + n + 1)
                    dve.tensor_reduce(hm[:, n:n + 1], hg[:, lo:lo + size], AX.X, ALU.max,
                                      apply_absolute_value=True).then_inc(hm_done, 1)

                softmax_head(2)
                a0, a1, a2 = (am[:, k:k + 1] for k in range(3))
                b0, b1, b2, b3 = (ah[:, k:k + 1] for k in range(4))
                if u:
                    xb = at(X, b - 2)
                    need(dve, x4_done, 2 * (b - 1), True)
                    step.then(dve.bn_stats(st[:, 0, :], xb))
                    dve.bn_aggr(mv4[:], st[:, 0, :]).then_inc(stats4, 1)
                softmax_head(3)
                if u:
                    need(dve, stats4, b - 1, True)
                    t1_done = step.mark(dve.scalar_tensor_tensor(t1[:], xb, mv4[:, 0:1], g1[:], ALU.subtract, ALU.mult))
                if d:
                    chunk_max(b - 1, 2)
                if u:
                    dve.wait_ge(dve_steps, t1_done)
                    a0_done = step.mark(dve.tensor_reduce(a0, t1[:], AX.X, ALU.max, apply_absolute_value=True))
                if d:
                    dve.wait_ge(hm_done, 3 * (b - 2))
                    b0_done = step.mark(dve.tensor_reduce(b0, hm[:], AX.X, ALU.max))
                if u:
                    dve.wait_ge(nrm_done, b - 1)
                    dve.wait_ge(dve_steps, a0_done)
                    step.then(dve.tensor_scalar(a1, a0, nrm[:, 3:4], 1e-5, ALU.mult, ALU.max))
                    step.mark(dve.reciprocal(a2, a1))
                    need(dve, hn_done, b - 3)
                    dqg_done = step.mark(dve.tensor_scalar(dqg[:, p, 0:1], a1, 1.0 / 127.0, m["wmean"][:, 0:1],
                                                           ALU.mult, ALU.mult))
                    dve.wait_ge(dve_steps, dqg_done)
                    dve.tensor_scalar(mq[:], a2, 127.0, nrm[:, 3:4], ALU.mult, ALU.mult).then_inc(mq_done, 1)
                    step.mark(dve.tensor_scalar(dqg[:, p, 1:2], dqg[:, p, 0:1], 0.5, None, ALU.mult))
                    dve.wait_ge(mq_done, b - 1)
                    step.then(dve.tensor_scalar(t1[:], t1[:], mq[:], ROUND, ALU.mult, ALU.add))
                    need(dve, ready["xqT"], b - 2)
                    dve.tensor_scalar(xq[:], t1[:], -ROUND, None, ALU.add).then_inc(xq_done, 1)
                if d:
                    dve.wait_ge(hn_done, b - 2)
                    dve.wait_ge(dve_steps, b0_done)
                    step.then(dve.tensor_scalar(b1, b0, hn[:, 3:4], 1e-5, ALU.mult, ALU.max))
                    b3_done = step.mark(dve.reciprocal(b3, b1))
                    step.mark(dve.tensor_scalar(dqd[:, p:p + 1], b1, 1.0 / 127.0, m["wmean"][:, 1:2], ALU.mult, ALU.mult))
                    dve.wait_ge(dve_steps, b3_done)
                    need(dve, hr_done, b - 3)
                    dve.tensor_scalar(b2, b3, 127.0, hn[:, 3:4], ALU.mult, ALU.mult).then_inc(mh_done, 1)
                softmax_head(4)
                if e:
                    dve.wait_ge(down_done, b - 3)
                    need(dve, stored[p], 16 * (j - 2))
                    dve.scalar_tensor_tensor(xo[:, p, :], UB[:], dqd[:, 1 - p:2 - p], at(X, b - 4), ALU.mult,
                                             ALU.add).then_inc(out_done, 1)
                softmax_head(5)
                gated(0)
                softmax_head(6)
                out_half(0)
                if u:
                    chunk_max(b, 0)
                softmax_head(7)
                gated(1)
                softmax_head(8)
                if stage(b + 1, 0):
                    front(b + 1, 1 - p, j + p)
                if u:
                    chunk_max(b, 1)
                gated(2)
                softmax_head(9)
                out_half(1)
                step.end()

            bodies(dve, NB, body, head=2, tail=3)


_INS = ['x', 'ctx_512', 'L0_xattn_Wq', 'L0_xattn_Wkv_expand', 'L0_xattn_Wout', 'L0_ffn_Wg', 'L0_ffn_W1', 'L0_ffn_W2',
        'L0_ffn_W3', 'L0_ffn_bias', 'L1_ffn_gate_w', 'L1_ffn_down_w', 'L1_ffn_gate_norm_w', 'L1_ffn_down_norm_w']


def kernel(**inputs):
    import numpy as np
    import concourse.bacc as bacc
    from concourse import mybir as _mybir
    from concourse.bass_utils import run_bass_kernel_spmd

    nc = bacc.Bacc("TRN2", target_bir_lowering=False, num_devices=1)
    arrays, args = {}, {}
    for name in _INS:
        a = np.ascontiguousarray(inputs[name])
        arrays[f"in_{name}"] = a
        args[name] = nc.dram_tensor(f"in_{name}", a.shape, _mybir.dt.from_np(a.dtype), kind="ExternalInput").ap()
    out = nc.dram_tensor("out", (B, P, H), _mybir.dt.float32, kind="ExternalOutput").ap()
    decoder_kernel(nc, args["x"], args["ctx_512"], args["L0_xattn_Wq"], args["L0_xattn_Wkv_expand"],
                   args["L0_xattn_Wout"], args["L0_ffn_Wg"], args["L0_ffn_W1"], args["L0_ffn_W2"],
                   args["L0_ffn_W3"], args["L0_ffn_bias"], args["L1_ffn_gate_w"], args["L1_ffn_down_w"],
                   args["L1_ffn_gate_norm_w"], args["L1_ffn_down_norm_w"], out)
    r = run_bass_kernel_spmd(nc, [arrays], core_ids=[0])
    return r.results[0]["out"]
```
